# Optimizing a Trainium2 kernel written in Bass

```python
import numpy as np
import jax
import jax.numpy as jnp

def _softmax(x, axis=-1):
    return jax.nn.softmax(x, axis=axis)

def _gelu(x):
    return jax.nn.gelu(x, approximate=True)

def _silu(x):
    return jax.nn.silu(x)

def _sigmoid(x):
    return jax.nn.sigmoid(x)

def _layernorm(x, axis=-1, eps=1e-05):
    m = jnp.mean(x, axis=axis, keepdims=True)
    v = jnp.var(x, axis=axis, keepdims=True)
    return (x - m) / jnp.sqrt(v + eps)

def _scatter_add(tgt, idx, src, axis=0):
    return tgt.at[idx].add(src)

def _segment_sum(src, seg, n):
    return jax.ops.segment_sum(src, seg, n)
kernel_name = 'mk_gnn_ffn_d1_gnn_r64_6b1605'

def setup_inputs(seed: int=0):
    np.random.seed(seed)
    _w = jnp.asarray

    def _rec_inputs():
        import jax
        import jax.numpy as jnp
        _gk = jax.random.key(seed)
        x = -0.0003747 + 1 * jax.random.normal(jax.random.fold_in(_gk, 1), (10000, 1024), jnp.float32)
        src = jax.random.randint(jax.random.fold_in(_gk, 2), (5000,), 0, 10000, jnp.int32)
        dst = jax.random.randint(jax.random.fold_in(_gk, 3), (5000,), 0, 10000, jnp.int32)
        _o = jnp.argsort(dst, stable=True)
        src = src[_o]
        dst = dst[_o]
        return (x, src, dst)
    x, src, dst = _rec_inputs()

    def _L0_gnn_setup():
        import jax, jax.numpy as jnp
        import numpy as np
        N_DIAS = 64
        L = 60
        N = N_DIAS * L
        E = N_DIAS * L * (L - 1)
        D = 1024
        H = 512
        K = 4

        def _build_edges():
            idx = np.arange(L)
            src = np.repeat(idx, L)
            dst = np.tile(idx, L)
            m = src != dst
            src, dst = (src[m], dst[m])
            offs = (np.arange(N_DIAS) * L)[:, None]
            row = (src[None, :] + offs).reshape(-1)
            col = (dst[None, :] + offs).reshape(-1)
            return (row.astype(np.int32), col.astype(np.int32))
        key = jax.random.key(seed)
        k0, k1, k2 = jax.random.split(key, 3)
        row, col = _build_edges()
        return {'emotions_feat': jax.random.normal(k0, (N, D), jnp.float32), 'W1': jax.random.normal(k1, (D, H), jnp.float32) * 0.02, 'b1': jnp.zeros((H,), jnp.float32), 'Wg': jax.random.normal(k2, (K, 2 * H, 1), jnp.float32) * 0.02, 'bg': jnp.zeros((K, 1), jnp.float32), 'row': jnp.asarray(row), 'col': jnp.asarray(col)}
    _L0_gnn_all = _L0_gnn_setup()
    _L0_gnn_in = {k: v for k, v in _L0_gnn_all.items() if k in ('W1', 'b1', 'Wg', 'bg')}
    del _L0_gnn_all

    def _L0_ffn_setup():
        import jax, jax.numpy as jnp
        import numpy as np
        B, S, HID, DFF, E, K = (4, 32, 1024, 64, 8, 32)
        key = jax.random.key(seed)
        ks = jax.random.split(key, 4)
        sc_h = 1.0 / np.sqrt(HID)
        sc_f = 1.0 / np.sqrt(DFF)
        return {'x': jax.random.normal(ks[0], (B, S, HID), jnp.float32), 'router_w': jax.random.normal(ks[1], (HID, E), jnp.float32) * sc_h, 'router_b': jnp.zeros((E,), jnp.float32), 'w1': jax.random.normal(ks[2], (E, HID, DFF), jnp.float32) * sc_h, 'b1': jnp.zeros((E, DFF), jnp.float32), 'w2': jax.random.normal(ks[3], (E, DFF, HID), jnp.float32) * sc_f, 'b2': jnp.zeros((E, HID), jnp.float32)}
    _L0_ffn_all = _L0_ffn_setup()
    _L0_ffn_in = {k: v for k, v in _L0_ffn_all.items() if k in ('router_w', 'router_b', 'w1', 'b1', 'w2', 'b2')}
    del _L0_ffn_all
    return {'x': x, 'src': src, 'dst': dst, 'L0_gnn_W1': _L0_gnn_in['W1'], 'L0_gnn_b1': _L0_gnn_in['b1'], 'L0_gnn_Wg': _L0_gnn_in['Wg'], 'L0_gnn_bg': _L0_gnn_in['bg'], 'L0_ffn_router_w': _L0_ffn_in['router_w'], 'L0_ffn_router_b': _L0_ffn_in['router_b'], 'L0_ffn_w1': _L0_ffn_in['w1'], 'L0_ffn_b1': _L0_ffn_in['b1'], 'L0_ffn_w2': _L0_ffn_in['w2'], 'L0_ffn_b2': _L0_ffn_in['b2']}

def reference(x, src, dst, L0_gnn_W1, L0_gnn_b1, L0_gnn_Wg, L0_gnn_bg, L0_ffn_router_w, L0_ffn_router_b, L0_ffn_w1, L0_ffn_b1, L0_ffn_w2, L0_ffn_b2):
    import jax
    import jax.numpy as jnp

    def _L0_gnn_ref(emotions_feat, W1, b1, Wg, bg, row, col):
        import jax, jax.numpy as jnp
        import numpy as np
        N_DIAS = 64
        L = 60
        N = N_DIAS * L
        E = N_DIAS * L * (L - 1)
        D = 1024
        H = 512
        K = 4

        def _build_edges():
            idx = np.arange(L)
            src = np.repeat(idx, L)
            dst = np.tile(idx, L)
            m = src != dst
            src, dst = (src[m], dst[m])
            offs = (np.arange(N_DIAS) * L)[:, None]
            row = (src[None, :] + offs).reshape(-1)
            col = (dst[None, :] + offs).reshape(-1)
            return (row.astype(np.int32), col.astype(np.int32))
        n = emotions_feat.shape[0]
        x1 = emotions_feat @ W1 + b1
        h = x1.shape[1]
        deg = jax.ops.segment_sum(jnp.ones_like(col, x1.dtype), col, num_segments=n)
        dis = jnp.clip(deg, 1.0) ** (-0.5)
        norm = dis[row] * dis[col]
        gnn = x1
        for k in range(Wg.shape[0]):
            Wi, Wj = (Wg[k, :h], Wg[k, h:])
            x_i = gnn[col]
            x_j = gnn[row]
            alpha = jnp.tanh(x_i @ Wi + x_j @ Wj + bg[k])
            msg = norm[:, None] * alpha * x_j
            agg = jax.ops.segment_sum(msg, col, num_segments=n)
            gnn = gnn + agg
        return jnp.concatenate([x1, gnn], axis=1)

    def _L0_ffn_ref(x, router_w, router_b, w1, b1, w2, b2):
        import jax, jax.numpy as jnp
        import numpy as np
        B, S, HID, DFF, E, K = (4, 32, 1024, 64, 8, 32)
        b, s, h = x.shape
        xf = x.reshape(-1, h)
        logits = xf @ router_w + router_b
        scores = jax.nn.softmax(logits, axis=-1)
        G, idx = jax.lax.top_k(scores.T, K)
        toks = xf[idx]
        h1 = jax.nn.relu(jnp.einsum('ekh,ehf->ekf', toks, w1) + b1[:, None, :])
        eo = jnp.einsum('ekf,efh->ekh', h1, w2) + b2[:, None, :]
        contrib = (eo * G[..., None]).reshape(-1, h)
        y = jnp.zeros_like(xf).at[idx.reshape(-1)].add(contrib)
        return y.reshape(b, s, h)
    x = x + _L0_gnn_ref(_layernorm(x, axis=-1), L0_gnn_W1, L0_gnn_b1, L0_gnn_Wg, L0_gnn_bg, src, dst)
    x = x + _L0_ffn_ref(_layernorm(x, axis=-1)[None], L0_ffn_router_w, L0_ffn_router_b, L0_ffn_w1, L0_ffn_b1, L0_ffn_w2, L0_ffn_b2)[0]
    return x

_drawn_inputs = setup_inputs


def setup_inputs(seed=0):
    import zlib

    import numpy as np

    out = dict(_drawn_inputs(seed))
    spreads = {'L0_gnn_b1': (0.0, 0.1),
     'L0_gnn_bg': (0.0, 0.1),
     'L0_ffn_router_b': (0.0, 0.8),
     'L0_ffn_b1': (0.0, 0.8),
     'L0_ffn_b2': (0.0, 0.8)}
    factors = {}
    for name, (base, spread) in spreads.items():
        noise = np.random.default_rng([zlib.crc32(name.encode()), seed]).standard_normal(out[name].shape)
        drawn = base * np.exp(spread * noise) if base else spread * noise
        out[name] = jnp.asarray(drawn.astype(out[name].dtype))
    for name, factor in factors.items():
        out[name] = (out[name] * factor).astype(out[name].dtype)
    return out
```

```python
from contextlib import ExitStack

import concourse.bass as bass
from concourse import mybir

F32 = mybir.dt.float32
BF16 = mybir.dt.bfloat16
I32 = mybir.dt.int32
U32 = mybir.dt.uint32
ALU = mybir.AluOpType
ACT = mybir.ActivationFunctionType
AX = mybir.AxisListType

P = 128
EPS = 1e-5
FAR = 1000000.0


def gnn_ffn(nc, x, src, dst, W1, b1, Wg, bg, rw, rb, fw1, fb1, fw2, fb2, out,
            G, SO, SD, T, Vd, NDA, NDB, SC, CV, CI, PQ):
    N, D = x.shape
    H = W1.shape[1]
    K = Wg.shape[0]
    NE = src.shape[0]
    EX, FF = fb1.shape
    NT = (N + P - 1) // P
    LAST = N - (NT - 1) * P
    NPAD = NT * P
    DC = D // P
    HC = H // P
    NP = 2 * K + EX
    R = H + NP
    NQ = NP + EX
    WX = H + NQ + EX
    ET = (NE + P - 1) // P
    EJ = ET
    EP = NE // EJ
    EPAD = ET * P
    PADV = NPAD - 1
    GQ = 4
    GT = ET // GQ
    TOPK = 32
    XS = 4
    assert EP * EJ == NE and NT == 79 and NP == 16

    xh = x.rearrange("n (h c) -> (n h) c", h=2)
    outh = out.rearrange("n (h c) -> (n h) c", h=2)

    with ExitStack() as ctx:
        def sb(name, shape, dt=F32, c=ctx):
            return c.enter_context(nc.sbuf_tensor(name, shape, dt))

        def sem(name):
            return ctx.enter_context(nc.semaphore(name))

        ident = sb("ident", [P, P])
        E = sb("E", [P, ET, P], BF16)
        Fsel = sb("Fsel", [2 * ET, ET, P], BF16)
        TBl = sb("TBl", [P, ET, 2 * ET], BF16)
        norm = sb("norm", [P, ET])
        m = sb("m", [P, ET])
        pre = sb("pre", [P, ET])
        al = sb("al", [P, ET])
        Vpi = sb("Vpi", [P, ET, K])
        bgb = sb("bgb", [P, K])
        rbb = sb("rbb", [P, EX])
        csrw = sb("csrw", [P, EX])
        bRa = sb("bRa", [P, EX])
        curf = sb("curf", [P, ET])
        isrc = sb("isrc", [P, ET], I32)
        idst = sb("idst", [P, ET], I32)
        ilsrc = sb("ilsrc", [P, ET], I32)
        iout = sb("iout", [P, ET], I32)
        inode = sb("inode", [P, ET], I32)
        ixr = sb("ixr", [P, ET], I32)
        Lm = sb("Lm", [ET, ET])
        fidx = sb("fidx", [ET, 1], I32)
        ilast = sb("ilast", [ET, 1], I32)
        ispo = sb("ispo", [ET, 1], I32)
        ispn = sb("ispn", [ET, 1], I32)
        ispx = sb("ispx", [ET, 1], I32)
        eps = sb("eps", [P, 1])

        with ExitStack() as c:
            Z = sb("Z", [P, ET, R], c=c)
            V = sb("V", [P, ET, R], c=c)
            E32 = sb("E32", [P, 2, P], c=c)
            RC = sb("RC", [ET, R], c=c)
            RC0 = sb("RC0", [ET, R], c=c)
            corr = sb("corr", [ET, R], c=c)
            zf = sb("zf", [P, GT, K], c=c)
            z3 = sb("z3", [P, ET, 3 * K], BF16, c=c)
            tbf = sb("tbf", [2 * ET, 3 * K], c=c)
            tb3 = sb("tb3", [2 * ET, 3 * K], BF16, c=c)
            junkc = sb("junkc", [P, H], BF16, c=c)
            Sv, Sx = RC0, RC
        with ExitStack() as c:
            wext = sb("wext", [P, DC, WX], c=c)
            xr = sb("xr", [P, XS, D], c=c)
            xn = sb("xn", [P, 2, D], c=c)
            xT = sb("xT", [P, 2, DC, P], c=c)
            x1s = sb("x1s", [P, 2, R], c=c)
            recA = sb("recA", [P, XS, 24], c=c)
            recB = sb("recB", [P, XS, 16], c=c)
            bns = sb("bns", [P, 2, 2, 6], c=c)
            sdv = sb("sdv", [P, 2], c=c)
            rsd = sb("rsd", [P, 2], c=c)
            nmr = sb("nmr", [P, 2], c=c)
            b1e = sb("b1e", [P, R], c=c)
            Rp = sb("Rp", [P, HC, NQ], c=c)
            wT = sb("wT", [P, 2, HC, P], c=c)
            b1c = sb("b1c", [P, HC], c=c)
            ones = sb("ones", [P, P], c=c)
            junka = sb("junka", [P, 2, H], BF16, c=c)
            keyr = sb("keyr", [EP, NE], c=c)
            junks = sb("junks", [EP, NE], BF16, c=c)
            drow = sb("drow", [P, EPAD], I32, c=c)
            eq = sb("eq", [EP, EJ, EJ], c=c)
            ei = sb("ei", [EP, 2, EJ], I32, c=c)
            pairs = sb("pairs", [EP, EJ, 2], I32, c=c)
            dstf = sb("dstf", [EP, EJ], c=c)
            key = sb("key", [EP, EJ], c=c)
            pcol = sb("pcol", [EP, 1], c=c)
            sgn = sb("sgn", [EP, EJ], c=c)
            ceq = sb("ceq", [EP, EJ], c=c)
            clt = sb("clt", [EP, EJ], c=c)
            c0 = sb("c0", [EP, EJ], c=c)
            posf = sb("posf", [EP, EJ], c=c)
            posi = sb("posi", [EP, EJ], I32, c=c)
            padi = sb("padi", [1, 2 * (EPAD - NE + 2)], I32, c=c)
            zt = sb("zt", [P, 2 * NPAD // P], c=c)
            cur = sb("cur", [P, ET, 2], I32, c=c)
            nxt = sb("nxt", [P, ET, 2], I32, c=c)
            prv = sb("prv", [P, ET, 2], I32, c=c)
            w = [sb(f"w{i}", [P, ET], c=c) for i in range(12)]
            slot = sb("slot", [P, ET], c=c)
            slot1 = sb("slot1", [P, ET], c=c)
            ifst = sb("ifst", [P, ET], I32, c=c)
            ilst = sb("ilst", [P, ET], I32, c=c)
            TS = sb("TS", [P, ET, 2], c=c)
            TD = sb("TD", [P, ET, 2], c=c)
            curR = sb("curR", [ET, P, 2], I32, c=c)
            dR = sb("dR", [ET, P], I32, c=c)
            dRf = sb("dRf", [ET, P], c=c)
            brow = sb("brow", [P, 2, ET], I32, c=c)
            browf = sb("browf", [P, 2, ET], c=c)
            bcol = sb("bcol", [2 * ET, 3], I32, c=c)
            bcf = sb("bcf", [2 * ET, 3], c=c)
            own = sb("own", [2 * ET, ET], c=c)
            nown = sb("nown", [P, 2, 2 * ET], c=c)
            sm = sb("sm", [ET, 10], c=c)
            fbase = sb("fbase", [ET, 1], c=c)
            TL = sb("TL", [ET, 2], c=c)
            ifn = sb("ifn", [ET, 1], I32, c=c)
            mhalf = sb("mhalf", [P, ET], c=c)
            ovl = sb("ovl", [2 * ET, 1], c=c)
        with ExitStack() as c:
            ndA = sb("ndA", [P, NT, 24], c=c)
            ndB = sb("ndB", [P, NT, 16], c=c)
            q = [sb(f"q{i}", [P, NT], c=c) for i in range(6)]
            lg = sb("lg", [P, NT, EX], c=c)
            lt = sb("lt", [P, NT, EX], c=c)
            sct = sb("sct", [P, EX, NT], c=c)
            tk = sb("tk", [P, NPAD * EX // P], c=c)
            tv = sb("tv", [P, TOPK], c=c)
            ti = sb("ti", [P, TOPK], U32, c=c)
            tif = sb("tif", [P, TOPK], c=c)
            tgi = sb("tgi", [P, TOPK], I32, c=c)
            tbase = sb("tbase", [P, 1], c=c)
            cv = sb("cv", [EX, 16 * TOPK], c=c)
            gv = sb("gv", [EX, TOPK], c=c)
            gi = sb("gi", [EX, TOPK], U32, c=c)
            gif = sb("gif", [EX, TOPK], c=c)
            gbase = sb("gbase", [EX, 1], c=c)
            gpi = sb("gpi", [EX, TOPK], I32, c=c)
            gcol = sb("gcol", [P, 2], c=c)
            pcl = sb("pcl", [P, 2], I32, c=c)
            tok = sb("tok", [P, 2], I32, c=c)
            tokf = sb("tokf", [P, 2], c=c)
            tokw = sb("tokw", [P, 2], I32, c=c)
            tw = sb("tw", [P, 6], c=c)
            fx = sb("fx", [P, 2, D], c=c)
            fn = sb("fn", [P, 2, D], c=c)
            fT = sb("fT", [P, DC, 2 * P], c=c)
            w1e = sb("w1e", [P, EX, DC, FF], c=c)
            w2e = sb("w2e", [FF, EX, D], c=c)
            b1t = sb("b1t", [FF, EX], c=c)
            b2t = sb("b2t", [EX, D], c=c)
            h1 = sb("h1", [FF, EX, P], c=c)
            esel = sb("esel", [EX, 2, P], c=c)
            ct = sb("ct", [P, 2, D], c=c)
            dq = sb("dq", [P, 2, 2, P], c=c)
            dlo = sb("dlo", [P, 2, 2, P], c=c)
            fst = sb("fst", [P, 2, 2, 6], c=c)
            fmv = sb("fmv", [P, 2, 2], c=c)
            fsd = sb("fsd", [P, 2], c=c)
            frs = sb("frs", [P, 2], c=c)
            fnm = sb("fnm", [P, 2], c=c)
            diag = sb("diag", [P, 2, P], c=c)
            onesf = sb("onesf", [P, P], c=c)
            ebase = sb("ebase", [P, 2], c=c)

        def psum(name, shape):
            return ctx.enter_context(nc.psum_tensor(name, shape, F32))

        pT = psum("pT", [P, 2, 2, 512])
        pA = psum("pA", [P, 2, 512])
        pB = psum("pB", [P, 512])
        pC = psum("pC", [P, 512])
        pBC = [pB, pC]
        pN = pT[:, 0, 0, :]

        s_x = [sem(f"s_x_slot{i}") for i in range(XS)]
        s_st = [sem(f"s_st_slot{i}") for i in range(XS)]
        s_sg = [sem(f"s_sg_slot{i}") for i in range(2)]
        s_sr = [sem(f"s_sr_slot{i}") for i in range(XS)]
        s_w = sem("s_w")
        s_id = sem("s_id")
        s_bn = sem("s_bn")
        s_var = sem("s_var")
        s_std = sem("s_std")
        s_rc = sem("s_rc")
        s_rstd = sem("s_rstd")
        s_xn = sem("s_xn")
        s_T = sem("s_T")
        s_evd = sem("s_evd")
        s_eva = sem("s_eva")
        s_mm = sem("s_mm")
        s_x1 = sem("s_x1")
        s_rec = sem("s_rec")
        s_o = sem("s_o")
        s_sq = sem("s_sq")
        s_wt = sem("s_wt")
        s_wc = sem("s_wc")
        s_wq = sem("s_wq")
        s_we = sem("s_we")
        s_ei = sem("s_ei")
        s_ek = sem("s_ek")
        s_ep = sem("s_ep")
        s_sgn = sem("s_sgn")
        s_p = sem("s_p")
        s_pd = sem("s_pd")
        s_init = sem("s_init")
        s_tab = sem("s_tab")
        s_zg = [sem(f"s_zg_slot{i}") for i in range(GQ)]
        s_vg = [sem(f"s_vg_slot{i}") for i in range(GQ)]
        s_r0 = sem("s_r0")
        s_vp = sem("s_vp")
        s_pre = sem("s_pre")
        s_th = sem("s_th")
        s_m = sem("s_m")
        s_zs = sem("s_zs")
        s_z3 = sem("s_z3")
        s_e32 = sem("s_e32")
        s_wm = sem("s_wm")
        s_va = sem("s_va")
        s_vw = [sem(f"s_vw_slot{i}") for i in range(GQ)]
        s_rl = sem("s_rl")
        s_rs = sem("s_rs")
        s_co = sem("s_co")
        s_cc = sem("s_cc")
        s_ca = sem("s_ca")
        s_tb = sem("s_tb")
        s_tc = sem("s_tc")
        s_na = sem("s_na")
        s_xg = [sem(f"s_xg_slot{i}") for i in range(GQ)]
        s_fo = sem("s_fo")
        s_fq = sem("s_fq")
        s_fr = sem("s_fr")
        s_fs = sem("s_fs")
        s_sp = sem("s_sp")
        s_sd = sem("s_sd")
        s_sa = sem("s_sa")
        s_ss = sem("s_ss")
        s_fw = sem("s_fw")
        s_nd = sem("s_nd")
        s_d = sem("s_d")
        s_a = sem("s_a")
        s_g = sem("s_g")
        s_t = sem("s_t")
        s_q = [sem(f"s_q_slot{i}") for i in range(10)]

        s_key = sem("s_key")
        s_eq = sem("s_eq")
        s_c0 = sem("s_c0")
        s_eps = sem("s_eps")
        s_one = sem("s_one")
        s_pk = sem("s_pk")
        s_E = sem("s_E")
        s_dr = sem("s_dr")
        s_sz = sem("s_sz")
        s_a1 = sem("s_a1")
        s_a2 = sem("s_a2")
        s_a3 = sem("s_a3")
        s_v2 = sem("s_v2")
        s_lg = sem("s_lg")
        s_sc = sem("s_sc")
        s_msk = sem("s_msk")
        s_l1 = sem("s_l1")
        s_l2 = sem("s_l2")
        s_tk = sem("s_tk")
        s_dg = sem("s_dg")
        s_dq = sem("s_dq")
        s_fv = sem("s_fv")
        s_fs2 = sem("s_fs2")
        s_fn = sem("s_fn")
        s_fT = sem("s_fT")
        s_h0 = sem("s_h0")
        s_h1 = sem("s_h1")
        s_ct = sem("s_ct")
        s_fz = sem("s_fz")
        s_lo = sem("s_lo")
        s_tw = sem("s_tw")
        s_fx = [sem(f"s_fx_slot{i}") for i in range(2)]
        NWL = 4 + 2 * K + 4

        block = ctx.enter_context(nc.Block())


        dyn = lambda ap, t: ap[:, bass.ds(t, 1)]
        row = lambda ap, t: ap[:, bass.ds(t, 1), :].rearrange("p a b -> p (a b)")

        def node_loop(eng, step, middle=None):
            for t in range(-2, XS):
                step(0, t)
            with eng.Fori(XS, ET - XS + 1, XS) as i:
                for u in range(XS):
                    step(i, u)
            if middle:
                middle()
            with eng.Fori(ET, NT - 3 - 2 * XS + 1, XS) as i:
                for u in range(XS):
                    step(i, u)
            for u in range(XS):
                step(NT - 3 - XS, u)
            for u in range(3):
                step(NT - 3, u)

        def has(i, u, ahead):
            return 0 <= i + u + ahead < NT if isinstance(i, int) else True

        def early(i, u, before):
            return isinstance(i, int) and i + u - before < 0

        def group_tiles(eng, first, lo, step):
            if first:
                for u in range(2):
                    step(lo, u)
                lo += 2
                with eng.Fori(lo, lo + GT - 3, 2) as i:
                    for u in range(2):
                        step(i, u)
            else:
                with eng.Fori(lo, lo + GT - 1, 2) as i:
                    for u in range(2):
                        step(i, u)

        @block.sync
        def _(sp):
            def load(i, u):
                t = i + u
                if isinstance(t, int) and t == NT - 1:
                    sp.dma_start(xr[0:LAST, u % XS, :], x[t * P:N, :]).then_inc(s_x[u % XS], 16)
                else:
                    sp.dma_start(xr[:, u % XS, :], x[bass.ds(t * P, P), :]).then_inc(s_x[u % XS], 16)

            for t in range(3):
                load(0, t)
            with nc.allow_non_contiguous_dma(reason="small weights"):
                sp.dma_start(wext[:, :, 0:H], W1.rearrange("(c p) h -> p c h", p=P)).then_inc(s_w, 16)
                sp.dma_start(wext[:, :, H + NQ:WX], rw.rearrange("(c p) e -> p c e", p=P)).then_inc(s_w, 16)
                for k in range(K):
                    for s in range(2):
                        sp.dma_start(Rp[:, :, s * K + k], Wg[k, s * H:(s + 1) * H, 0].rearrange("(c p) -> p c", p=P)).then_inc(s_w, 16)
                sp.dma_start(Rp[:, :, 2 * K:NP], rw[H:D, :].rearrange("(c p) e -> p c e", p=P)).then_inc(s_w, 16)
                sp.dma_start(Rp[:, :, NP:NQ], rw[0:H, :].rearrange("(c p) e -> p c e", p=P)).then_inc(s_w, 16)
                sp.dma_start(b1c[:, :], b1.rearrange("(c p) -> p c", p=P)).then_inc(s_w, 16)
                sp.dma_start(b1e[:, 0:H], b1.rearrange("(a h) -> a h", a=1).to_broadcast([P, H])).then_inc(s_w, 16)
                sp.dma_start(bgb[:, :], bg.rearrange("k a -> a k").to_broadcast([P, K])).then_inc(s_w, 16)
                sp.dma_start(rbb[:, :], rb.rearrange("(a h) -> a h", a=1).to_broadcast([P, EX])).then_inc(s_w, 16)
                sp.dma_start(ei[:, 0, :], dst.rearrange("(p j) -> p j", j=EJ)).then_inc(s_ei, 16)
                sp.dma_start(ei[:, 1, :], src.rearrange("(p j) -> p j", j=EJ)).then_inc(s_ei, 16)
                sp.dma_start(drow[0:EP, 0:NE], dst.rearrange("(a e) -> a e", a=1).to_broadcast([EP, NE])).then_inc(s_ei, 16)

            def step(i, u):
                if u < 0:
                    return
                t = i + u
                last = isinstance(t, int) and t == NT - 1
                sp.wait_ge(s_o, t + 1)
                sp.wait_ge(s_sq, t * 2 + 2)
                if last:
                    sp.dma_start(out[t * P:N, :], xr[0:LAST, u % XS, :]).then_inc(s_st[u % XS], 16)
                else:
                    sp.dma_start(out[bass.ds(t * P, P), :], xr[:, u % XS, :]).then_inc(s_st[u % XS], 16)
                sp.dma_start(G[bass.ds(t * P, P), :], x1s[:, u % 2, :]).then_inc(s_sg[u % 2], 16)
                sp.dma_start(NDA[bass.ds(t * P, P), :], recA[:, u % XS, :]).then_inc(s_sr[u % XS], 16)
                sp.dma_start(NDB[bass.ds(t * P, P), :], recB[:, u % XS, :]).then_inc(s_sr[u % XS], 16)
                if has(i, u, 3):
                    if not early(i, u, 1):
                        sp.wait_ge(s_st[(u - 1) % XS], i * (16 // XS) + (16 if u else 0))
                    load(i, u + 3)

            node_loop(sp, step)

            for k in range(K):
                vd = Vd[k % 2]
                for g in range(GQ):
                    sp.wait_ge(s_va, ET * k + GT * (g + 1))
                    sp.dma_start(vd[g * GT * P:(g + 1) * GT * P, :].rearrange("(t p) c -> p t c", p=P),
                                 V[:, g * GT:(g + 1) * GT, :]).then_inc(s_vw[g], 16)
                for g in range(GQ):
                    sp.wait_ge(s_vw[g], 16 * (k + 1))
                if k:
                    sp.wait_ge(s_co, k)
                sp.dma_start(RC[:, :], vd.rearrange("(t p) c -> p t c", p=P)[P - 1]).then_inc(s_rl, 16)

            sp.wait_ge(s_fs, 16 * 2 * ET)
            sp.wait_ge(s_ss, 32)
            sp.dma_start(ndA[:, :, :].rearrange("p j c -> p (j c)"), NDA.rearrange("(p j) c -> p (j c)", p=P)).then_inc(s_nd, 16)
            sp.dma_start(ndB[:, :, :].rearrange("p j c -> p (j c)"), NDB.rearrange("(p j) c -> p (j c)", p=P)).then_inc(s_nd, 16)
            for e in range(EX):
                sp.dma_start(w1e[:, e, :, :], fw1[e].rearrange("(c p) f -> p c f", p=P)).then_inc(s_fw, 16)
            sp.dma_start(w2e[:, :, :], fw2.rearrange("e f h -> f e h")).then_inc(s_fw, 16)
            with nc.allow_non_contiguous_dma(reason="bias columns"):
                sp.dma_start(b1t[:, :], fb1.rearrange("e f -> f e")).then_inc(s_fw, 16)
            sp.dma_start(b2t[:, :], fb2).then_inc(s_fw, 16)
            sp.wait_ge(s_msk, 1)
            sp.dma_start(SC.rearrange("e (p j) -> p e j", p=P), sct[:, :, :]).then_inc(s_q[0], 16)
            sp.wait_ge(s_q[0], 16)
            sp.dma_start(tk[:, :], SC.rearrange("e (g n) -> (e g) n", g=16)).then_inc(s_q[1], 16)
            sp.wait_ge(s_l1, 1)
            sp.dma_start(CV.rearrange("(p r) -> p r", p=P), tv[:, :]).then_inc(s_q[2], 16)
            sp.dma_start(CI.rearrange("(p r) a -> p (r a)", p=P), tgi[:, :]).then_inc(s_q[3], 16)
            sp.wait_ge(s_q[2], 16)
            sp.dma_start(cv[:, :], CV.rearrange("(e n) -> e n", e=EX)).then_inc(s_q[4], 16)
            sp.wait_ge(s_l2, 1)
            sp.dma_start(PQ[0:EX * TOPK].rearrange("(e r) -> e r", e=EX), gpi[:, :]).then_inc(s_q[5], 16)
            sp.dma_start(PQ[EX * TOPK:2 * EX * TOPK].rearrange("(e r) -> e r", e=EX), gv[:, :].bitcast(I32)).then_inc(s_q[5], 16)
            sp.wait_ge(s_q[5], 32)
            with nc.allow_non_contiguous_dma(reason="columns of chosen pairs"):
                sp.dma_start(pcl[:, :], PQ[0:EX * TOPK].rearrange("(h p) -> p h", p=P)).then_inc(s_q[6], 16)
                sp.dma_start(gcol[:, :].bitcast(I32), PQ[EX * TOPK:2 * EX * TOPK].rearrange("(h p) -> p h", p=P)).then_inc(s_q[7], 16)
            sp.wait_ge(s_q[9], 32)

        @block.tensor
        def _(pe):
            mmul = nc.tensor.matmul
            pe.wait_ge(s_w, 16 * NWL)
            pe.wait_ge(s_id, 1)
            def wturn(c):
                if c >= 2:
                    pe.wait_ge(s_wc, c - 1)
                for q4 in range(HC):
                    mm = nc.tensor.transpose(pT[:, c % 2, 0, q4 * P:(q4 + 1) * P], wext[:, c, q4 * P:(q4 + 1) * P], ident[:, :])
                mm.then_inc(s_wt, 1)

            wturn(0)
            for c in range(DC):
                if c + 1 < DC:
                    wturn(c + 1)
                pe.wait_ge(s_wc, c + 1)
                if c >= 1:
                    pe.wait_ge(s_we, c)
                for q4 in range(HC):
                    mm = mmul(pB[:, 0:NQ], lhsT=wT[:, c % 2, q4, :], rhs=Rp[:, q4, :], start=(q4 == 0), stop=(q4 == HC - 1))
                mm.then_inc(s_wq, 1)
            pe.wait_ge(s_we, DC)
            pe.wait_ge(s_one, 1)
            for q4 in range(HC):
                mm = mmul(pB[:, 0:NQ], lhsT=b1c[:, q4:q4 + 1].to_broadcast([P, P]), rhs=Rp[:, q4, :], start=(q4 == 0), stop=(q4 == HC - 1))
            for c in range(DC):
                mm = mmul(pC[:, 0:EX], lhsT=ones[:, :], rhs=wext[:, c, H + NQ:WX], start=(c == 0), stop=(c == DC - 1))
            mm.then_inc(s_wq, 1)
            pe.wait_ge(s_we, DC + 1)

            def step(i, u):
                t = i + u
                if has(i, u, 1) and u >= -1:
                    pe.wait_ge(s_xn, t + 2)
                    if not early(i, u, 1):
                        pe.wait_ge(s_evd, t)
                        pe.wait_ge(s_eva, t)
                    n = (u + 1) % 2
                    for c in range(DC):
                        mm = nc.tensor.transpose(pT[:, n, c // 4, (c % 4) * P:(c % 4 + 1) * P], xn[:, n, c * P:(c + 1) * P], ident[:, :])
                    mm.then_inc(s_T, 1)
                if u >= 0:
                    pe.wait_ge(s_evd, t + 1)
                    pe.wait_ge(s_eva, t + 1)
                    if not early(i, u, 2):
                        pe.wait_ge(s_x1, t - 1)
                    n = u % 2
                    for c in range(DC):
                        mmul(pA[:, n, :], lhsT=xT[:, n, c, :], rhs=wext[:, c, 0:H], start=(c == 0), stop=(c == DC - 1))
                        mm = mmul(pBC[n][:, 0:WX - H], lhsT=xT[:, n, c, :], rhs=wext[:, c, H:WX], start=(c == 0), stop=(c == DC - 1))
                    mm.then_inc(s_mm, 1)

            node_loop(pe, step)

            for k in range(K):
                for g in range(GQ):
                    def wide(i, u):
                        t = i + u
                        pe.wait_ge(s_e32, t + (ET * k + 1))
                        if not (k == 0 and g == 0 and isinstance(i, int) and i == 0):
                            pe.wait_ge(s_va, t + (ET * k - 1))
                        mmul(pA[:, u, :], lhsT=E32[:, u, :], rhs=row(Z[:, :, 0:H], t), start=True, stop=True)
                        mmul(pBC[u][:, 0:NP], lhsT=E32[:, u, :], rhs=row(Z[:, :, H:R], t), start=True, stop=True).then_inc(s_wm, 1)
                    group_tiles(pe, k == 0 and g == 0, g * GT, wide)
                if k < K - 1:
                    for g in range(GQ):
                        pe.wait_ge(s_z3, GQ * k + g + 1)
                    pe.wait_ge(s_va, ET * (k + 1))
                    def bsum(t, start, stop):
                        mmul(pC[0:2 * ET, 0:3 * K], lhsT=row(TBl, t), rhs=row(z3, t), start=start, stop=stop,
                             skip_group_check=True)
                    bsum(0, True, False)
                    with pe.Fori(1, ET - 1, 1) as t:
                        bsum(t, False, False)
                    mmul(pC[0:2 * ET, 0:3 * K], lhsT=TBl[:, ET - 1, :], rhs=z3[:, ET - 1, :], start=False, stop=True,
                         skip_group_check=True).then_inc(s_tb, 1)
                    pe.wait_ge(s_tc, 4 * (k + 1))
                    def nsum(t):
                        o = pN[:, bass.ds(t * (3 * K), 3 * K)]
                        mmul(o, lhsT=row(E, t), rhs=row(z3, t), start=True, stop=False, skip_group_check=True)
                        return mmul(o, lhsT=row(Fsel, t), rhs=tb3[:, :], start=False, stop=True, skip_group_check=True)
                    with pe.Fori(0, ET - 1, 1) as t:
                        nsum(t)
                    nsum(ET - 1).then_inc(s_na, 1)
                pe.wait_ge(s_rs, k + 1)
                mmul(pT[0:ET, 1, 0, :], lhsT=Lm[:, :], rhs=RC[:, 0:H], start=True, stop=True)
                mmul(pT[0:ET, 1, 1, 0:NP], lhsT=Lm[:, :], rhs=RC[:, H:R], start=True, stop=True).then_inc(s_co, 1)

            pe.wait_ge(s_dg, 1)
            for h in range(2):
                mm = mmul(pC[:, h * P:(h + 1) * P], lhsT=onesf[:, :], rhs=diag[:, h, :], start=True, stop=True)
            mm.then_inc(s_t, 1)
            for h in range(2):
                pe.wait_ge(s_fn, h + 1)
                for c in range(DC):
                    mm = nc.tensor.transpose(pT[:, h, c // 4, (c % 4) * P:(c % 4 + 1) * P], fn[:, h, c * P:(c + 1) * P], ident[:, :])
                mm.then_inc(s_t, 1)
            pe.wait_ge(s_fw, 16 * (EX + 3))
            pe.wait_ge(s_fT, 2)
            for e in range(EX):
                for c in range(DC):
                    mm = mmul(pA[0:FF, 0, e * TOPK:(e + 1) * TOPK], lhsT=w1e[:, e, c, :], rhs=fT[:, c, e * TOPK:(e + 1) * TOPK],
                              start=(c == 0), stop=(c == DC - 1))
            mm.then_inc(s_t, 1)
            pe.wait_ge(s_h1, 1)
            pe.wait_ge(s_g, 1)
            for h in range(2):
                for n in range(2):
                    o = pT[:, h, n, :]
                    for e in range(4 * h, 4 * h + 4):
                        mmul(o, lhsT=h1[:, e, :], rhs=w2e[:, e, n * 512:(n + 1) * 512], start=(e == 4 * h), stop=False)
                    mm = mmul(o, lhsT=esel[:, h, :], rhs=b2t[:, n * 512:(n + 1) * 512], start=False, stop=True)
                mm.then_inc(s_t, 1)
            pe.wait_ge(s_ct, 1)
            for h in range(2):
                for n in range(2):
                    for f in range(2):
                        mm = mmul(pT[:, h, n, :], lhsT=dq[:, f, h, :], rhs=ct[:, f, n * 512:(n + 1) * 512], start=(f == 0), stop=(f == 1))
            mm.then_inc(s_t, 1)

        @block.scalar
        def _(act):
            A = nc.scalar.activation
            act.wait_ge(s_eps, 1)

            def step(i, u):
                t = i + u
                if has(i, u, 1) and u >= -1:
                    act.wait_ge(s_T, t + 2)
                    if not early(i, u, 1):
                        act.wait_ge(s_mm, t)
                    A(xT[:, (u + 1) % 2, 4:8, :].rearrange("p a b -> p (a b)"), pT[:, (u + 1) % 2, 1, :], ACT.Copy).then_inc(s_eva, 1)
                if has(i, u, 2):
                    n = (u + 2) % 2
                    act.wait_ge(s_var, t + 3)
                    A(sdv[:, n:n + 1], recA[:, (u + 2) % XS, 1:2], ACT.Sqrt, bias=eps[:, :]).then_inc(s_std, 1)
                    act.wait_ge(s_rstd, t + 3)
                    if not early(i, u, 0):
                        act.wait_ge(s_T, t + 1)
                    A(xn[:, n, :], xr[:, (u + 2) % XS, :], ACT.Identity, bias=nmr[:, n:n + 1], scale=rsd[:, n:n + 1]).then_inc(s_xn, 1)
                if u >= 0:
                    act.wait_ge(s_o, t + 1)
                    if not early(i, u, 1):
                        act.wait_ge(s_sq, t * 2)
                    A(junka[:, 0, :], xr[:, u % XS, 0:H], ACT.Square, accum_out=recA[:, u % XS, 3:4]).then_inc(s_sq, 1)
                    A(junka[:, 1, :], xr[:, u % XS, H:D], ACT.Square, accum_out=recB[:, u % XS, 9:10]).then_inc(s_sq, 1)
                if (isinstance(i, int) and 0 <= t < XS) or (not isinstance(i, int) and in_ranks[0]):
                    if isinstance(i, int) and t == 0:
                        act.wait_ge(s_key, 1)
                    if not early(i, u, 1):
                        act.wait_ge(s_sgn, t)
                    A(junks[:, :], keyr[:, :], ACT.Sign, bias=dyn(key, t), scale=-1.0, accum_out=dyn(sgn, t)).then_inc(s_sgn, 1)

            in_ranks = [True]
            node_loop(act, step, lambda: in_ranks.clear() or in_ranks.append(False))

            for k in range(K):
                for g in range(GQ):
                    a, b = g * GT, (g + 1) * GT
                    act.wait_ge(s_pre, GQ * k + g + 1)
                    A(al[:, a:b], pre[:, a:b], ACT.Tanh, bias=bgb[:, k:k + 1]).then_inc(s_th, 1)
                    act.wait_ge(s_m, GQ * k + g + 1)
                    if k == 0:
                        act.wait_ge(s_E, g + 1)

                    def scale(i, u):
                        t = i + u
                        if not (k == 0 and g == 0 and isinstance(i, int) and i == 0):
                            act.wait_ge(s_wm, t + (ET * k - 1))
                        A(E32[:, u, :], row(E, t), ACT.Copy, scale=dyn(m, t)).then_inc(s_e32, 1)
                    group_tiles(act, k == 0 and g == 0, a, scale)

            def squares(t):
                act.wait_ge(s_fo, t + 1)
                if not isinstance(t, int):
                    act.wait_ge(s_fq, t)
                A(junkc[:, :], row(Z[:, :, 0:H], t), ACT.Square, accum_out=row(Z[:, :, H + 9:H + 10], t)).then_inc(s_fq, 1)
            squares(0)
            with act.Fori(1, ET, 1) as t:
                squares(t)
            act.wait_ge(s_fq, ET)
            act.wait_ge(s_sd, 1)
            A(junkc[0:ET, :], Sx[:, 0:H], ACT.Square, accum_out=Sx[:, H + 9:H + 10]).then_inc(s_sa, 1)

            act.wait_ge(s_nd, 32)
            A(q[0][:, :], ndA[:, :, 1], ACT.Sqrt, bias=eps[:, :]).then_inc(s_a1, 1)
            act.wait_ge(s_v2, 1)
            A(q[4][:, :], q[3][:, :], ACT.Sqrt, bias=eps[:, :]).then_inc(s_a1, 1)
            act.wait_ge(s_lg, 1)
            A(lt[:, :, :], lg[:, :, :], ACT.Exp).then_inc(s_a2, 1)
            for h in range(2):
                act.wait_ge(s_fv, h + 1)
                A(fsd[:, h:h + 1], fmv[:, h, 1:2], ACT.Sqrt, bias=eps[:, :]).then_inc(s_a3, 1)
            for h in range(2):
                act.wait_ge(s_fs2, h + 1)
                A(fn[:, h, :], fx[:, h, :], ACT.Identity, bias=fnm[:, h:h + 1], scale=frs[:, h:h + 1]).then_inc(s_fn, 1)
            act.wait_ge(s_t, 4)
            act.wait_ge(s_h0, 1)
            act.wait_ge(s_fw, 16 * (EX + 3))
            for e in range(EX):
                c = (e % 4) * TOPK
                ins = A(h1[:, e, c:c + TOPK], pA[0:FF, 0, e * TOPK:(e + 1) * TOPK], ACT.Relu, bias=b1t[:, e:e + 1])
            ins.then_inc(s_h1, 1)

        @block.vector
        def _(dve):
            v = nc.vector
            chain = [0]

            def link(ins):
                chain[0] += 1
                ins.then_inc(s_d, 1)
                dve.wait_ge(s_d, chain[0])

            v.memset(eps[:, :], EPS).then_inc(s_eps, 1)
            v.memset(ones[:, :], 1.0).then_inc(s_one, 1)
            v.memset(recA[:, :, :], 0.0)
            link(v.memset(recB[:, :, :], 0.0))

            dve.wait_ge(s_ei, 48)
            dve.wait_ge(s_pk, 1)
            v.tensor_copy(pairs[:, :, 0], ei[:, 0, :])
            v.tensor_copy(pairs[:, :, 1], ei[:, 1, :])
            link(v.tensor_copy(dstf[:, :], ei[:, 0, :]))
            v.tensor_scalar(key[:, :], dstf[:, :], float(P), pcol[:, :], ALU.mult, ALU.add)
            v.scalar_tensor_tensor(keyr[:, :], drow[0:EP, 0:NE], float(P), keyr[:, :], ALU.mult, ALU.add).then_inc(s_key, 1)
            v.tensor_tensor(eq[:, :, :], dstf[:, :].unsqueeze(2).to_broadcast([EP, EJ, EJ]),
                            dstf[:, :].unsqueeze(1).to_broadcast([EP, EJ, EJ]), ALU.is_equal).then_inc(s_eq, 1)
            dve.wait_ge(s_eq, 1)
            v.tensor_reduce(ceq[:, :], eq[:, :, :], AX.X, ALU.add).then_inc(s_eq, 1)
            dve.wait_ge(s_eq, 3)
            link(v.tensor_reduce(clt[:, :], eq[:, :, :], AX.X, ALU.add))
            link(v.tensor_scalar(c0[:, :], ceq[:, :], -0.5, NE / 2.0 + 1.0, ALU.mult, ALU.add))
            v.tensor_tensor(c0[:, :], c0[:, :], clt[:, :], ALU.add).then_inc(s_c0, 1)

            dve.wait_ge(s_w, 16 * NWL)
            for c in range(DC):
                dve.wait_ge(s_wt, c + 1)
                if c >= 2:
                    dve.wait_ge(s_wq, c - 1)
                v.tensor_copy(wT[:, c % 2, :, :].rearrange("p a b -> p (a b)"), pT[:, c % 2, 0, :]).then_inc(s_wc, 1)
                dve.wait_ge(s_wq, c + 1)
                v.tensor_copy(wext[:, c, H:H + NQ], pB[:, 0:NQ]).then_inc(s_we, 1)
            dve.wait_ge(s_wq, DC + 1)
            v.tensor_copy(b1e[:, H:R], pB[:, 0:NP])
            v.tensor_copy(bRa[:, :], pB[:, NP:NQ])
            v.tensor_copy(csrw[:, :], pC[:, 0:EX]).then_inc(s_we, 1)
            dve.wait_ge(s_we, DC + 1)

            def step(i, u):
                t = i + u
                if has(i, u, 2):
                    s, n = (u + 2) % XS, (u + 2) % 2
                    dve.wait_ge(s_x[s], slot16(i, u + 2))
                    v.bn_stats(bns[:, n, 0, :], xr[:, s, 0:H]).then_inc(s_bn, 1)
                    v.bn_stats(bns[:, n, 1, :], xr[:, s, H:D]).then_inc(s_bn, 1)
                    dve.wait_ge(s_bn, t * 2 + 6)
                    if not early(i, u, 2):
                        dve.wait_ge(s_sr[s], slot32(i, u - 2))
                if has(i, u, 1) and u >= -1:
                    dve.wait_ge(s_T, t + 2)
                    if not early(i, u, 1):
                        dve.wait_ge(s_mm, t)
                    v.tensor_copy(xT[:, (u + 1) % 2, 0:4, :].rearrange("p a b -> p (a b)"), pT[:, (u + 1) % 2, 0, :]).then_inc(s_evd, 1)
                if has(i, u, 2):
                    v.bn_aggr(recA[:, s, 0:2], bns[:, n, :, :].rearrange("p a b -> p (a b)")).then_inc(s_var, 1)
                    dve.wait_ge(s_std, t + 3)
                    v.reciprocal(rsd[:, n:n + 1], sdv[:, n:n + 1]).then_inc(s_rc, 1)
                    dve.wait_ge(s_rc, t + 3)
                    v.tensor_scalar(nmr[:, n:n + 1], recA[:, s, 0:1], rsd[:, n:n + 1], -1.0, ALU.mult, ALU.mult).then_inc(s_rstd, 1)
                if u >= 0:
                    s, n = u % XS, u % 2
                    dve.wait_ge(s_mm, t + 1)
                    if not early(i, u, 2):
                        dve.wait_ge(s_sg[n], slot16(i, u - 2, 2))
                    v.tensor_tensor(x1s[:, n, H:R], pBC[n][:, 0:NP], b1e[:, H:R], ALU.add).then_inc(s_rec, 1)
                    v.tensor_copy(recA[:, s, 8:24], pBC[n][:, NP:WX - H])
                    v.tensor_tensor(x1s[:, n, 0:H], pA[:, n, :], b1e[:, 0:H], ALU.add).then_inc(s_x1, 1)
                    dve.wait_ge(s_rec, t + 1)
                    v.tensor_copy(recB[:, s, 0:8], x1s[:, n, H + 8:R])
                    dve.wait_ge(s_x1, t + 1)
                    dve.wait_ge(s_xn, t + 1)
                    v.scalar_tensor_tensor(xr[:, s, 0:H], xr[:, s, 0:H], 1.0, x1s[:, n, 0:H], ALU.mult, ALU.add, accum_out=recA[:, s, 2:3])
                    v.scalar_tensor_tensor(xr[:, s, H:D], xr[:, s, H:D], 1.0, x1s[:, n, 0:H], ALU.mult, ALU.add, accum_out=recB[:, s, 8:9]).then_inc(s_o, 1)

            def slot16(i, u, ring=XS):
                return i * (16 // ring) + 16 * (u // ring + 1)

            def slot32(i, u, ring=XS):
                return i * (32 // ring) + 32 * (u // ring + 1)

            node_loop(dve, step)

            dve.wait_ge(s_tab, 1)
            dve.wait_ge(s_dr, 16)
            for g in range(GQ):
                with dve.Fori(g * GT, (g + 1) * GT, 1) as t:
                    v.tensor_scalar(row(E, t), drow[:, bass.ds(t * P, P)], dyn(curf, t), None, ALU.is_equal)
                    v.scalar_tensor_tensor(row(TBl, t).rearrange("p (a b) -> p a b", a=2), browf[:, :, :], dyn(curf, t),
                                           nown[:, :, bass.ds(ET - 1 - t, ET)], ALU.is_equal, ALU.mult)
                    v.tensor_scalar(row(Fsel, t), drow[0:2 * ET, bass.ds(t * P, P)], bcf[:, 0:1], dyn(own, t), ALU.is_equal, ALU.mult)
                v.memset(pre[:, g:g + 1], 0.0).then_inc(s_E, 1)

            for k in range(K):
                for g in range(GQ):
                    a, b = g * GT, (g + 1) * GT
                    dve.wait_ge(s_zg[g], 16 * GT * (k + 1))
                    if k == 0:
                        dve.wait_ge(s_vg[g], 16 * GT)
                        link(v.tensor_copy(Vpi[:, a:b, :], V[:, a:b, H:H + K]))
                    v.tensor_tensor(pre[:, a:b], Z[:, a:b, H + K + k], Vpi[:, a:b, k], ALU.add).then_inc(s_pre, 1)
                    dve.wait_ge(s_th, GQ * k + g + 1)
                    v.tensor_tensor(m[:, a:b], al[:, a:b], norm[:, a:b], ALU.mult).then_inc(s_m, 1)
                    if k < K - 1:
                        dve.wait_ge(s_m, GQ * k + g + 1)
                        mb = m[:, a:b].unsqueeze(2).to_broadcast([P, GT, K])
                        link(v.tensor_tensor(zf[:, :, :], Z[:, a:b, H:H + K], mb, ALU.mult))
                        link(v.tensor_copy(z3[:, a:b, 0:K], zf[:, :, :]))
                        link(v.tensor_tensor(zf[:, :, :], zf[:, :, :], z3[:, a:b, 0:K], ALU.subtract))
                        link(v.tensor_copy(z3[:, a:b, K:2 * K], zf[:, :, :]))
                        link(v.tensor_tensor(zf[:, :, :], zf[:, :, :], z3[:, a:b, K:2 * K], ALU.subtract))
                        v.tensor_copy(z3[:, a:b, 2 * K:3 * K], zf[:, :, :]).then_inc(s_z3, 1)

                    def add(i, u):
                        t = i + u
                        dve.wait_ge(s_wm, t + (ET * k + 1))
                        vt = row(V[:, :, 0:H], t)
                        vp = row(V[:, :, H:R], t)
                        v.tensor_tensor(vt, vt, pA[:, u, :], ALU.add)
                        v.tensor_tensor(vp, vp, pBC[u][:, 0:NP], ALU.add).then_inc(s_va, 1)
                    group_tiles(dve, k == 0 and g == 0, a, add)
                if k < K - 1:
                    dve.wait_ge(s_tb, k + 1)
                    tc = 4 * k
                    v.tensor_copy(tbf[:, :], pC[0:2 * ET, 0:3 * K]).then_inc(s_tc, 1)
                    dve.wait_ge(s_tc, tc + 1)
                    link(v.tensor_tensor(tbf[:, 0:K], tbf[:, 0:K], tbf[:, K:2 * K], ALU.add))
                    link(v.tensor_tensor(tbf[:, 0:K], tbf[:, 0:K], tbf[:, 2 * K:3 * K], ALU.add))
                    v.tensor_copy(tb3[:, 0:K], tbf[:, 0:K]).then_inc(s_tc, 1)
                    dve.wait_ge(s_tc, tc + 2)
                    link(v.tensor_tensor(tbf[:, 0:K], tbf[:, 0:K], tb3[:, 0:K], ALU.subtract))
                    v.tensor_copy(tb3[:, K:2 * K], tbf[:, 0:K]).then_inc(s_tc, 1)
                    dve.wait_ge(s_tc, tc + 3)
                    link(v.tensor_tensor(tbf[:, 0:K], tbf[:, 0:K], tb3[:, K:2 * K], ALU.subtract))
                    v.tensor_copy(tb3[:, 2 * K:3 * K], tbf[:, 0:K]).then_inc(s_tc, 1)
                    dve.wait_ge(s_na, k + 1)
                    nar = pN[:, 0:3 * K * ET].rearrange("p (t c) -> p t c", c=3 * K)
                    for s in range(3):
                        link(v.tensor_tensor(Vpi[:, :, :], Vpi[:, :, :], nar[:, :, s * K:(s + 1) * K], ALU.add))
                if k == 0:
                    dve.wait_ge(s_r0, 16)
                dve.wait_ge(s_rl, 16 * (k + 1))
                v.tensor_tensor(RC[:, :], RC[:, :], RC0[:, :], ALU.subtract).then_inc(s_rs, 1)
                dve.wait_ge(s_co, k + 1)
                if k:
                    dve.wait_ge(s_ca, 16 * k)
                v.tensor_copy(corr[:, 0:H], pT[0:ET, 1, 0, :])
                v.tensor_copy(corr[:, H:R], pT[0:ET, 1, 1, 0:NP]).then_inc(s_cc, 1)

            def final(t):
                zr = row(Z[:, :, 0:H], t)
                v.scalar_tensor_tensor(zr, zr, 1.0, row(V[:, :, 0:H], t), ALU.mult, ALU.add, accum_out=row(Z[:, :, H + 8:H + 9], t))
                v.tensor_copy(row(Z[:, :, H:H + 8], t), row(V[:, :, H + 8:R], t)).then_inc(s_fo, 1)
            for g in range(GQ):
                dve.wait_ge(s_xg[g], 16 * GT)
                with dve.Fori(g * GT, (g + 1) * GT, 1) as t:
                    final(t)
            link(v.memset(Sx[:, :], 0.0))
            v.memset(Sv[:, :], 0.0).then_inc(s_sz, 1)
            dve.wait_ge(s_sp, 32)
            v.tensor_copy(Sx[:, H:H + 8], Sv[:, H + 8:R])
            v.scalar_tensor_tensor(Sx[:, 0:H], Sx[:, 0:H], 1.0, Sv[:, 0:H], ALU.mult, ALU.add, accum_out=Sx[:, H + 8:H + 9]).then_inc(s_sd, 1)

            dve.wait_ge(s_nd, 32)
            link(v.tensor_tensor(q[1][:, :], ndA[:, :, 2], ndB[:, :, 8], ALU.add))
            link(v.tensor_scalar(q[1][:, :], q[1][:, :], 1.0 / D, None, ALU.mult))
            link(v.tensor_tensor(q[2][:, :], ndA[:, :, 3], ndB[:, :, 9], ALU.add))
            link(v.tensor_tensor(q[5][:, :], q[1][:, :], q[1][:, :], ALU.mult))
            v.scalar_tensor_tensor(q[3][:, :], q[2][:, :], 1.0 / D, q[5][:, :], ALU.mult, ALU.subtract).then_inc(s_v2, 1)
            dve.wait_ge(s_v2, 1)
            link(v.tensor_tensor(q[2][:, :], ndA[:, :, 0], q[1][:, :], ALU.subtract))
            dve.wait_ge(s_a1, 1)
            b8 = lambda ap: ap[:, :].unsqueeze(2).to_broadcast([P, NT, EX])
            c8 = lambda ap: ap[:, :].unsqueeze(1).to_broadcast([P, NT, EX])
            link(v.tensor_tensor(lt[:, :, :], ndA[:, :, 16:24], b8(q[0]), ALU.mult))
            link(v.tensor_tensor(lg[:, :, :], ndA[:, :, 8:16], lt[:, :, :], ALU.add))
            link(v.tensor_tensor(lg[:, :, :], lg[:, :, :], ndB[:, :, 0:8], ALU.add))
            link(v.tensor_tensor(lg[:, :, :], lg[:, :, :], c8(bRa), ALU.add))
            link(v.tensor_tensor(lt[:, :, :], b8(q[2]), c8(csrw), ALU.mult))
            link(v.tensor_tensor(lg[:, :, :], lg[:, :, :], lt[:, :, :], ALU.add))
            dve.wait_ge(s_a1, 2)
            link(v.reciprocal(q[4][:, :], q[4][:, :]))
            link(v.tensor_tensor(lg[:, :, :], lg[:, :, :], b8(q[4]), ALU.mult))
            link(v.tensor_tensor(lg[:, :, :], lg[:, :, :], c8(rbb), ALU.add))
            link(v.tensor_reduce(q[1][:, :], lg[:, :, :], AX.X, ALU.max))
            v.tensor_tensor(lg[:, :, :], lg[:, :, :], b8(q[1]), ALU.subtract).then_inc(s_lg, 1)
            dve.wait_ge(s_a2, 1)
            link(v.tensor_reduce(q[2][:, :], lt[:, :, :], AX.X, ALU.add))
            link(v.reciprocal(q[3][:, :], q[2][:, :]))
            v.tensor_tensor(sct[:, :, :].rearrange("p e j -> p j e"), lt[:, :, :], b8(q[3]), ALU.mult).then_inc(s_sc, 1)

            def best(vals, idx, data):
                for r in range(TOPK // 8):
                    o = slice(8 * r, 8 * r + 8)
                    link(v.max(vals[:, o], data[:, :]))
                    link(v.max_index(idx[:, o], vals[:, o], data[:, :]))
                    if r < TOPK // 8 - 1:
                        link(v.match_replace(data[:, :], vals[:, o], data[:, :], -2.0))
            dve.wait_ge(s_q[1], 16)
            best(tv, ti, tk)
            link(v.tensor_copy(tif[:, :], ti[:, :]))
            dve.wait_ge(s_g, 1)
            v.tensor_scalar(tgi[:, :], tif[:, :], tbase[:, :], None, ALU.add).then_inc(s_l1, 1)
            link(v.memset(onesf[:, :], 1.0))
            v.memset(h1[:, :, :], 0.0).then_inc(s_h0, 1)
            dve.wait_ge(s_q[4], 16)
            best(gv, gi, cv)
            link(v.tensor_copy(gif[:, :], gi[:, :]))
            v.tensor_scalar(gpi[:, :], gif[:, :], gbase[:, :], None, ALU.add).then_inc(s_l2, 1)

            dve.wait_ge(s_q[8], 32)
            link(v.tensor_copy(tokf[:, :], tokw[:, :]))
            link(v.tensor_tensor(tokf[:, :], tokf[:, :], ebase[:, :], ALU.subtract))
            v.tensor_copy(tok[:, :], tokf[:, :]).then_inc(s_tk, 1)
            for h in range(2):
                ins = v.tensor_scalar(diag[:, h, :], ident[:, :], tokf[:, h:h + 1], None, ALU.mult)
            ins.then_inc(s_dg, 1)
            dve.wait_ge(s_t, 1)
            for f in range(2):
                for h in range(2):
                    ins = v.tensor_scalar(dq[:, f, h, :], pC[:, h * P:(h + 1) * P], tokf[:, f:f + 1], None, ALU.is_equal)
            ins.then_inc(s_dq, 1)
            for h in range(2):
                dve.wait_ge(s_fx[h], 16)
                v.bn_stats(fst[:, h, 0, :], fx[:, h, 0:H])
                link(v.bn_stats(fst[:, h, 1, :], fx[:, h, H:D]))
                v.bn_aggr(fmv[:, h, :], fst[:, h, :, :].rearrange("p a b -> p (a b)")).then_inc(s_fv, 1)
            for h in range(2):
                dve.wait_ge(s_a3, h + 1)
                link(v.reciprocal(frs[:, h:h + 1], fsd[:, h:h + 1]))
                v.tensor_scalar(fnm[:, h:h + 1], fmv[:, h, 0:1], frs[:, h:h + 1], -1.0, ALU.mult, ALU.mult).then_inc(s_fs2, 1)
            dve.wait_ge(s_lo, 1)
            link(v.tensor_reduce(tw[:, 0:1], dlo[:, 0, 0, :], AX.X, ALU.add))
            link(v.tensor_reduce(tw[:, 1:2], dlo[:, 1, :, :], AX.XY, ALU.add))
            link(v.tensor_scalar(tw[:, 2:4], tw[:, 0:2], 1.0, FAR, ALU.min, ALU.mult))
            link(v.tensor_tensor(tw[:, 4:6], tw[:, 2:4], tokf[:, :], ALU.add))
            v.tensor_copy(tokw[:, :], tw[:, 4:6]).then_inc(s_tw, 1)
            for h in range(2):
                dve.wait_ge(s_t, 2 + h)
                v.tensor_copy(fT[:, 0:4, h * P:(h + 1) * P], pT[:, h, 0, :].rearrange("p (a b) -> p a b", b=P))
                v.tensor_copy(fT[:, 4:8, h * P:(h + 1) * P], pT[:, h, 1, :].rearrange("p (a b) -> p a b", b=P)).then_inc(s_fT, 1)
            dve.wait_ge(s_q[7], 16)
            for h in range(2):
                dve.wait_ge(s_t, 5 + h)
                for n in range(2):
                    ins = v.tensor_scalar(ct[:, h, n * 512:(n + 1) * 512], pT[:, h, n, :], gcol[:, h:h + 1], None, ALU.mult)
            ins.then_inc(s_ct, 1)
            dve.wait_ge(s_t, 7)
            dve.wait_ge(s_fn, 2)
            for h in range(2):
                for n in range(2):
                    o = slice(n * 512, (n + 1) * 512)
                    ins = v.tensor_tensor(fx[:, h, o], fx[:, h, o], pT[:, h, n, :], ALU.add)
            ins.then_inc(s_fz, 1)

        @block.gpsimd
        def _(pool):
            g_ = nc.gpsimd
            chain = [0]

            def link(ins):
                chain[0] += 1
                ins.then_inc(s_p, 1)
                pool.wait_ge(s_p, chain[0])

            dmas = [0]

            def dma_all(issue):
                dmas[0] += issue()
                pool.wait_ge(s_pd, 16 * dmas[0])

            link(g_.memset(ident[:, :], 0.0))
            g_.affine_select(out=ident[:, :], in_=ident[:, :], compare_op=ALU.not_equal, fill=1.0, base=0,
                             pattern=[[-1, P]], channel_multiplier=1).then_inc(s_id, 1)
            g_.iota(pcol[:, :], [[0, 1]], base=0, channel_multiplier=1, allow_small_or_imprecise_dtypes=True)
            g_.iota(keyr[:, :], [[1, EP], [0, EJ]], base=0, channel_multiplier=0, allow_small_or_imprecise_dtypes=True).then_inc(s_pk, 1)
            npad = EPAD - NE
            g_.memset(padi[:, 0:2], -1)
            g_.memset(padi[:, 2:2 + 2 * npad], PADV)
            link(g_.memset(padi[:, 2 + 2 * npad:4 + 2 * npad], 2 * NPAD))
            link(g_.memset(zt[:, :], 0.0))
            def init():
                pool.dma_start(SO[0:1, :], padi[:, 0:2]).then_inc(s_pd, 16)
                pool.dma_start(SO[NE + 1:EPAD + 2, :].rearrange("(a n) c -> a (n c)", a=1), padi[:, 2:4 + 2 * npad]).then_inc(s_pd, 16)
                pool.dma_start(T.rearrange("(p n) a -> p (n a)", p=P), zt[:, :]).then_inc(s_pd, 16)
                return 3
            dma_all(init)
            pool.wait_ge(s_eq, 2)
            g_.affine_select(out=eq[:, :, :], in_=eq[:, :, :], compare_op=ALU.is_gt, fill=0.0, base=0,
                             pattern=[[1, EJ], [-1, EJ]], channel_multiplier=0).then_inc(s_eq, 1)
            g_.iota(slot[:, :], [[P, ET]], base=0, channel_multiplier=1, allow_small_or_imprecise_dtypes=True)
            g_.iota(slot1[:, :], [[P, ET]], base=1, channel_multiplier=1, allow_small_or_imprecise_dtypes=True)
            g_.iota(fbase[:, :], [[0, 1]], base=-1, channel_multiplier=P, allow_small_or_imprecise_dtypes=True)
            link(g_.memset(nown[:, :, :], 1.0))
            link(g_.memset(nown[:, :, ET - 1:ET], 0.0))
            link(g_.memset(own[:, :], 1.0))
            link(g_.affine_select(out=own[:, :], in_=own[:, :], compare_op=ALU.not_equal, fill=0.0, base=0,
                                  pattern=[[-1, ET]], channel_multiplier=1))
            link(g_.affine_select(out=own[:, :], in_=own[:, :], compare_op=ALU.not_equal, fill=0.0, base=-ET,
                                  pattern=[[-1, ET]], channel_multiplier=1))
            link(g_.tensor_scalar(own[:, :], own[:, :], -1.0, 1.0, ALU.mult, ALU.add))

            pool.wait_ge(s_sgn, EJ)
            pool.wait_ge(s_c0, 1)
            link(g_.tensor_scalar(posf[:, :], sgn[:, :], 0.5, 0.0, ALU.mult, ALU.add))
            link(g_.tensor_tensor(posf[:, :], posf[:, :], c0[:, :], ALU.add))
            link(g_.tensor_copy(posi[:, :], posf[:, :]))

            def scatter(dst_, idx, src_, bound, s):
                pool.indirect_dma_start(out=dst_, out_offset=bass.IndirectOffsetOnAxis(ap=idx, axis=0), in_=src_, in_offset=None,
                                        bounds_check=bound, oob_is_err=False).then_inc(s, 16)

            def gather(dst_, src_, idx, bound, s):
                pool.indirect_dma_start(out=dst_, out_offset=None, in_=src_, in_offset=bass.IndirectOffsetOnAxis(ap=idx, axis=0),
                                        bounds_check=bound, oob_is_err=False).then_inc(s, 16)

            def sort():
                for j in range(EJ):
                    scatter(SO[:, :], posi[:, j:j + 1], pairs[:, j, :], EPAD + 1, s_pd)
                return EJ
            dma_all(sort)

            def sorted_loads():
                for o, tile in ((1, cur), (2, nxt), (0, prv)):
                    pool.dma_start(tile[:, :, :], SO[o:o + EPAD, :].rearrange("(t p) c -> p t c", p=P)).then_inc(s_pd, 16)
                pool.dma_start(curR[:, :, :], SO[1:1 + EPAD, :].rearrange("(t p) c -> t p c", p=P)).then_inc(s_pd, 16)
                tiles = SO[1:1 + EPAD, :].rearrange("(t p) c -> p t c", p=P)
                with nc.allow_non_contiguous_dma(reason="boundary nodes"):
                    for s, r in ((0, 0), (1, P - 1)):
                        pool.dma_start(brow[:, s, :], tiles[r, :, 0].unsqueeze(0).to_broadcast([P, ET])).then_inc(s_pd, 16)
                        pool.dma_start(bcol[s * ET:(s + 1) * ET, 0:1], tiles[r, :, 0:1]).then_inc(s_pd, 16)
                        pool.dma_start(bcol[0:ET, 1 + s:2 + s], tiles[r, :, 0:1]).then_inc(s_pd, 16)
                        pool.dma_start(bcol[ET:2 * ET, 1 + s:2 + s], tiles[r, :, 0:1]).then_inc(s_pd, 16)
                return 12
            dma_all(sorted_loads)
            link(g_.tensor_copy(dR[:, :], curR[:, :, 0]))

            def rows_out():
                pool.dma_start(SD.rearrange("(t p) -> t p", p=P), dR[:, :]).then_inc(s_pd, 16)
                return 1
            dma_all(rows_out)
            pool.wait_ge(s_key, 1)
            pool.dma_start(drow[:, :], SD.rearrange("(a n) -> a n", a=1).to_broadcast([P, EPAD])).then_inc(s_dr, 16)

            def f32(dst_, src_):
                link(g_.tensor_copy(dst_, src_))
            f32(curf[:, :], cur[:, :, 0])
            f32(w[0][:, :], nxt[:, :, 0])
            f32(w[1][:, :], prv[:, :, 0])
            f32(w[2][:, :], cur[:, :, 1])
            f32(browf[:, :, :], brow[:, :, :])
            f32(bcf[:, :], bcol[:, :])
            f32(dRf[:, :], dR[:, :])
            sub = lambda o, a, b: link(g_.tensor_tensor(o, a, b, ALU.subtract))
            add = lambda o, a, b: link(g_.tensor_tensor(o, a, b, ALU.add))
            ts = lambda o, a, s1, s2, o0, o1: link(g_.tensor_scalar(o, a, s1, s2, o0, o1))
            sub(w[3][:, :], w[0][:, :], curf[:, :])
            ts(w[3][:, :], w[3][:, :], 0.0, FAR, ALU.is_equal, ALU.mult)
            sub(w[4][:, :], curf[:, :], w[1][:, :])
            ts(w[4][:, :], w[4][:, :], 0.0, FAR, ALU.is_equal, ALU.mult)
            ts(w[5][:, :], curf[:, :], 2.0, 0.0, ALU.mult, ALU.add)
            ts(w[6][:, :], curf[:, :], 2.0, 1.0, ALU.mult, ALU.add)
            add(w[4][:, :], w[4][:, :], w[5][:, :])
            link(g_.tensor_copy(ifst[:, :], w[4][:, :]))
            add(w[7][:, :], w[3][:, :], w[6][:, :])
            link(g_.tensor_copy(ilst[:, :], w[7][:, :]))
            link(g_.tensor_copy(iout[:, :], w[7][:, :]))
            add(w[8][:, :], w[3][:, :], curf[:, :])
            link(g_.tensor_copy(inode[:, :], w[8][:, :]))
            link(g_.tensor_copy(ixr[:, :], w[6][:, :]))
            link(g_.tensor_copy(isrc[:, :], w[2][:, :]))
            link(g_.tensor_copy(idst[:, :], curf[:, :]))
            link(g_.tensor_copy(ilast[:, :], bcf[0:ET, 2:3]))
            link(g_.tensor_copy(ifn[:, :], bcf[0:ET, 1:2]))

            def spans():
                for t in range(ET):
                    scatter(T, ifst[:, t:t + 1], slot[:, t:t + 1], 2 * NPAD - 1, s_pd)
                    scatter(T, ilst[:, t:t + 1], slot1[:, t:t + 1], 2 * NPAD - 1, s_pd)
                return 2 * ET
            dma_all(spans)
            T2 = T.rearrange("(n c) a -> n (c a)", c=2)

            def span_rows():
                for t in range(ET):
                    gather(TS[:, t, :], T2, isrc[:, t:t + 1], NPAD - 1, s_pd)
                    gather(TD[:, t, :], T2, idst[:, t:t + 1], NPAD - 1, s_pd)
                gather(TL[:, :], T2, ifn[:, :], NPAD - 1, s_pd)
                return 2 * ET + 1
            dma_all(span_rows)
            sub(w[9][:, :], TS[:, :, 1], TS[:, :, 0])
            sub(w[10][:, :], TD[:, :, 1], TD[:, :, 0])
            ts(w[0][:, :], w[9][:, :], 0.0, FAR, ALU.is_equal, ALU.mult)
            add(w[0][:, :], w[0][:, :], TS[:, :, 1])
            ts(w[0][:, :], w[0][:, :], 1.0, -1.0, ALU.mult, ALU.add)
            link(g_.tensor_copy(ilsrc[:, :], w[0][:, :]))
            ts(w[9][:, :], w[9][:, :], 1.0, 0.0, ALU.max, ALU.add)
            ts(w[10][:, :], w[10][:, :], 1.0, 0.0, ALU.max, ALU.add)
            link(g_.tensor_tensor(w[9][:, :], w[9][:, :], w[10][:, :], ALU.mult))
            link(g_.memset(mhalf[:, :], -0.5))
            link(g_.tensor_tensor(norm[:, :], w[9][:, :], mhalf[:, :], ALU.pow))
            sub(ovl[:, :], bcf[:, 1:2], bcf[:, 2:3])
            ts(ovl[:, :], ovl[:, :], 0.0, 1.0, ALU.is_equal, ALU.mult)
            ts(ovl[:, :], ovl[:, :], -1.0, 1.0, ALU.mult, ALU.add)
            link(g_.memset(ovl[0:ET, :], 1.0))
            ts(own[:, :], own[:, :], ovl[:, :], 0.0, ALU.mult, ALU.add)
            ts(sm[:, 0:1], bcf[0:ET, 2:3], 1.0, 0.0, ALU.mult, ALU.add)
            ts(Lm[:, :], browf[0:ET, 0, :], sm[:, 0:1], 1.0, ALU.is_equal, ALU.mult)
            link(g_.affine_select(out=Lm[:, :], in_=Lm[:, :], compare_op=ALU.is_gt, fill=0.0, base=0,
                                  pattern=[[1, ET]], channel_multiplier=-1))
            ts(sm[:, 1:2], fbase[:, :], 1.0, float(P), ALU.mult, ALU.add)
            ts(sm[:, 2:3], TL[:, 1:2], 1.0, -1.0, ALU.mult, ALU.add)
            ts(sm[:, 3:4], sm[:, 2:3], sm[:, 1:2], 0.0, ALU.min, ALU.add)
            link(g_.tensor_copy(fidx[:, :], sm[:, 3:4]))
            sub(sm[:, 4:5], sm[:, 2:3], sm[:, 3:4])
            ts(sm[:, 4:5], sm[:, 4:5], 0.0, FAR, ALU.is_gt, ALU.mult)
            ts(sm[:, 5:6], bcf[0:ET, 1:2], 2.0, 1.0, ALU.mult, ALU.add)
            add(sm[:, 6:7], sm[:, 4:5], sm[:, 5:6])
            link(g_.tensor_copy(ispo[:, :], sm[:, 6:7]))
            link(g_.tensor_copy(ispx[:, :], sm[:, 5:6]))
            add(sm[:, 7:8], sm[:, 4:5], bcf[0:ET, 1:2])
            link(g_.tensor_copy(ispn[:, :], sm[:, 7:8]))
            pool.wait_ge(s_p, chain[0])
            g_.memset(mhalf[:, 0:1], 0.0).then_inc(s_tab, 1)

            pool.wait_ge(s_sg[0], 16 * ((NT + 1) // 2))
            pool.wait_ge(s_sg[1], 16 * (NT // 2))
            for s in range(XS):
                n = (NT - s + XS - 1) // XS
                pool.wait_ge(s_st[s], 16 * n)
                pool.wait_ge(s_sr[s], 32 * n)
            pool.wait_ge(s_mm, NT)
            for g in range(GQ):
                for t in range(g * GT, (g + 1) * GT):
                    gather(Z[:, t, :], G, isrc[:, t:t + 1], NPAD - 1, s_zg[g])
                if g == 0:
                    pool.wait_ge(s_E, GQ)
                for t in range(g * GT, (g + 1) * GT):
                    gather(V[:, t, :], G, idst[:, t:t + 1], NPAD - 1, s_vg[g])
            gather(RC0[:, :], G, ilast[:, :], NPAD - 1, s_r0)

            for k in range(K):
                if k == K - 1:
                    for g in range(GQ):
                        pool.wait_ge(s_wm, ET * k + GT * (g + 1))
                        for t in range(g * GT, (g + 1) * GT):
                            gather(Z[:, t, 0:H], xh, ixr[:, t:t + 1], 2 * N - 1, s_xg[g])
                for g in range(GQ):
                    pool.wait_ge(s_vw[g], 16 * (k + 1))
                pool.wait_ge(s_cc, k + 1)
                pool.indirect_dma_start(out=Vd[k % 2], out_offset=bass.IndirectOffsetOnAxis(ap=fidx[:, :], axis=0), in_=corr[:, :],
                                        in_offset=None, bounds_check=EPAD - 1, oob_is_err=True, compute_op=ALU.add).then_inc(s_ca, 16)
                pool.wait_ge(s_ca, 16 * (k + 1))
                if k < K - 1:
                    for g in range(GQ):
                        for t in range(g * GT, (g + 1) * GT):
                            gather(Z[:, t, :], Vd[k % 2], ilsrc[:, t:t + 1], EPAD - 1, s_zg[g])

            pool.wait_ge(s_sz, 1)
            gather(Sv[:, :], Vd[(K - 1) % 2], fidx[:, :], EPAD - 1, s_sp)
            gather(Sx[:, 0:H], xh, ispx[:, :], 2 * N - 1, s_sp)
            for t in range(ET):
                pool.wait_ge(s_fq, t + 1)
                scatter(outh, iout[:, t:t + 1], Z[:, t, 0:H], 2 * N - 1, s_fs)
                scatter(NDB, inode[:, t:t + 1], Z[:, t, H:R], NPAD - 1, s_fs)
            pool.wait_ge(s_fs, 16 * 2 * ET)
            pool.wait_ge(s_sa, 1)
            scatter(outh, ispo[:, :], Sx[:, 0:H], 2 * N - 1, s_ss)
            scatter(NDB, ispn[:, :], Sx[:, H:R], NPAD - 1, s_ss)
            pool.wait_ge(s_ss, 32)

            link(g_.iota(tbase[:, :], [[0, 1]], base=0, channel_multiplier=NPAD // 16, allow_small_or_imprecise_dtypes=True))
            link(g_.iota(gbase[:, :], [[0, 1]], base=0, channel_multiplier=16 * TOPK, allow_small_or_imprecise_dtypes=True))
            for r in range(4):
                for h in range(2):
                    link(g_.memset(ebase[32 * r:32 * r + 32, h:h + 1], float(NPAD * (4 * h + r))))
            link(g_.memset(esel[:, :, :], 1.0))
            for h in range(2):
                link(g_.affine_select(out=esel[:, h, :], in_=esel[:, h, :], compare_op=ALU.is_ge, fill=0.0, base=P * h,
                                      pattern=[[1, P]], channel_multiplier=-TOPK))
                link(g_.affine_select(out=esel[:, h, :], in_=esel[:, h, :], compare_op=ALU.is_ge, fill=0.0, base=TOPK - 1 - P * h,
                                      pattern=[[-1, P]], channel_multiplier=TOPK))
            g_.memset(tw[:, :], 0.0).then_inc(s_g, 1)
            pool.wait_ge(s_sc, 1)
            g_.affine_select(out=sct[:, :, :], in_=sct[:, :, :], compare_op=ALU.is_ge, fill=-1.0, base=N - 1,
                             pattern=[[0, EX], [-1, NT]], channel_multiplier=-NT).then_inc(s_msk, 1)
            pool.wait_ge(s_q[6], 16)
            pool.wait_ge(s_q[3], 16)
            for h in range(2):
                gather(tokw[:, h:h + 1], CI, pcl[:, h:h + 1], P * TOPK - 1, s_q[8])
            pool.wait_ge(s_tk, 1)
            for h in range(2):
                gather(fx[:, h, :], out, tok[:, h:h + 1], N - 1, s_fx[h])
            pool.wait_ge(s_dq, 1)
            g_.affine_select(out=dlo[:, 0, 0, :], in_=dq[:, 0, 0, :], compare_op=ALU.is_gt, fill=0.0, base=0,
                             pattern=[[-1, P]], channel_multiplier=1)
            g_.affine_select(out=dlo[:, 1, 1, :], in_=dq[:, 1, 1, :], compare_op=ALU.is_gt, fill=0.0, base=0,
                             pattern=[[-1, P]], channel_multiplier=1)
            g_.tensor_copy(dlo[:, 1, 0, :], dq[:, 1, 0, :]).then_inc(s_lo, 1)
            pool.wait_ge(s_fz, 1)
            pool.wait_ge(s_tw, 1)
            for h in range(2):
                scatter(out, tokw[:, h:h + 1], fx[:, h, :], N - 1, s_q[9])
            pool.wait_ge(s_q[9], 32)


_INS = ["x", "src", "dst", "L0_gnn_W1", "L0_gnn_b1", "L0_gnn_Wg", "L0_gnn_bg", "L0_ffn_router_w", "L0_ffn_router_b",
        "L0_ffn_w1", "L0_ffn_b1", "L0_ffn_w2", "L0_ffn_b2"]


def kernel(**inputs):
    import numpy as _np
    import concourse.bacc as _bacc
    from concourse import mybir as _mybir
    from concourse.bass_utils import run_bass_kernel_spmd as _run

    nc = _bacc.Bacc("TRN2", target_bir_lowering=False, num_devices=1)
    arrays, args = {}, []
    for name in _INS:
        a = _np.ascontiguousarray(inputs[name])
        arrays[f"in_{name}"] = a
        args.append(nc.dram_tensor(f"in_{name}", a.shape, _mybir.dt.from_np(a.dtype), kind="ExternalInput").ap())
    f32, i32 = _mybir.dt.float32, _mybir.dt.int32
    args.append(nc.dram_tensor("out_0", inputs["x"].shape, f32, kind="ExternalOutput").ap())

    def scratch(name, shape, dt):
        return nc.dram_tensor(name, shape, dt, kind="Internal").ap()

    npad, epad = 10112, 5120
    args += [scratch("node_rows", (npad, 528), f32), scratch("sorted_pairs", (epad + 2, 2), i32),
             scratch("sorted_dst", (epad,), i32), scratch("spans", (2 * npad, 1), f32),
             [scratch("v_even", (epad, 528), f32), scratch("v_odd", (epad, 528), f32)],
             scratch("node_left", (npad, 24), f32), scratch("node_right", (npad, 16), f32),
             scratch("scores", (8, npad), f32), scratch("cand_values", (4096,), f32),
             scratch("cand_numbers", (4096, 1), i32), scratch("chosen", (512,), i32)]
    gnn_ffn(nc, *args)
    r = _run(nc, [arrays], core_ids=[0])
    return r.results[0]["out_0"]
```

```python
from contextlib import ExitStack

import concourse.bass as bass
from concourse import mybir

F32 = mybir.dt.float32
BF16 = mybir.dt.bfloat16
I32 = mybir.dt.int32
U32 = mybir.dt.uint32
F32R = mybir.dt.float32r
ALU = mybir.AluOpType
ACT = mybir.ActivationFunctionType
AX = mybir.AxisListType

P = 128
EPS = 1e-5
FAR = 1000000.0


def gnn_ffn(nc, x, src, dst, W1, b1, Wg, bg, rw, rb, fw1, fb1, fw2, fb2, out,
            G, SO, SD, T, Vd, NDA, NDB, SC, CV, CI, PQ):
    N, D = x.shape
    H = W1.shape[1]
    K = Wg.shape[0]
    NE = src.shape[0]
    EX, FF = fb1.shape
    NT = (N + P - 1) // P
    LAST = N - (NT - 1) * P
    NPAD = NT * P
    DC = D // P
    HC = H // P
    NP = 2 * K + EX
    WHALF = (H + NP + 2 * EX) // 2
    R = H + NP
    NQ = NP + EX
    WX = H + NQ + EX
    ET = (NE + P - 1) // P
    EJ = ET
    EP = NE // EJ
    EPAD = ET * P
    PADV = NPAD - 1
    GQ = 8
    GT = ET // GQ
    TOPK = 32
    XS = 6
    AHEAD = 4
    assert EP * EJ == NE and NT == 79 and NP == 16 and XS % 2 == 0

    xh = x.rearrange("n (h c) -> (n h) c", h=2)
    outh = out.rearrange("n (h c) -> (n h) c", h=2)

    with ExitStack() as ctx:
        def sb(name, shape, dt=F32, c=ctx):
            return c.enter_context(nc.sbuf_tensor(name, shape, dt))

        def sem(name):
            return ctx.enter_context(nc.semaphore(name))

        ident = sb("ident", [P, P])
        E = sb("E", [P, ET, P], BF16)
        Fsel = sb("Fsel", [2 * ET, ET, P], BF16)
        TBl = sb("TBl", [P, ET, 2 * ET], BF16)
        norm = sb("norm", [P, ET])
        m = sb("m", [P, ET])
        pre = sb("pre", [P, ET])
        al = sb("al", [P, ET])
        Vpi = sb("Vpi", [P, ET, K])
        bgb = sb("bgb", [P, K])
        rbb = sb("rbb", [P, EX])
        csrw = sb("csrw", [P, EX])
        bRa = sb("bRa", [P, EX])
        curf = sb("curf", [P, ET])
        isrc = sb("isrc", [P, ET], I32)
        idst = sb("idst", [P, ET], I32)
        ilsrc = sb("ilsrc", [P, ET], I32)
        iout = sb("iout", [P, ET], I32)
        inode = sb("inode", [P, ET], I32)
        ixr = sb("ixr", [P, ET], I32)
        Lm = sb("Lm", [ET, ET])
        fidx = sb("fidx", [ET, 1], I32)
        ilast = sb("ilast", [ET, 1], I32)
        ispo = sb("ispo", [ET, 1], I32)
        ispn = sb("ispn", [ET, 1], I32)
        ispx = sb("ispx", [ET, 1], I32)
        eps = sb("eps", [P, 1])

        with ExitStack() as c:
            Z = sb("Z", [P, ET, R], c=c)
            V = sb("V", [P, ET, R], c=c)
            E32 = sb("E32", [P, 2, P], c=c)
            RC = sb("RC", [ET, R], c=c)
            RC0 = sb("RC0", [ET, R], c=c)
            corr = sb("corr", [ET, R], c=c)
            zf = sb("zf", [P, GT, K], c=c)
            z3 = sb("z3", [P, ET, 3 * K], BF16, c=c)
            tbf = sb("tbf", [2 * ET, 3 * K], c=c)
            tb3 = sb("tb3", [2 * ET, 3 * K], BF16, c=c)
            junkc = sb("junkc", [P, H], BF16, c=c)
            Sv, Sx = RC0, RC
        with ExitStack() as c:
            wext = sb("wext", [P, DC, WX], c=c)
            xr = sb("xr", [P, XS, D], c=c)
            xn = sb("xn", [P, 2, D], c=c)
            xh_ = sb("xh", [P, 2, DC, P], F32R, c=c)
            xl_ = sb("xl", [P, 2, DC, P], F32R, c=c)
            wh = sb("wh", [P, DC, WX], F32R, c=c)
            wl = sb("wl", [P, DC, WX], F32R, c=c)
            x1s = sb("x1s", [P, 2, R], c=c)
            recA = sb("recA", [P, XS, 24], c=c)
            recB = sb("recB", [P, XS, 16], c=c)
            bns = sb("bns", [P, 2, 2, 6], c=c)
            sdv = sb("sdv", [P, 2], c=c)
            rsd = sb("rsd", [P, 2], c=c)
            nmr = sb("nmr", [P, 2], c=c)
            b1e = sb("b1e", [P, R], c=c)
            Rp = sb("Rp", [P, HC, NQ], c=c)
            wT = xn[:, 0, :].rearrange("p (s a b) -> p s a b", s=2, b=P)
            b1c = sb("b1c", [P, HC], c=c)
            ones = sb("ones", [P, P], c=c)
            junka = sb("junka", [P, 2, H], BF16, c=c)
            keyr = sb("keyr", [EP, NE], c=c)
            junks = sb("junks", [EP, NE], BF16, c=c)
            drow = sb("drow", [P, EPAD], I32, c=c)
            eq = sb("eq", [EP, EJ, EJ], c=c)
            ei = sb("ei", [EP, 2, EJ], I32, c=c)
            pairs = sb("pairs", [EP, EJ, 2], I32, c=c)
            dstf = sb("dstf", [EP, EJ], c=c)
            key = sb("key", [EP, EJ], c=c)
            pcol = sb("pcol", [EP, 1], c=c)
            sgn = sb("sgn", [EP, EJ], c=c)
            ceq = sb("ceq", [EP, EJ], c=c)
            clt = sb("clt", [EP, EJ], c=c)
            c0 = sb("c0", [EP, EJ], c=c)
            posf = sb("posf", [EP, EJ], c=c)
            posi = sb("posi", [EP, EJ], I32, c=c)
            padi = sb("padi", [1, 2 * (EPAD - NE + 2)], I32, c=c)
            zt = sb("zt", [P, 2 * NPAD // P], c=c)
            cur = sb("cur", [P, ET, 2], I32, c=c)
            nxt = sb("nxt", [P, ET, 2], I32, c=c)
            prv = sb("prv", [P, ET, 2], I32, c=c)
            w = [sb(f"w{i}", [P, ET], c=c) for i in range(12)]
            slot = sb("slot", [P, ET], c=c)
            slot1 = sb("slot1", [P, ET], c=c)
            ifst = sb("ifst", [P, ET], I32, c=c)
            ilst = sb("ilst", [P, ET], I32, c=c)
            TS = sb("TS", [P, ET, 2], c=c)
            TD = sb("TD", [P, ET, 2], c=c)
            curR = sb("curR", [ET, P, 2], I32, c=c)
            dR = sb("dR", [ET, P], I32, c=c)
            dRf = sb("dRf", [ET, P], c=c)
            brow = sb("brow", [P, 2, ET], I32, c=c)
            browf = sb("browf", [P, 2, ET], c=c)
            bcol = sb("bcol", [2 * ET, 3], I32, c=c)
            bcf = sb("bcf", [2 * ET, 3], c=c)
            own = sb("own", [2 * ET, ET], c=c)
            sm = sb("sm", [ET, 10], c=c)
            fbase = sb("fbase", [ET, 1], c=c)
            TL = sb("TL", [ET, 2], c=c)
            ifn = sb("ifn", [ET, 1], I32, c=c)
            mhalf = sb("mhalf", [P, ET], c=c)
            ovl = sb("ovl", [2 * ET, 1], c=c)
        with ExitStack() as c:
            ndA = sb("ndA", [P, NT, 24], c=c)
            ndB = sb("ndB", [P, NT, 16], c=c)
            q = [sb(f"q{i}", [P, NT], c=c) for i in range(6)]
            lg = sb("lg", [P, NT, EX], c=c)
            lt = sb("lt", [P, NT, EX], c=c)
            sct = sb("sct", [P, EX, NT], c=c)
            tk = sb("tk", [P, NPAD * EX // P], c=c)
            tv = sb("tv", [P, TOPK], c=c)
            ti = sb("ti", [P, TOPK], U32, c=c)
            tif = sb("tif", [P, TOPK], c=c)
            tgi = sb("tgi", [P, TOPK], I32, c=c)
            tbase = sb("tbase", [P, 1], c=c)
            cv = sb("cv", [EX, 16 * TOPK], c=c)
            gv = sb("gv", [EX, TOPK], c=c)
            gi = sb("gi", [EX, TOPK], U32, c=c)
            gif = sb("gif", [EX, TOPK], c=c)
            gbase = sb("gbase", [EX, 1], c=c)
            gpi = sb("gpi", [EX, TOPK], I32, c=c)
            gcol = sb("gcol", [P, 2], c=c)
            pcl = sb("pcl", [P, 2], I32, c=c)
            tok = sb("tok", [P, 2], I32, c=c)
            tokf = sb("tokf", [P, 2], c=c)
            tokw = sb("tokw", [P, 2], I32, c=c)
            tw = sb("tw", [P, 6], c=c)
            fx = sb("fx", [P, 2, D], c=c)
            fn = sb("fn", [P, 2, D], c=c)
            fT = sb("fT", [P, DC, 2 * P], c=c)
            w1e = sb("w1e", [P, EX, DC, FF], c=c)
            w2e = sb("w2e", [FF, EX, D], c=c)
            b1t = sb("b1t", [FF, EX], c=c)
            b2t = sb("b2t", [EX, D], c=c)
            h1 = sb("h1", [FF, EX, P], c=c)
            esel = sb("esel", [EX, 2, P], c=c)
            ct = sb("ct", [P, 2, D], c=c)
            dq = sb("dq", [P, 2, 2, P], c=c)
            dlo = sb("dlo", [P, 2, 2, P], c=c)
            fst = sb("fst", [P, 2, 2, 6], c=c)
            fmv = sb("fmv", [P, 2, 2], c=c)
            fsd = sb("fsd", [P, 2], c=c)
            frs = sb("frs", [P, 2], c=c)
            fnm = sb("fnm", [P, 2], c=c)
            diag = sb("diag", [P, 2, P], c=c)
            onesf = sb("onesf", [P, P], c=c)
            ebase = sb("ebase", [P, 2], c=c)

        def psum(name, shape):
            return ctx.enter_context(nc.psum_tensor(name, shape, F32))

        pT = psum("pT", [P, 2, 2, 512])
        pA = psum("pA", [P, 2, 512])
        pB = psum("pB", [P, 512])
        pC = psum("pC", [P, 512])
        pBC = [pB, pC]
        pN = pT[:, 0, 0, :]

        s_x = [sem(f"s_x_slot{i}") for i in range(XS)]
        s_st = [sem(f"s_st_slot{i}") for i in range(XS)]
        s_sg = [sem(f"s_sg_slot{i}") for i in range(2)]
        s_sr = [sem(f"s_sr_slot{i}") for i in range(XS)]
        s_w = sem("s_w")
        s_id = sem("s_id")
        s_bn = sem("s_bn")
        s_var = sem("s_var")
        s_std = sem("s_std")
        s_rc = sem("s_rc")
        s_rstd = sem("s_rstd")
        s_xn = sem("s_xn")
        s_T = sem("s_T")
        s_hd = sem("s_hd")
        s_evd = sem("s_evd")
        s_wh = sem("s_wh")
        s_eva = sem("s_eva")
        s_mm = sem("s_mm")
        s_x1 = sem("s_x1")
        s_rec = sem("s_rec")
        s_o = sem("s_o")
        s_sq = sem("s_sq")
        s_wt = sem("s_wt")
        s_wc = sem("s_wc")
        s_wq = sem("s_wq")
        s_we = sem("s_we")
        s_ei = sem("s_ei")
        s_sgn = sem("s_sgn")
        s_p = sem("s_p")
        s_pd = sem("s_pd")
        s_tab = sem("s_tab")
        s_zg = [sem(f"s_zg_slot{i}") for i in range(GQ)]
        s_vg = [sem(f"s_vg_slot{i}") for i in range(GQ)]
        s_r0 = sem("s_r0")
        s_pre = sem("s_pre")
        s_th = sem("s_th")
        s_m = sem("s_m")
        s_z3 = sem("s_z3")
        s_e32 = sem("s_e32")
        s_wm = sem("s_wm")
        s_va = sem("s_va")
        s_vw = [sem(f"s_vw_slot{i}") for i in range(GQ)]
        s_rl = sem("s_rl")
        s_rs = sem("s_rs")
        s_co = sem("s_co")
        s_cc = sem("s_cc")
        s_ca = sem("s_ca")
        s_tb = sem("s_tb")
        s_tc = sem("s_tc")
        s_na = sem("s_na")
        s_xg = [sem(f"s_xg_slot{i}") for i in range(GQ)]
        s_fo = sem("s_fo")
        s_fq = sem("s_fq")
        s_fs = sem("s_fs")
        s_sp = sem("s_sp")
        s_sd = sem("s_sd")
        s_sa = sem("s_sa")
        s_ss = sem("s_ss")
        s_fw = sem("s_fw")
        s_nd = sem("s_nd")
        s_d = sem("s_d")
        s_g = sem("s_g")
        s_t = sem("s_t")
        s_q = [sem(f"s_q_slot{i}") for i in range(10)]

        s_key = sem("s_key")
        s_wl = sem("s_wl")
        s_eq = sem("s_eq")
        s_c0 = sem("s_c0")
        s_eps = sem("s_eps")
        s_one = sem("s_one")
        s_pk = sem("s_pk")
        s_E = sem("s_E")
        s_nrm = sem("s_nrm")
        s_dr = sem("s_dr")
        s_sz = sem("s_sz")
        s_a1 = sem("s_a1")
        s_a2 = sem("s_a2")
        s_a3 = sem("s_a3")
        s_v2 = sem("s_v2")
        s_lg = sem("s_lg")
        s_sc = sem("s_sc")
        s_msk = sem("s_msk")
        s_l1 = sem("s_l1")
        s_l2 = sem("s_l2")
        s_tk = sem("s_tk")
        s_dg = sem("s_dg")
        s_dq = sem("s_dq")
        s_fv = sem("s_fv")
        s_fs2 = sem("s_fs2")
        s_fn = sem("s_fn")
        s_fT = sem("s_fT")
        s_h0 = sem("s_h0")
        s_h1 = sem("s_h1")
        s_ct = sem("s_ct")
        s_fz = sem("s_fz")
        s_lo = sem("s_lo")
        s_tw = sem("s_tw")
        s_fx = [sem(f"s_fx_slot{i}") for i in range(2)]
        NWL = 4 + 2 * K + 4

        block = ctx.enter_context(nc.Block())


        dyn = lambda ap, t: ap[:, bass.ds(t, 1)]
        row = lambda ap, t: ap[:, bass.ds(t, 1), :].rearrange("p a b -> p (a b)")

        def node_loop(eng, step):
            turns, end = ET // XS, (NT - 3) // XS
            for t in range(-2, XS):
                step(0, t, True)
            with eng.Fori(1, turns, 1) as j:
                for u in range(XS):
                    step(j, u, True)
            for u in range(XS):
                step(turns, u, turns * XS + u < ET)
            with eng.Fori(turns + 1, end, 1) as j:
                for u in range(XS):
                    step(j, u, False)
            for u in range(NT - end * XS):
                step(end, u, False)

        def has(i, u, ahead):
            return 0 <= i + u + ahead < NT if isinstance(i, int) else True

        def early(i, u, before):
            return isinstance(i, int) and i + u - before < 0

        def group_tiles(lo, eng, step):
            if lo is None:
                for u in range(GT):
                    step(0, u, u % 2)
                return
            with eng.Fori(lo, lo + GT - 2, 2) as i:
                for u in range(2):
                    step(i, u, (lo + u) % 2)
            step(lo + GT - 1, 0, (lo + GT - 1) % 2)

        @block.sync
        def _(sp):
            def load(i, u):
                t = i + u
                if isinstance(t, int) and t == NT - 1:
                    sp.dma_start(xr[0:LAST, u % XS, :], x[t * P:N, :]).then_inc(s_x[u % XS], 16)
                else:
                    sp.dma_start(xr[:, u % XS, :], x[bass.ds(t * P, P), :]).then_inc(s_x[u % XS], 16)

            with nc.allow_non_contiguous_dma(reason="small weights"):
                sp.dma_start(wext[:, :, 0:H], W1.rearrange("(c p) h -> p c h", p=P)).then_inc(s_w, 16)
                sp.dma_start(wext[:, :, H + NQ:WX], rw.rearrange("(c p) e -> p c e", p=P)).then_inc(s_w, 16)
                for k in range(K):
                    for s in range(2):
                        sp.dma_start(Rp[:, :, s * K + k], Wg[k, s * H:(s + 1) * H, 0].rearrange("(c p) -> p c", p=P)).then_inc(s_w, 16)
                sp.dma_start(Rp[:, :, 2 * K:NP], rw[H:D, :].rearrange("(c p) e -> p c e", p=P)).then_inc(s_w, 16)
                sp.dma_start(Rp[:, :, NP:NQ], rw[0:H, :].rearrange("(c p) e -> p c e", p=P)).then_inc(s_w, 16)
                sp.dma_start(b1c[:, :], b1.rearrange("(c p) -> p c", p=P)).then_inc(s_w, 16)
                sp.dma_start(b1e[:, 0:H], b1.rearrange("(a h) -> a h", a=1).to_broadcast([P, H])).then_inc(s_w, 16)
                sp.dma_start(bgb[:, :], bg.rearrange("k a -> a k").to_broadcast([P, K])).then_inc(s_w, 16)
                sp.dma_start(rbb[:, :], rb.rearrange("(a h) -> a h", a=1).to_broadcast([P, EX])).then_inc(s_w, 16)
                for t in range(AHEAD):
                    load(0, t)
                sp.dma_start(ei[:, 0, :], dst.rearrange("(p j) -> p j", j=EJ)).then_inc(s_ei, 16)
                sp.dma_start(ei[:, 1, :], src.rearrange("(p j) -> p j", j=EJ)).then_inc(s_ei, 16)
                sp.dma_start(drow[0:EP, 0:NE], dst.rearrange("(a e) -> a e", a=1).to_broadcast([EP, NE])).then_inc(s_ei, 16)

            def step(j, u, ranked):
                if u < 0:
                    return
                i = j * XS
                t = i + u
                last = isinstance(t, int) and t == NT - 1
                if has(i, u, AHEAD):
                    if not early(i, u, XS - AHEAD):
                        sp.wait_ge(s_st[(u + AHEAD) % XS], j * 16 + (16 if u + AHEAD >= XS else 0))
                    load(i, u + AHEAD)
                sp.wait_ge(s_o, t + 1)
                sp.wait_ge(s_sq, t * 2 + 2)
                if last:
                    sp.dma_start(out[t * P:N, :], xr[0:LAST, u % XS, :]).then_inc(s_st[u % XS], 16)
                else:
                    sp.dma_start(out[bass.ds(t * P, P), :], xr[:, u % XS, :]).then_inc(s_st[u % XS], 16)
                sp.dma_start(G[bass.ds(t * P, P), :], x1s[:, u % 2, :]).then_inc(s_sg[u % 2], 16)
                sp.dma_start(NDA[bass.ds(t * P, P), :], recA[:, u % XS, :]).then_inc(s_sr[u % XS], 16)
                sp.dma_start(NDB[bass.ds(t * P, P), :], recB[:, u % XS, :]).then_inc(s_sr[u % XS], 16)

            node_loop(sp, step)

            for k in range(K):
                vd = Vd[k % 2]
                for g in range(GQ):
                    a, b = g * GT, (g + 1) * GT
                    sp.wait_ge(s_va, ET * k + b)
                    sp.dma_start(vd[a * P:b * P, :].rearrange("(t p) c -> p t c", p=P), V[:, a:b, :]).then_inc(s_vw[g], 16)
                for g in range(GQ):
                    sp.wait_ge(s_vw[g], 16 * (k + 1))
                if k:
                    sp.wait_ge(s_co, k)
                sp.dma_start(RC[:, :], vd.rearrange("(t p) c -> p t c", p=P)[P - 1]).then_inc(s_rl, 16)

            sp.wait_ge(s_fs, 16 * 2 * ET)
            sp.wait_ge(s_ss, 32)
            sp.dma_start(ndA[:, :, :].rearrange("p j c -> p (j c)"), NDA.rearrange("(p j) c -> p (j c)", p=P)).then_inc(s_nd, 16)
            sp.dma_start(ndB[:, :, :].rearrange("p j c -> p (j c)"), NDB.rearrange("(p j) c -> p (j c)", p=P)).then_inc(s_nd, 16)
            for e in range(EX):
                sp.dma_start(w1e[:, e, :, :], fw1[e].rearrange("(c p) f -> p c f", p=P)).then_inc(s_fw, 16)
            sp.dma_start(w2e[:, :, :], fw2.rearrange("e f h -> f e h")).then_inc(s_fw, 16)
            with nc.allow_non_contiguous_dma(reason="bias columns"):
                sp.dma_start(b1t[:, :], fb1.rearrange("e f -> f e")).then_inc(s_fw, 16)
            sp.dma_start(b2t[:, :], fb2).then_inc(s_fw, 16)
            sp.wait_ge(s_msk, 1)
            sp.dma_start(SC.rearrange("e (p j) -> p e j", p=P), sct[:, :, :]).then_inc(s_q[0], 16)
            sp.wait_ge(s_q[0], 16)
            sp.dma_start(tk[:, :], SC.rearrange("e (g n) -> (e g) n", g=16)).then_inc(s_q[1], 16)
            sp.wait_ge(s_l1, 1)
            sp.dma_start(CV.rearrange("(p r) -> p r", p=P), tv[:, :]).then_inc(s_q[2], 16)
            sp.dma_start(CI.rearrange("(p r) a -> p (r a)", p=P), tgi[:, :]).then_inc(s_q[3], 16)
            sp.wait_ge(s_q[2], 16)
            sp.dma_start(cv[:, :], CV.rearrange("(e n) -> e n", e=EX)).then_inc(s_q[4], 16)
            sp.wait_ge(s_l2, 1)
            sp.dma_start(PQ[0:EX * TOPK].rearrange("(e r) -> e r", e=EX), gpi[:, :]).then_inc(s_q[5], 16)
            sp.dma_start(PQ[EX * TOPK:2 * EX * TOPK].rearrange("(e r) -> e r", e=EX), gv[:, :].bitcast(I32)).then_inc(s_q[5], 16)
            sp.wait_ge(s_q[5], 32)
            with nc.allow_non_contiguous_dma(reason="columns of chosen pairs"):
                sp.dma_start(pcl[:, :], PQ[0:EX * TOPK].rearrange("(h p) -> p h", p=P)).then_inc(s_q[6], 16)
                sp.dma_start(gcol[:, :].bitcast(I32), PQ[EX * TOPK:2 * EX * TOPK].rearrange("(h p) -> p h", p=P)).then_inc(s_q[7], 16)
            sp.wait_ge(s_q[9], 32)

        @block.tensor
        def _(pe):
            mmul = nc.tensor.matmul
            pe.wait_ge(s_w, 16 * NWL)
            pe.wait_ge(s_id, 1)
            def wturn(c):
                if c >= 2:
                    pe.wait_ge(s_wc, c - 1)
                for q4 in range(HC):
                    mm = nc.tensor.transpose(pT[:, c % 2, 0, q4 * P:(q4 + 1) * P], wext[:, c, q4 * P:(q4 + 1) * P], ident[:, :])
                mm.then_inc(s_wt, 1)

            wturn(0)
            for c in range(DC):
                if c + 1 < DC:
                    wturn(c + 1)
                pe.wait_ge(s_wc, c + 1)
                if c >= 1:
                    pe.wait_ge(s_we, c)
                for q4 in range(HC):
                    mm = mmul(pB[:, 0:NQ], lhsT=wT[:, c % 2, q4, :], rhs=Rp[:, q4, :], start=(q4 == 0), stop=(q4 == HC - 1))
                mm.then_inc(s_wq, 1)
            def bias_products():
                pe.wait_ge(s_one, 1)
                for q4 in range(HC):
                    mm = mmul(pC[:, 0:NQ], lhsT=b1c[:, q4:q4 + 1].to_broadcast([P, P]), rhs=Rp[:, q4, :], start=(q4 == 0), stop=(q4 == HC - 1))
                for c in range(DC):
                    mm = mmul(pC[:, NQ:NQ + EX], lhsT=ones[:, :], rhs=wext[:, c, H + NQ:WX], start=(c == 0), stop=(c == DC - 1))
                mm.then_inc(s_wq, 1)

            pe.wait_ge(s_we, DC)
            def step(j, u, ranked):
                i = j * XS
                t = i + u
                if has(i, u, 1) and u >= -1:
                    pe.wait_ge(s_xn, t + 2)
                    if not early(i, u, 1):
                        pe.wait_ge(s_evd, t)
                        pe.wait_ge(s_eva, t)
                    n = (u + 1) % 2
                    for c in range(DC):
                        mm = nc.tensor.transpose(pT[:, n, c // 4, (c % 4) * P:(c % 4 + 1) * P], xn[:, n, c * P:(c + 1) * P], ident[:, :])
                    mm.then_inc(s_T, 1)
                if u >= 0:
                    if isinstance(t, int) and t == 0:
                        bias_products()
                        pe.wait_ge(s_wl, DC)
                    if isinstance(t, int) and t == 1:
                        pe.wait_ge(s_we, DC + 1)
                    pe.wait_ge(s_evd, t + 1)
                    pe.wait_ge(s_eva, t + 1)
                    if not early(i, u, 2):
                        pe.wait_ge(s_x1, t - 1)
                    n = u % 2
                    for c in range(DC):
                        first, last = c == 0, c == DC - 1
                        h, l = xh_[:, n, c, :], xl_[:, n, c, :]
                        for bank, o in ((pA[:, n, 0:WHALF], slice(0, WHALF)), (pBC[n][:, 0:WHALF], slice(WHALF, WX))):
                            mmul(bank, lhsT=h, rhs=wh[:, c, o], start=first, stop=False)
                            mmul(bank, lhsT=h, rhs=wl[:, c, o], start=False, stop=False)
                        for bank, o in ((pA[:, n, 0:WHALF], slice(0, WHALF)), (pBC[n][:, 0:WHALF], slice(WHALF, WX))):
                            mm = mmul(bank, lhsT=l, rhs=wh[:, c, o], start=False, stop=last)
                    mm.then_inc(s_mm, 1)

            node_loop(pe, step)

            for k in range(K):
                for g in range(GQ):
                    def wide(i, u, n):
                        t = i + u
                        pe.wait_ge(s_e32, t + (ET * k + 1))
                        if k or g or u >= 2:
                            pe.wait_ge(s_va, t + (ET * k - 1))
                        mmul(pA[:, n, :], lhsT=E32[:, n, :], rhs=row(Z[:, :, 0:H], t), start=True, stop=True)
                        mmul(pBC[n][:, 0:NP], lhsT=E32[:, n, :], rhs=row(Z[:, :, H:R], t), start=True, stop=True).then_inc(s_wm, 1)
                    group_tiles(g * GT if k or g else None, pe, wide)
                if k < K - 1:
                    for g in range(GQ):
                        pe.wait_ge(s_z3, GQ * k + g + 1)
                    pe.wait_ge(s_va, ET * (k + 1))
                    pe.wait_ge(s_E, 2)
                    def bsum(t, start, stop):
                        return mmul(pC[0:2 * ET, 0:3 * K], lhsT=TBl[:, t, :], rhs=z3[:, t, :], start=start, stop=stop)
                    for t in range(ET):
                        mm = bsum(t, t == 0, t == ET - 1)
                    mm.then_inc(s_tb, 1)
                    pe.wait_ge(s_tc, 4 * (k + 1))
                    def nsum(t):
                        o = pN[:, t * 3 * K:(t + 1) * 3 * K]
                        mmul(o, lhsT=E[:, t, :], rhs=z3[:, t, :], start=True, stop=False)
                        return mmul(o, lhsT=Fsel[:, t, :], rhs=tb3[:, :], start=False, stop=True)
                    for t in range(ET):
                        mm = nsum(t)
                    mm.then_inc(s_na, 1)
                pe.wait_ge(s_rs, k + 1)
                mmul(pT[0:ET, 1, 0, :], lhsT=Lm[:, :], rhs=RC[:, 0:H], start=True, stop=True)
                mmul(pT[0:ET, 1, 1, 0:NP], lhsT=Lm[:, :], rhs=RC[:, H:R], start=True, stop=True).then_inc(s_co, 1)

            pe.wait_ge(s_dg, 1)
            for h in range(2):
                mm = mmul(pC[:, h * P:(h + 1) * P], lhsT=onesf[:, :], rhs=diag[:, h, :], start=True, stop=True)
            mm.then_inc(s_t, 1)
            for h in range(2):
                pe.wait_ge(s_fn, h + 1)
                for c in range(DC):
                    mm = nc.tensor.transpose(pT[:, h, c // 4, (c % 4) * P:(c % 4 + 1) * P], fn[:, h, c * P:(c + 1) * P], ident[:, :])
                mm.then_inc(s_t, 1)
            pe.wait_ge(s_fw, 16 * (EX + 3))
            pe.wait_ge(s_fT, 2)
            for e in range(EX):
                for c in range(DC):
                    mm = mmul(pA[0:FF, 0, e * TOPK:(e + 1) * TOPK], lhsT=w1e[:, e, c, :], rhs=fT[:, c, e * TOPK:(e + 1) * TOPK],
                              start=(c == 0), stop=(c == DC - 1))
            mm.then_inc(s_t, 1)
            pe.wait_ge(s_h1, 1)
            pe.wait_ge(s_g, 1)
            for h in range(2):
                for n in range(2):
                    o = pT[:, h, n, :]
                    for e in range(4 * h, 4 * h + 4):
                        mmul(o, lhsT=h1[:, e, :], rhs=w2e[:, e, n * 512:(n + 1) * 512], start=(e == 4 * h), stop=False)
                    mm = mmul(o, lhsT=esel[:, h, :], rhs=b2t[:, n * 512:(n + 1) * 512], start=False, stop=True)
                mm.then_inc(s_t, 1)
            pe.wait_ge(s_ct, 1)
            for h in range(2):
                for n in range(2):
                    for f in range(2):
                        mm = mmul(pT[:, h, n, :], lhsT=dq[:, f, h, :], rhs=ct[:, f, n * 512:(n + 1) * 512], start=(f == 0), stop=(f == 1))
            mm.then_inc(s_t, 1)

        @block.scalar
        def _(act):
            A = nc.scalar.activation
            act.wait_ge(s_eps, 1)
            def ranks(t):
                A(junks[:, :], keyr[:, :], ACT.Sign, bias=dyn(key, t), scale=-1.0, accum_out=dyn(sgn, t)).then_inc(s_sgn, 1)

            for c in range(DC):
                act.wait_ge(s_we, c + 1)
                A(wh[:, c, :], wext[:, c, :], ACT.Copy).then_inc(s_wh, 1)

            def deviation(t, u):
                act.wait_ge(s_var, t + 1)
                A(sdv[:, u % 2:u % 2 + 1], recA[:, u % XS, 1:2], ACT.Sqrt, bias=eps[:, :]).then_inc(s_std, 1)

            deviation(0, 0)

            def step(j, u, ranked):
                i = j * XS
                t = i + u
                if has(i, u, 1) and (u == -1 or not ranked):
                    act.wait_ge(s_T, t + 2)
                    if not early(i, u, 1):
                        act.wait_ge(s_mm, t)
                    A(xh_[:, (u + 1) % 2, 4:8, :].rearrange("p a b -> p (a b)"), pT[:, (u + 1) % 2, 1, :], ACT.Copy).then_inc(s_eva, 1)
                if has(i, u, 2):
                    n = (u + 2) % 2
                    act.wait_ge(s_rstd, t + 3)
                    if not early(i, u, 0):
                        act.wait_ge(s_T, t + 1)
                    A(xn[:, n, :], xr[:, (u + 2) % XS, :], ACT.Identity, bias=nmr[:, n:n + 1], scale=rsd[:, n:n + 1]).then_inc(s_xn, 1)
                if u >= 0 and ranked:
                    if isinstance(t, int) and t == 0:
                        act.wait_ge(s_key, 1)
                    else:
                        act.wait_ge(s_sgn, t)
                    ranks(t)
                if has(i, u, 3):
                    deviation(t + 3, u + 3)
                if u >= 0:
                    act.wait_ge(s_o, t + 1)
                    if not early(i, u, 1):
                        act.wait_ge(s_sq, t * 2)
                    A(junka[:, 0, :], xr[:, u % XS, 0:H], ACT.Square, accum_out=recA[:, u % XS, 3:4]).then_inc(s_sq, 1)
                    A(junka[:, 1, :], xr[:, u % XS, H:D], ACT.Square, accum_out=recB[:, u % XS, 9:10]).then_inc(s_sq, 1)

            node_loop(act, step)

            for k in range(K):
                for g in range(GQ):
                    a, b = g * GT, (g + 1) * GT
                    act.wait_ge(s_pre, GQ * k + g + 1)
                    A(al[:, a:b], pre[:, a:b], ACT.Tanh, bias=bgb[:, k:k + 1]).then_inc(s_th, 1)
                    act.wait_ge(s_m, GQ * k + g + 1)
                    if k == 0 and g == 0:
                        act.wait_ge(s_E, 1)

                    def scale(i, u, n):
                        t = i + u
                        if k or g or u >= 2:
                            act.wait_ge(s_wm, t + (ET * k - 1))
                        A(E32[:, n, :], row(E, t), ACT.Copy, scale=dyn(m, t)).then_inc(s_e32, 1)
                    group_tiles(a if k or g else None, act, scale)

            def squares(t):
                act.wait_ge(s_fo, t + 1)
                if not isinstance(t, int):
                    act.wait_ge(s_fq, t)
                A(junkc[:, :], row(Z[:, :, 0:H], t), ACT.Square, accum_out=row(Z[:, :, H + 9:H + 10], t)).then_inc(s_fq, 1)
            squares(0)
            with act.Fori(1, ET, 1) as t:
                squares(t)
            act.wait_ge(s_fq, ET)
            act.wait_ge(s_sd, 1)
            A(junkc[0:ET, :], Sx[:, 0:H], ACT.Square, accum_out=Sx[:, H + 9:H + 10]).then_inc(s_sa, 1)

            act.wait_ge(s_nd, 32)
            A(q[0][:, :], ndA[:, :, 1], ACT.Sqrt, bias=eps[:, :]).then_inc(s_a1, 1)
            act.wait_ge(s_v2, 1)
            A(q[4][:, :], q[3][:, :], ACT.Sqrt, bias=eps[:, :]).then_inc(s_a1, 1)
            act.wait_ge(s_lg, 1)
            A(lt[:, :, :], lg[:, :, :], ACT.Exp).then_inc(s_a2, 1)
            for h in range(2):
                act.wait_ge(s_fv, h + 1)
                A(fsd[:, h:h + 1], fmv[:, h, 1:2], ACT.Sqrt, bias=eps[:, :]).then_inc(s_a3, 1)
            for h in range(2):
                act.wait_ge(s_fs2, h + 1)
                A(fn[:, h, :], fx[:, h, :], ACT.Identity, bias=fnm[:, h:h + 1], scale=frs[:, h:h + 1]).then_inc(s_fn, 1)
            act.wait_ge(s_t, 4)
            act.wait_ge(s_h0, 1)
            act.wait_ge(s_fw, 16 * (EX + 3))
            for e in range(EX):
                c = (e % 4) * TOPK
                ins = A(h1[:, e, c:c + TOPK], pA[0:FF, 0, e * TOPK:(e + 1) * TOPK], ACT.Relu, bias=b1t[:, e:e + 1])
            ins.then_inc(s_h1, 1)

        @block.vector
        def _(dve):
            v = nc.vector
            chain = [0]

            def link(ins):
                chain[0] += 1
                ins.then_inc(s_d, 1)
                dve.wait_ge(s_d, chain[0])

            v.memset(eps[:, :], EPS).then_inc(s_eps, 1)
            v.memset(ones[:, :], 1.0).then_inc(s_one, 1)
            v.memset(recA[:, :, :], 0.0)
            link(v.memset(recB[:, :, :], 0.0))

            def keys():
                dve.wait_ge(s_ei, 48)
                dve.wait_ge(s_pk, 1)
                v.tensor_copy(pairs[:, :, 0], ei[:, 0, :])
                v.tensor_copy(pairs[:, :, 1], ei[:, 1, :])
                link(v.tensor_copy(dstf[:, :], ei[:, 0, :]))
                v.tensor_scalar(key[:, :], dstf[:, :], float(P), pcol[:, :], ALU.mult, ALU.add)
                v.scalar_tensor_tensor(keyr[:, :], drow[0:EP, 0:NE], float(P), keyr[:, :], ALU.mult, ALU.add).then_inc(s_key, 1)
                v.tensor_tensor(eq[:, :, :], dstf[:, :].unsqueeze(2).to_broadcast([EP, EJ, EJ]),
                                dstf[:, :].unsqueeze(1).to_broadcast([EP, EJ, EJ]), ALU.is_equal).then_inc(s_eq, 1)
                dve.wait_ge(s_eq, 1)
                v.tensor_reduce(ceq[:, :], eq[:, :, :], AX.X, ALU.add).then_inc(s_eq, 1)
                dve.wait_ge(s_eq, 3)
                link(v.tensor_reduce(clt[:, :], eq[:, :, :], AX.X, ALU.add))
                link(v.tensor_scalar(c0[:, :], ceq[:, :], -0.5, NE / 2.0 + 1.0, ALU.mult, ALU.add))
                v.tensor_tensor(c0[:, :], c0[:, :], clt[:, :], ALU.add).then_inc(s_c0, 1)

            def lower(c):
                dve.wait_ge(s_wh, c + 1)
                v.tensor_tensor(wl[:, c, :], wext[:, c, :], wh[:, c, :].bitcast(F32), ALU.subtract).then_inc(s_wl, 1)

            dve.wait_ge(s_w, 16 * NWL)
            for c in range(DC):
                dve.wait_ge(s_wt, c + 1)
                if c >= 2:
                    dve.wait_ge(s_wq, c - 1)
                v.tensor_copy(wT[:, c % 2, :, :].rearrange("p a b -> p (a b)"), pT[:, c % 2, 0, :]).then_inc(s_wc, 1)
                dve.wait_ge(s_wq, c + 1)
                v.tensor_copy(wext[:, c, H:H + NQ], pB[:, 0:NQ]).then_inc(s_we, 1)
                if c:
                    lower(c - 1)
            lower(DC - 1)

            def bias_projections():
                dve.wait_ge(s_wq, DC + 1)
                v.tensor_copy(b1e[:, H:R], pC[:, 0:NP])
                v.tensor_copy(bRa[:, :], pC[:, NP:NQ])
                v.tensor_copy(csrw[:, :], pC[:, NQ:NQ + EX]).then_inc(s_we, 1)
                dve.wait_ge(s_we, DC + 1)

            def step(j, u, ranked):
                i = j * XS
                t = i + u
                if has(i, u, 2):
                    s, n = (u + 2) % XS, (u + 2) % 2
                    dve.wait_ge(s_x[s], slot16(j, u + 2))
                    v.bn_stats(bns[:, n, 0, :], xr[:, s, 0:H]).then_inc(s_bn, 1)
                    v.bn_stats(bns[:, n, 1, :], xr[:, s, H:D]).then_inc(s_bn, 1)
                    if not early(i, u, XS - 2):
                        dve.wait_ge(s_sr[s], slot32(j, u + 2 - XS))
                    dve.wait_ge(s_bn, t * 2 + 6)
                    v.memset(recA[:, s, 4:5], 0.0)
                    v.bn_aggr(recA[:, s, 0:2], bns[:, n, :, :].rearrange("p a b -> p (a b)")).then_inc(s_var, 1)
                if has(i, u, 1) and u >= -1:
                    dve.wait_ge(s_T, t + 2)
                    if not early(i, u, 1):
                        dve.wait_ge(s_mm, t)
                    nt = (u + 1) % 2
                    half = lambda ap, k: ap[:, nt, 4 * k:4 * k + 4, :].rearrange("p a b -> p (a b)")
                    v.tensor_copy(half(xh_, 0), pT[:, nt, 0, :]).then_inc(s_hd, 1)
                    if ranked and u >= 0:
                        v.tensor_copy(half(xh_, 1), pT[:, nt, 1, :]).then_inc(s_eva, 1)
                if has(i, u, 2):
                    dve.wait_ge(s_std, t + 3)
                    v.reciprocal(rsd[:, n:n + 1], sdv[:, n:n + 1]).then_inc(s_rc, 1)
                    dve.wait_ge(s_rc, t + 3)
                    v.tensor_scalar(nmr[:, n:n + 1], recA[:, s, 0:1], rsd[:, n:n + 1], -1.0, ALU.mult, ALU.mult).then_inc(s_rstd, 1)
                if has(i, u, 1) and u >= -1:
                    dve.wait_ge(s_hd, t + 2)
                    v.tensor_tensor(half(xl_, 0), pT[:, nt, 0, :], half(xh_, 0).bitcast(F32), ALU.subtract)
                    dve.wait_ge(s_eva, t + 2)
                    v.tensor_tensor(half(xl_, 1), pT[:, nt, 1, :], half(xh_, 1).bitcast(F32), ALU.subtract).then_inc(s_evd, 1)
                if isinstance(t, int) and t == 0:
                    bias_projections()
                    keys()
                if u >= 0:
                    s, n = u % XS, u % 2
                    dve.wait_ge(s_mm, t + 1)
                    if not early(i, u, 2):
                        dve.wait_ge(s_sg[n], slot16(j, u - 2, 2))
                    v.tensor_tensor(x1s[:, n, WHALF:R], pBC[n][:, 0:R - WHALF], b1e[:, WHALF:R], ALU.add).then_inc(s_rec, 1)
                    v.tensor_copy(recA[:, s, 8:24], pBC[n][:, R - WHALF:WHALF])
                    v.tensor_tensor(x1s[:, n, 0:WHALF], pA[:, n, 0:WHALF], b1e[:, 0:WHALF], ALU.add).then_inc(s_x1, 1)
                    dve.wait_ge(s_rec, t + 1)
                    v.tensor_copy(recB[:, s, 0:8], x1s[:, n, H + 8:R])
                    dve.wait_ge(s_x1, t + 1)
                    dve.wait_ge(s_xn, t + 1)
                    v.scalar_tensor_tensor(xr[:, s, 0:H], xr[:, s, 0:H], 1.0, x1s[:, n, 0:H], ALU.mult, ALU.add, accum_out=recA[:, s, 2:3])
                    v.scalar_tensor_tensor(xr[:, s, H:D], xr[:, s, H:D], 1.0, x1s[:, n, 0:H], ALU.mult, ALU.add, accum_out=recB[:, s, 8:9]).then_inc(s_o, 1)

            def slot16(j, u, ring=XS):
                return j * (16 * XS // ring) + 16 * (u // ring + 1)

            def slot32(j, u, ring=XS):
                return j * (32 * XS // ring) + 32 * (u // ring + 1)

            node_loop(dve, step)

            dve.wait_ge(s_tab, 1)
            dve.wait_ge(s_dr, 16)
            v.tensor_tensor(E[:, :, :], drow[:, :].rearrange("p (t e) -> p t e", e=P),
                            curf[:, :].unsqueeze(2).to_broadcast([P, ET, P]), ALU.is_equal).then_inc(s_E, 1)
            link(v.tensor_tensor(TBl[:, :, :], browf[:, :, :].rearrange("p a b -> p (a b)").unsqueeze(1).to_broadcast([P, ET, 2 * ET]),
                                 curf[:, :].unsqueeze(2).to_broadcast([P, ET, 2 * ET]), ALU.is_equal))
            for s in range(2):
                v.memset(TBl[:, :, :].rearrange("p t b -> p (t b)")[:, s * ET:s * ET + (ET - 1) * (2 * ET + 1) + 1:2 * ET + 1], 0.0)
            v.scalar_tensor_tensor(Fsel[:, :, :], drow[0:2 * ET, :].rearrange("p (t e) -> p t e", e=P), bcf[:, 0:1],
                                   own[:, :].unsqueeze(2).to_broadcast([2 * ET, ET, P]), ALU.is_equal, ALU.mult).then_inc(s_E, 1)

            for k in range(K):
                for g in range(GQ):
                    a, b = g * GT, (g + 1) * GT
                    dve.wait_ge(s_zg[g], 16 * GT * (k + 1))
                    if k == 0:
                        dve.wait_ge(s_vg[g], 16 * GT)
                        link(v.tensor_copy(Vpi[:, a:b, :], V[:, a:b, H:H + K]))
                    v.tensor_tensor(pre[:, a:b], Z[:, a:b, H + K + k], Vpi[:, a:b, k], ALU.add).then_inc(s_pre, 1)
                    dve.wait_ge(s_th, GQ * k + g + 1)
                    if k == 0 and g == 0:
                        dve.wait_ge(s_nrm, 1)
                    v.tensor_tensor(m[:, a:b], al[:, a:b], norm[:, a:b], ALU.mult).then_inc(s_m, 1)
                    if k < K - 1:
                        dve.wait_ge(s_m, GQ * k + g + 1)
                        mb = m[:, a:b].unsqueeze(2).to_broadcast([P, GT, K])
                        link(v.tensor_tensor(zf[:, :, :], Z[:, a:b, H:H + K], mb, ALU.mult))
                        link(v.tensor_copy(z3[:, a:b, 0:K], zf[:, :, :]))
                        link(v.tensor_tensor(zf[:, :, :], zf[:, :, :], z3[:, a:b, 0:K], ALU.subtract))
                        link(v.tensor_copy(z3[:, a:b, K:2 * K], zf[:, :, :]))
                        link(v.tensor_tensor(zf[:, :, :], zf[:, :, :], z3[:, a:b, K:2 * K], ALU.subtract))
                        v.tensor_copy(z3[:, a:b, 2 * K:3 * K], zf[:, :, :]).then_inc(s_z3, 1)

                    def add(i, u, n):
                        t = i + u
                        dve.wait_ge(s_wm, t + (ET * k + 1))
                        vt = row(V[:, :, 0:H], t)
                        vp = row(V[:, :, H:R], t)
                        v.tensor_tensor(vt, vt, pA[:, n, :], ALU.add)
                        v.tensor_tensor(vp, vp, pBC[n][:, 0:NP], ALU.add).then_inc(s_va, 1)
                    group_tiles(a if k or g else None, dve, add)
                if k < K - 1:
                    dve.wait_ge(s_tb, k + 1)
                    tc = 4 * k
                    v.tensor_copy(tbf[:, :], pC[0:2 * ET, 0:3 * K]).then_inc(s_tc, 1)
                    dve.wait_ge(s_tc, tc + 1)
                    link(v.tensor_tensor(tbf[:, 0:K], tbf[:, 0:K], tbf[:, K:2 * K], ALU.add))
                    link(v.tensor_tensor(tbf[:, 0:K], tbf[:, 0:K], tbf[:, 2 * K:3 * K], ALU.add))
                    v.tensor_copy(tb3[:, 0:K], tbf[:, 0:K]).then_inc(s_tc, 1)
                    dve.wait_ge(s_tc, tc + 2)
                    link(v.tensor_tensor(tbf[:, 0:K], tbf[:, 0:K], tb3[:, 0:K], ALU.subtract))
                    v.tensor_copy(tb3[:, K:2 * K], tbf[:, 0:K]).then_inc(s_tc, 1)
                    dve.wait_ge(s_tc, tc + 3)
                    link(v.tensor_tensor(tbf[:, 0:K], tbf[:, 0:K], tb3[:, K:2 * K], ALU.subtract))
                    v.tensor_copy(tb3[:, 2 * K:3 * K], tbf[:, 0:K]).then_inc(s_tc, 1)
                    dve.wait_ge(s_na, k + 1)
                    nar = pN[:, 0:3 * K * ET].rearrange("p (t c) -> p t c", c=3 * K)
                    for s in range(3):
                        link(v.tensor_tensor(Vpi[:, :, :], Vpi[:, :, :], nar[:, :, s * K:(s + 1) * K], ALU.add))
                if k == 0:
                    dve.wait_ge(s_r0, 16)
                dve.wait_ge(s_rl, 16 * (k + 1))
                v.tensor_tensor(RC[:, :], RC[:, :], RC0[:, :], ALU.subtract).then_inc(s_rs, 1)
                dve.wait_ge(s_co, k + 1)
                if k:
                    dve.wait_ge(s_ca, 16 * k)
                v.tensor_copy(corr[:, 0:H], pT[0:ET, 1, 0, :])
                v.tensor_copy(corr[:, H:R], pT[0:ET, 1, 1, 0:NP]).then_inc(s_cc, 1)

            def final(t):
                zr = row(Z[:, :, 0:H], t)
                v.scalar_tensor_tensor(zr, zr, 1.0, row(V[:, :, 0:H], t), ALU.mult, ALU.add, accum_out=row(Z[:, :, H + 8:H + 9], t))
                v.tensor_copy(row(Z[:, :, H:H + 8], t), row(V[:, :, H + 8:R], t)).then_inc(s_fo, 1)
            for g in range(GQ):
                dve.wait_ge(s_xg[g], 16 * GT)
                with dve.Fori(g * GT, (g + 1) * GT, 1) as t:
                    final(t)
            link(v.memset(Sx[:, :], 0.0))
            v.memset(Sv[:, :], 0.0).then_inc(s_sz, 1)
            dve.wait_ge(s_sp, 32)
            v.tensor_copy(Sx[:, H:H + 8], Sv[:, H + 8:R])
            v.scalar_tensor_tensor(Sx[:, 0:H], Sx[:, 0:H], 1.0, Sv[:, 0:H], ALU.mult, ALU.add, accum_out=Sx[:, H + 8:H + 9]).then_inc(s_sd, 1)

            dve.wait_ge(s_nd, 32)
            link(v.tensor_tensor(q[1][:, :], ndA[:, :, 2], ndB[:, :, 8], ALU.add))
            link(v.tensor_scalar(q[1][:, :], q[1][:, :], 1.0 / D, None, ALU.mult))
            link(v.tensor_tensor(q[2][:, :], ndA[:, :, 3], ndB[:, :, 9], ALU.add))
            link(v.tensor_tensor(q[5][:, :], q[1][:, :], q[1][:, :], ALU.mult))
            v.scalar_tensor_tensor(q[3][:, :], q[2][:, :], 1.0 / D, q[5][:, :], ALU.mult, ALU.subtract).then_inc(s_v2, 1)
            dve.wait_ge(s_v2, 1)
            link(v.tensor_tensor(q[2][:, :], ndA[:, :, 0], q[1][:, :], ALU.subtract))
            dve.wait_ge(s_a1, 1)
            b8 = lambda ap: ap[:, :].unsqueeze(2).to_broadcast([P, NT, EX])
            c8 = lambda ap: ap[:, :].unsqueeze(1).to_broadcast([P, NT, EX])
            link(v.tensor_tensor(lt[:, :, :], ndA[:, :, 16:24], b8(q[0]), ALU.mult))
            link(v.tensor_tensor(lg[:, :, :], ndA[:, :, 8:16], lt[:, :, :], ALU.add))
            link(v.tensor_tensor(lg[:, :, :], lg[:, :, :], ndB[:, :, 0:8], ALU.add))
            link(v.tensor_tensor(lg[:, :, :], lg[:, :, :], c8(bRa), ALU.add))
            link(v.tensor_tensor(lt[:, :, :], b8(q[2]), c8(csrw), ALU.mult))
            link(v.tensor_tensor(lg[:, :, :], lg[:, :, :], lt[:, :, :], ALU.add))
            dve.wait_ge(s_a1, 2)
            link(v.reciprocal(q[4][:, :], q[4][:, :]))
            link(v.tensor_tensor(lg[:, :, :], lg[:, :, :], b8(q[4]), ALU.mult))
            link(v.tensor_tensor(lg[:, :, :], lg[:, :, :], c8(rbb), ALU.add))
            link(v.tensor_reduce(q[1][:, :], lg[:, :, :], AX.X, ALU.max))
            v.tensor_tensor(lg[:, :, :], lg[:, :, :], b8(q[1]), ALU.subtract).then_inc(s_lg, 1)
            dve.wait_ge(s_a2, 1)
            link(v.tensor_reduce(q[2][:, :], lt[:, :, :], AX.X, ALU.add))
            link(v.reciprocal(q[3][:, :], q[2][:, :]))
            v.tensor_tensor(sct[:, :, :].rearrange("p e j -> p j e"), lt[:, :, :], b8(q[3]), ALU.mult).then_inc(s_sc, 1)

            def best(vals, idx, data):
                for r in range(TOPK // 8):
                    o = slice(8 * r, 8 * r + 8)
                    link(v.max(vals[:, o], data[:, :]))
                    link(v.max_index(idx[:, o], vals[:, o], data[:, :]))
                    if r < TOPK // 8 - 1:
                        link(v.match_replace(data[:, :], vals[:, o], data[:, :], -2.0))
            dve.wait_ge(s_q[1], 16)
            best(tv, ti, tk)
            link(v.tensor_copy(tif[:, :], ti[:, :]))
            dve.wait_ge(s_g, 1)
            v.tensor_scalar(tgi[:, :], tif[:, :], tbase[:, :], None, ALU.add).then_inc(s_l1, 1)
            link(v.memset(onesf[:, :], 1.0))
            v.memset(h1[:, :, :], 0.0).then_inc(s_h0, 1)
            dve.wait_ge(s_q[4], 16)
            best(gv, gi, cv)
            link(v.tensor_copy(gif[:, :], gi[:, :]))
            v.tensor_scalar(gpi[:, :], gif[:, :], gbase[:, :], None, ALU.add).then_inc(s_l2, 1)

            dve.wait_ge(s_q[8], 32)
            link(v.tensor_copy(tokf[:, :], tokw[:, :]))
            link(v.tensor_tensor(tokf[:, :], tokf[:, :], ebase[:, :], ALU.subtract))
            v.tensor_copy(tok[:, :], tokf[:, :]).then_inc(s_tk, 1)
            for h in range(2):
                ins = v.tensor_scalar(diag[:, h, :], ident[:, :], tokf[:, h:h + 1], None, ALU.mult)
            ins.then_inc(s_dg, 1)
            dve.wait_ge(s_t, 1)
            for f in range(2):
                for h in range(2):
                    ins = v.tensor_scalar(dq[:, f, h, :], pC[:, h * P:(h + 1) * P], tokf[:, f:f + 1], None, ALU.is_equal)
            ins.then_inc(s_dq, 1)
            for h in range(2):
                dve.wait_ge(s_fx[h], 16)
                v.bn_stats(fst[:, h, 0, :], fx[:, h, 0:H])
                link(v.bn_stats(fst[:, h, 1, :], fx[:, h, H:D]))
                v.bn_aggr(fmv[:, h, :], fst[:, h, :, :].rearrange("p a b -> p (a b)")).then_inc(s_fv, 1)
            for h in range(2):
                dve.wait_ge(s_a3, h + 1)
                link(v.reciprocal(frs[:, h:h + 1], fsd[:, h:h + 1]))
                v.tensor_scalar(fnm[:, h:h + 1], fmv[:, h, 0:1], frs[:, h:h + 1], -1.0, ALU.mult, ALU.mult).then_inc(s_fs2, 1)
            dve.wait_ge(s_lo, 1)
            link(v.tensor_reduce(tw[:, 0:1], dlo[:, 0, 0, :], AX.X, ALU.add))
            link(v.tensor_reduce(tw[:, 1:2], dlo[:, 1, :, :], AX.XY, ALU.add))
            link(v.tensor_scalar(tw[:, 2:4], tw[:, 0:2], 1.0, FAR, ALU.min, ALU.mult))
            link(v.tensor_tensor(tw[:, 4:6], tw[:, 2:4], tokf[:, :], ALU.add))
            v.tensor_copy(tokw[:, :], tw[:, 4:6]).then_inc(s_tw, 1)
            for h in range(2):
                dve.wait_ge(s_t, 2 + h)
                v.tensor_copy(fT[:, 0:4, h * P:(h + 1) * P], pT[:, h, 0, :].rearrange("p (a b) -> p a b", b=P))
                v.tensor_copy(fT[:, 4:8, h * P:(h + 1) * P], pT[:, h, 1, :].rearrange("p (a b) -> p a b", b=P)).then_inc(s_fT, 1)
            dve.wait_ge(s_q[7], 16)
            for h in range(2):
                dve.wait_ge(s_t, 5 + h)
                for n in range(2):
                    ins = v.tensor_scalar(ct[:, h, n * 512:(n + 1) * 512], pT[:, h, n, :], gcol[:, h:h + 1], None, ALU.mult)
            ins.then_inc(s_ct, 1)
            dve.wait_ge(s_t, 7)
            dve.wait_ge(s_fn, 2)
            for h in range(2):
                for n in range(2):
                    o = slice(n * 512, (n + 1) * 512)
                    ins = v.tensor_tensor(fx[:, h, o], fx[:, h, o], pT[:, h, n, :], ALU.add)
            ins.then_inc(s_fz, 1)

        @block.gpsimd
        def _(pool):
            g_ = nc.gpsimd
            chain = [0]

            def link(ins):
                chain[0] += 1
                ins.then_inc(s_p, 1)
                pool.wait_ge(s_p, chain[0])

            dmas = [0]

            def dma_all(issue):
                dmas[0] += issue()
                pool.wait_ge(s_pd, 16 * dmas[0])

            link(g_.memset(ident[:, :], 0.0))
            g_.affine_select(out=ident[:, :], in_=ident[:, :], compare_op=ALU.not_equal, fill=1.0, base=0,
                             pattern=[[-1, P]], channel_multiplier=1).then_inc(s_id, 1)
            g_.iota(pcol[:, :], [[0, 1]], base=0, channel_multiplier=1, allow_small_or_imprecise_dtypes=True)
            g_.iota(keyr[:, :], [[1, EP], [0, EJ]], base=0, channel_multiplier=0, allow_small_or_imprecise_dtypes=True).then_inc(s_pk, 1)
            npad = EPAD - NE
            g_.memset(padi[:, 0:2], -1)
            g_.memset(padi[:, 2:2 + 2 * npad], PADV)
            link(g_.memset(padi[:, 2 + 2 * npad:4 + 2 * npad], 2 * NPAD))
            link(g_.memset(zt[:, :], 0.0))
            def init():
                pool.dma_start(SO[0:1, :], padi[:, 0:2]).then_inc(s_pd, 16)
                pool.dma_start(SO[NE + 1:EPAD + 2, :].rearrange("(a n) c -> a (n c)", a=1), padi[:, 2:4 + 2 * npad]).then_inc(s_pd, 16)
                pool.dma_start(T.rearrange("(p n) a -> p (n a)", p=P), zt[:, :]).then_inc(s_pd, 16)
                return 3
            dma_all(init)
            pool.wait_ge(s_eq, 2)
            g_.affine_select(out=eq[:, :, :], in_=eq[:, :, :], compare_op=ALU.is_gt, fill=0.0, base=0,
                             pattern=[[1, EJ], [-1, EJ]], channel_multiplier=0).then_inc(s_eq, 1)
            g_.iota(slot[:, :], [[P, ET]], base=0, channel_multiplier=1, allow_small_or_imprecise_dtypes=True)
            g_.iota(slot1[:, :], [[P, ET]], base=1, channel_multiplier=1, allow_small_or_imprecise_dtypes=True)
            g_.iota(fbase[:, :], [[0, 1]], base=-1, channel_multiplier=P, allow_small_or_imprecise_dtypes=True)
            link(g_.memset(own[:, :], 1.0))
            link(g_.affine_select(out=own[:, :], in_=own[:, :], compare_op=ALU.not_equal, fill=0.0, base=0,
                                  pattern=[[-1, ET]], channel_multiplier=1))
            link(g_.affine_select(out=own[:, :], in_=own[:, :], compare_op=ALU.not_equal, fill=0.0, base=-ET,
                                  pattern=[[-1, ET]], channel_multiplier=1))
            link(g_.tensor_scalar(own[:, :], own[:, :], -1.0, 1.0, ALU.mult, ALU.add))

            pool.wait_ge(s_sgn, EJ)
            pool.wait_ge(s_c0, 1)
            link(g_.tensor_scalar(posf[:, :], sgn[:, :], 0.5, 0.0, ALU.mult, ALU.add))
            link(g_.tensor_tensor(posf[:, :], posf[:, :], c0[:, :], ALU.add))
            link(g_.tensor_copy(posi[:, :], posf[:, :]))

            def scatter(dst_, idx, src_, bound, s):
                pool.indirect_dma_start(out=dst_, out_offset=bass.IndirectOffsetOnAxis(ap=idx, axis=0), in_=src_, in_offset=None,
                                        bounds_check=bound, oob_is_err=False).then_inc(s, 16)

            def gather(dst_, src_, idx, bound, s):
                pool.indirect_dma_start(out=dst_, out_offset=None, in_=src_, in_offset=bass.IndirectOffsetOnAxis(ap=idx, axis=0),
                                        bounds_check=bound, oob_is_err=False).then_inc(s, 16)

            def sort():
                for j in range(EJ):
                    scatter(SO[:, :], posi[:, j:j + 1], pairs[:, j, :], EPAD + 1, s_pd)
                return EJ
            dma_all(sort)

            def sorted_loads():
                for o, tile in ((1, cur), (2, nxt), (0, prv)):
                    pool.dma_start(tile[:, :, :], SO[o:o + EPAD, :].rearrange("(t p) c -> p t c", p=P)).then_inc(s_pd, 16)
                pool.dma_start(curR[:, :, :], SO[1:1 + EPAD, :].rearrange("(t p) c -> t p c", p=P)).then_inc(s_pd, 16)
                tiles = SO[1:1 + EPAD, :].rearrange("(t p) c -> p t c", p=P)
                with nc.allow_non_contiguous_dma(reason="boundary nodes"):
                    for s, r in ((0, 0), (1, P - 1)):
                        pool.dma_start(brow[:, s, :], tiles[r, :, 0].unsqueeze(0).to_broadcast([P, ET])).then_inc(s_pd, 16)
                        pool.dma_start(bcol[s * ET:(s + 1) * ET, 0:1], tiles[r, :, 0:1]).then_inc(s_pd, 16)
                        pool.dma_start(bcol[0:ET, 1 + s:2 + s], tiles[r, :, 0:1]).then_inc(s_pd, 16)
                        pool.dma_start(bcol[ET:2 * ET, 1 + s:2 + s], tiles[r, :, 0:1]).then_inc(s_pd, 16)
                return 12
            dma_all(sorted_loads)
            link(g_.tensor_copy(dR[:, :], curR[:, :, 0]))

            def rows_out():
                pool.dma_start(SD.rearrange("(t p) -> t p", p=P), dR[:, :]).then_inc(s_pd, 16)
                return 1
            dma_all(rows_out)
            pool.wait_ge(s_key, 1)
            pool.dma_start(drow[:, :], SD.rearrange("(a n) -> a n", a=1).to_broadcast([P, EPAD])).then_inc(s_dr, 16)

            def f32(dst_, src_):
                link(g_.tensor_copy(dst_, src_))
            f32(curf[:, :], cur[:, :, 0])
            f32(w[0][:, :], nxt[:, :, 0])
            f32(w[1][:, :], prv[:, :, 0])
            f32(w[2][:, :], cur[:, :, 1])
            f32(browf[:, :, :], brow[:, :, :])
            f32(bcf[:, :], bcol[:, :])
            f32(dRf[:, :], dR[:, :])
            sub = lambda o, a, b: link(g_.tensor_tensor(o, a, b, ALU.subtract))
            add = lambda o, a, b: link(g_.tensor_tensor(o, a, b, ALU.add))
            ts = lambda o, a, s1, s2, o0, o1: link(g_.tensor_scalar(o, a, s1, s2, o0, o1))
            sub(w[3][:, :], w[0][:, :], curf[:, :])
            ts(w[3][:, :], w[3][:, :], 0.0, FAR, ALU.is_equal, ALU.mult)
            sub(w[4][:, :], curf[:, :], w[1][:, :])
            ts(w[4][:, :], w[4][:, :], 0.0, FAR, ALU.is_equal, ALU.mult)
            ts(w[5][:, :], curf[:, :], 2.0, 0.0, ALU.mult, ALU.add)
            ts(w[6][:, :], curf[:, :], 2.0, 1.0, ALU.mult, ALU.add)
            add(w[4][:, :], w[4][:, :], w[5][:, :])
            link(g_.tensor_copy(ifst[:, :], w[4][:, :]))
            add(w[7][:, :], w[3][:, :], w[6][:, :])
            link(g_.tensor_copy(ilst[:, :], w[7][:, :]))
            link(g_.tensor_copy(iout[:, :], w[7][:, :]))
            add(w[8][:, :], w[3][:, :], curf[:, :])
            link(g_.tensor_copy(inode[:, :], w[8][:, :]))
            link(g_.tensor_copy(ixr[:, :], w[6][:, :]))
            link(g_.tensor_copy(isrc[:, :], w[2][:, :]))
            link(g_.tensor_copy(idst[:, :], curf[:, :]))
            link(g_.tensor_copy(ilast[:, :], bcf[0:ET, 2:3]))
            link(g_.tensor_copy(ifn[:, :], bcf[0:ET, 1:2]))

            sub(ovl[:, :], bcf[:, 1:2], bcf[:, 2:3])
            ts(ovl[:, :], ovl[:, :], 0.0, 1.0, ALU.is_equal, ALU.mult)
            ts(ovl[:, :], ovl[:, :], -1.0, 1.0, ALU.mult, ALU.add)
            link(g_.memset(ovl[0:ET, :], 1.0))
            ts(own[:, :], own[:, :], ovl[:, :], 0.0, ALU.mult, ALU.add)
            g_.memset(mhalf[:, 0:1], 0.0).then_inc(s_tab, 1)

            def spans():
                for t in range(ET):
                    scatter(T, ifst[:, t:t + 1], slot[:, t:t + 1], 2 * NPAD - 1, s_pd)
                    scatter(T, ilst[:, t:t + 1], slot1[:, t:t + 1], 2 * NPAD - 1, s_pd)
                return 2 * ET
            dma_all(spans)
            T2 = T.rearrange("(n c) a -> n (c a)", c=2)

            def span_rows():
                for t in range(ET):
                    gather(TS[:, t, :], T2, isrc[:, t:t + 1], NPAD - 1, s_pd)
                    gather(TD[:, t, :], T2, idst[:, t:t + 1], NPAD - 1, s_pd)
                gather(TL[:, :], T2, ifn[:, :], NPAD - 1, s_pd)
                return 2 * ET + 1
            dma_all(span_rows)
            pool.wait_ge(s_sg[0], 16 * ((NT + 1) // 2))
            pool.wait_ge(s_sg[1], 16 * (NT // 2))
            for s in range(XS):
                n = (NT - s + XS - 1) // XS
                pool.wait_ge(s_st[s], 16 * n)
                pool.wait_ge(s_sr[s], 32 * n)
            pool.wait_ge(s_mm, NT)
            for g in range(GQ):
                for t in range(g * GT, (g + 1) * GT):
                    gather(Z[:, t, :], G, isrc[:, t:t + 1], NPAD - 1, s_zg[g])
            sub(w[9][:, :], TS[:, :, 1], TS[:, :, 0])
            sub(w[10][:, :], TD[:, :, 1], TD[:, :, 0])
            ts(w[0][:, :], w[9][:, :], 0.0, FAR, ALU.is_equal, ALU.mult)
            add(w[0][:, :], w[0][:, :], TS[:, :, 1])
            ts(w[0][:, :], w[0][:, :], 1.0, -1.0, ALU.mult, ALU.add)
            link(g_.tensor_copy(ilsrc[:, :], w[0][:, :]))
            ts(w[9][:, :], w[9][:, :], 1.0, 0.0, ALU.max, ALU.add)
            ts(w[10][:, :], w[10][:, :], 1.0, 0.0, ALU.max, ALU.add)
            link(g_.tensor_tensor(w[9][:, :], w[9][:, :], w[10][:, :], ALU.mult))
            link(g_.memset(mhalf[:, :], -0.5))
            link(g_.tensor_tensor(norm[:, :], w[9][:, :], mhalf[:, :], ALU.pow))
            ts(sm[:, 0:1], bcf[0:ET, 2:3], 1.0, 0.0, ALU.mult, ALU.add)
            ts(Lm[:, :], browf[0:ET, 0, :], sm[:, 0:1], 1.0, ALU.is_equal, ALU.mult)
            link(g_.affine_select(out=Lm[:, :], in_=Lm[:, :], compare_op=ALU.is_gt, fill=0.0, base=0,
                                  pattern=[[1, ET]], channel_multiplier=-1))
            ts(sm[:, 1:2], fbase[:, :], 1.0, float(P), ALU.mult, ALU.add)
            ts(sm[:, 2:3], TL[:, 1:2], 1.0, -1.0, ALU.mult, ALU.add)
            ts(sm[:, 3:4], sm[:, 2:3], sm[:, 1:2], 0.0, ALU.min, ALU.add)
            link(g_.tensor_copy(fidx[:, :], sm[:, 3:4]))
            sub(sm[:, 4:5], sm[:, 2:3], sm[:, 3:4])
            ts(sm[:, 4:5], sm[:, 4:5], 0.0, FAR, ALU.is_gt, ALU.mult)
            ts(sm[:, 5:6], bcf[0:ET, 1:2], 2.0, 1.0, ALU.mult, ALU.add)
            add(sm[:, 6:7], sm[:, 4:5], sm[:, 5:6])
            link(g_.tensor_copy(ispo[:, :], sm[:, 6:7]))
            link(g_.tensor_copy(ispx[:, :], sm[:, 5:6]))
            add(sm[:, 7:8], sm[:, 4:5], bcf[0:ET, 1:2])
            link(g_.tensor_copy(ispn[:, :], sm[:, 7:8]))
            g_.memset(mhalf[:, 0:1], 0.0).then_inc(s_nrm, 1)
            pool.wait_ge(s_E, 2)
            for g in range(GQ):
                for t in range(g * GT, (g + 1) * GT):
                    gather(V[:, t, :], G, idst[:, t:t + 1], NPAD - 1, s_vg[g])
            gather(RC0[:, :], G, ilast[:, :], NPAD - 1, s_r0)

            for k in range(K):
                if k == K - 1:
                    for g in range(GQ):
                        pool.wait_ge(s_wm, ET * k + GT * (g + 1))
                        for t in range(g * GT, (g + 1) * GT):
                            gather(Z[:, t, 0:H], xh, ixr[:, t:t + 1], 2 * N - 1, s_xg[g])
                for g in range(GQ):
                    pool.wait_ge(s_vw[g], 16 * (k + 1))
                pool.wait_ge(s_cc, k + 1)
                pool.indirect_dma_start(out=Vd[k % 2], out_offset=bass.IndirectOffsetOnAxis(ap=fidx[:, :], axis=0), in_=corr[:, :],
                                        in_offset=None, bounds_check=EPAD - 1, oob_is_err=True, compute_op=ALU.add).then_inc(s_ca, 16)
                pool.wait_ge(s_ca, 16 * (k + 1))
                if k < K - 1:
                    for g in range(GQ):
                        for t in range(g * GT, (g + 1) * GT):
                            gather(Z[:, t, :], Vd[k % 2], ilsrc[:, t:t + 1], EPAD - 1, s_zg[g])

            for t in range(ET):
                pool.wait_ge(s_fq, t + 1)
                scatter(outh, iout[:, t:t + 1], Z[:, t, 0:H], 2 * N - 1, s_fs)
                scatter(NDB, inode[:, t:t + 1], Z[:, t, H:R], NPAD - 1, s_fs)
            pool.wait_ge(s_sz, 1)
            gather(Sv[:, :], Vd[(K - 1) % 2], fidx[:, :], EPAD - 1, s_sp)
            gather(Sx[:, 0:H], xh, ispx[:, :], 2 * N - 1, s_sp)
            pool.wait_ge(s_fs, 16 * 2 * ET)
            pool.wait_ge(s_sa, 1)
            scatter(outh, ispo[:, :], Sx[:, 0:H], 2 * N - 1, s_ss)
            scatter(NDB, ispn[:, :], Sx[:, H:R], NPAD - 1, s_ss)
            pool.wait_ge(s_ss, 32)

            link(g_.iota(tbase[:, :], [[0, 1]], base=0, channel_multiplier=NPAD // 16, allow_small_or_imprecise_dtypes=True))
            link(g_.iota(gbase[:, :], [[0, 1]], base=0, channel_multiplier=16 * TOPK, allow_small_or_imprecise_dtypes=True))
            for r in range(4):
                for h in range(2):
                    link(g_.memset(ebase[32 * r:32 * r + 32, h:h + 1], float(NPAD * (4 * h + r))))
            link(g_.memset(esel[:, :, :], 1.0))
            for h in range(2):
                link(g_.affine_select(out=esel[:, h, :], in_=esel[:, h, :], compare_op=ALU.is_ge, fill=0.0, base=P * h,
                                      pattern=[[1, P]], channel_multiplier=-TOPK))
                link(g_.affine_select(out=esel[:, h, :], in_=esel[:, h, :], compare_op=ALU.is_ge, fill=0.0, base=TOPK - 1 - P * h,
                                      pattern=[[-1, P]], channel_multiplier=TOPK))
            g_.memset(tw[:, :], 0.0).then_inc(s_g, 1)
            pool.wait_ge(s_sc, 1)
            g_.affine_select(out=sct[:, :, :], in_=sct[:, :, :], compare_op=ALU.is_ge, fill=-1.0, base=N - 1,
                             pattern=[[0, EX], [-1, NT]], channel_multiplier=-NT).then_inc(s_msk, 1)
            pool.wait_ge(s_q[6], 16)
            pool.wait_ge(s_q[3], 16)
            for h in range(2):
                gather(tokw[:, h:h + 1], CI, pcl[:, h:h + 1], P * TOPK - 1, s_q[8])
            pool.wait_ge(s_tk, 1)
            for h in range(2):
                gather(fx[:, h, :], out, tok[:, h:h + 1], N - 1, s_fx[h])
            pool.wait_ge(s_dq, 1)
            g_.affine_select(out=dlo[:, 0, 0, :], in_=dq[:, 0, 0, :], compare_op=ALU.is_gt, fill=0.0, base=0,
                             pattern=[[-1, P]], channel_multiplier=1)
            g_.affine_select(out=dlo[:, 1, 1, :], in_=dq[:, 1, 1, :], compare_op=ALU.is_gt, fill=0.0, base=0,
                             pattern=[[-1, P]], channel_multiplier=1)
            g_.tensor_copy(dlo[:, 1, 0, :], dq[:, 1, 0, :]).then_inc(s_lo, 1)
            pool.wait_ge(s_fz, 1)
            pool.wait_ge(s_tw, 1)
            for h in range(2):
                scatter(out, tokw[:, h:h + 1], fx[:, h, :], N - 1, s_q[9])
            pool.wait_ge(s_q[9], 32)


_INS = ["x", "src", "dst", "L0_gnn_W1", "L0_gnn_b1", "L0_gnn_Wg", "L0_gnn_bg", "L0_ffn_router_w", "L0_ffn_router_b",
        "L0_ffn_w1", "L0_ffn_b1", "L0_ffn_w2", "L0_ffn_b2"]


def kernel(**inputs):
    import numpy as _np
    import concourse.bacc as _bacc
    from concourse import mybir as _mybir
    from concourse.bass_utils import run_bass_kernel_spmd as _run

    nc = _bacc.Bacc("TRN2", target_bir_lowering=False, num_devices=1)
    arrays, args = {}, []
    for name in _INS:
        a = _np.ascontiguousarray(inputs[name])
        arrays[f"in_{name}"] = a
        args.append(nc.dram_tensor(f"in_{name}", a.shape, _mybir.dt.from_np(a.dtype), kind="ExternalInput").ap())
    f32, i32 = _mybir.dt.float32, _mybir.dt.int32
    args.append(nc.dram_tensor("out_0", inputs["x"].shape, f32, kind="ExternalOutput").ap())

    def scratch(name, shape, dt):
        return nc.dram_tensor(name, shape, dt, kind="Internal").ap()

    npad, epad = 10112, 5120
    args += [scratch("node_rows", (npad, 528), f32), scratch("sorted_pairs", (epad + 2, 2), i32),
             scratch("sorted_dst", (epad,), i32), scratch("spans", (2 * npad, 1), f32),
             [scratch("v_even", (epad, 528), f32), scratch("v_odd", (epad, 528), f32)],
             scratch("node_left", (npad, 24), f32), scratch("node_right", (npad, 16), f32),
             scratch("scores", (8, npad), f32), scratch("cand_values", (4096,), f32),
             scratch("cand_numbers", (4096, 1), i32), scratch("chosen", (512,), i32)]
    gnn_ffn(nc, *args)
    r = _run(nc, [arrays], core_ids=[0])
    return r.results[0]["out_0"]
```

```python
from contextlib import ExitStack

import concourse.bass as bass
from concourse import mybir

F32 = mybir.dt.float32
BF16 = mybir.dt.bfloat16
I32 = mybir.dt.int32
U32 = mybir.dt.uint32
F32R = mybir.dt.float32r
ALU = mybir.AluOpType
ACT = mybir.ActivationFunctionType
AX = mybir.AxisListType

P = 128
EPS = 1e-5
FAR = 1000000.0


def gnn_ffn(nc, x, src, dst, W1, b1, Wg, bg, rw, rb, fw1, fb1, fw2, fb2, out,
            G, SO, SD, T, Vd, NDA, NDB, SC, CV, CI, PQ):
    N, D = x.shape
    H = W1.shape[1]
    K = Wg.shape[0]
    NE = src.shape[0]
    EX, FF = fb1.shape
    NT = (N + P - 1) // P
    LAST = N - (NT - 1) * P
    NPAD = NT * P
    DC = D // P
    HC = H // P
    NP = 2 * K + EX
    WHALF = (H + NP + 2 * EX) // 2
    R = H + NP
    NQ = NP + EX
    WX = H + NQ + EX
    ET = (NE + P - 1) // P
    EJ = ET
    EP = NE // EJ
    EPAD = ET * P
    PADV = NPAD - 1
    GQ = 8
    GT = ET // GQ
    TOPK = 32
    XS = 6
    AHEAD = 4
    assert EP * EJ == NE and NT == 79 and NP == 16 and XS % 2 == 0

    xh = x.rearrange("n (h c) -> (n h) c", h=2)
    outh = out.rearrange("n (h c) -> (n h) c", h=2)

    with ExitStack() as ctx:
        def sb(name, shape, dt=F32, c=ctx):
            return c.enter_context(nc.sbuf_tensor(name, shape, dt))

        def sem(name):
            return ctx.enter_context(nc.semaphore(name))

        ident = sb("ident", [P, P])
        E = sb("E", [P, ET, P], BF16)
        Fsel = sb("Fsel", [2 * ET, ET, P], BF16)
        TBl = sb("TBl", [P, ET, 2 * ET], BF16)
        norm = sb("norm", [P, ET])
        m = sb("m", [P, ET])
        pre = sb("pre", [P, ET])
        al = sb("al", [P, ET])
        Vpi = sb("Vpi", [P, ET, K])
        bgb = sb("bgb", [P, K])
        rbb = sb("rbb", [P, EX])
        csrw = sb("csrw", [P, EX])
        bRa = sb("bRa", [P, EX])
        curf = sb("curf", [P, ET])
        isrc = sb("isrc", [P, ET], I32)
        idst = sb("idst", [P, ET], I32)
        ilsrc = sb("ilsrc", [P, ET], I32)
        iout = sb("iout", [P, ET], I32)
        inode = sb("inode", [P, ET], I32)
        ixr = sb("ixr", [P, ET], I32)
        Lm = sb("Lm", [ET, ET])
        fidx = sb("fidx", [ET, 1], I32)
        ilast = sb("ilast", [ET, 1], I32)
        ispo = sb("ispo", [ET, 1], I32)
        ispn = sb("ispn", [ET, 1], I32)
        ispx = sb("ispx", [ET, 1], I32)
        eps = sb("eps", [P, 1])

        with ExitStack() as c:
            Z = sb("Z", [P, ET, R], c=c)
            V = sb("V", [P, ET, R], c=c)
            E32 = sb("E32", [P, 2, P], c=c)
            RC = sb("RC", [ET, R], c=c)
            RC0 = sb("RC0", [ET, R], c=c)
            corr = sb("corr", [ET, R], c=c)
            zf = sb("zf", [P, 2 * GT, K], c=c)
            z3 = sb("z3", [P, ET, 3 * K], BF16, c=c)
            tbf = sb("tbf", [2 * ET, 3 * K], c=c)
            tb3 = sb("tb3", [2 * ET, 3 * K], BF16, c=c)
            junkc = sb("junkc", [P, H], BF16, c=c)
            Sv, Sx = RC0, RC
        with ExitStack() as c:
            wext = sb("wext", [P, DC, WX], c=c)
            xr = sb("xr", [P, XS, D], c=c)
            xn = sb("xn", [P, 2, D], c=c)
            xh_ = sb("xh", [P, 2, DC, P], F32R, c=c)
            xl_ = sb("xl", [P, 2, DC, P], F32R, c=c)
            wh = sb("wh", [P, DC, WX], F32R, c=c)
            wl = sb("wl", [P, DC, WX], F32R, c=c)
            x1s = sb("x1s", [P, 2, R], c=c)
            recA = sb("recA", [P, XS, 24], c=c)
            recB = sb("recB", [P, XS, 16], c=c)
            bns = sb("bns", [P, 2, 2, 6], c=c)
            sdv = sb("sdv", [P, 2], c=c)
            rsd = sb("rsd", [P, 2], c=c)
            nmr = sb("nmr", [P, 2], c=c)
            b1e = sb("b1e", [P, R], c=c)
            Rp = sb("Rp", [P, HC, NQ], c=c)
            wT = xn[:, 0, :].rearrange("p (s a b) -> p s a b", s=2, b=P)
            b1c = sb("b1c", [P, HC], c=c)
            ones = sb("ones", [P, P], c=c)
            junka = sb("junka", [P, 2, H], BF16, c=c)
            keyr = sb("keyr", [EP, NE], c=c)
            junks = sb("junks", [EP, NE], BF16, c=c)
            drow = sb("drow", [P, EPAD], I32, c=c)
            eq = sb("eq", [EP, EJ, EJ], c=c)
            ei = sb("ei", [EP, 2, EJ], I32, c=c)
            pairs = sb("pairs", [EP, EJ, 2], I32, c=c)
            dstf = sb("dstf", [EP, EJ], c=c)
            key = sb("key", [EP, EJ], c=c)
            pcol = sb("pcol", [EP, 1], c=c)
            sgn = sb("sgn", [EP, EJ], c=c)
            ceq = sb("ceq", [EP, EJ], c=c)
            clt = sb("clt", [EP, EJ], c=c)
            c0 = sb("c0", [EP, EJ], c=c)
            posf = sb("posf", [EP, EJ], c=c)
            posi = sb("posi", [EP, EJ], I32, c=c)
            padi = sb("padi", [1, 2 * (EPAD - NE + 2)], I32, c=c)
            zt = sb("zt", [P, 2 * NPAD // P], c=c)
            cur = sb("cur", [P, ET, 2], I32, c=c)
            nxt = sb("nxt", [P, ET, 2], I32, c=c)
            prv = sb("prv", [P, ET, 2], I32, c=c)
            w = [sb(f"w{i}", [P, ET], c=c) for i in range(12)]
            slot = sb("slot", [P, ET], c=c)
            slot1 = sb("slot1", [P, ET], c=c)
            ifst = sb("ifst", [P, ET], I32, c=c)
            ilst = sb("ilst", [P, ET], I32, c=c)
            TS = sb("TS", [P, ET, 2], c=c)
            TD = sb("TD", [P, ET, 2], c=c)
            curR = sb("curR", [ET, P, 2], I32, c=c)
            dR = sb("dR", [ET, P], I32, c=c)
            dRf = sb("dRf", [ET, P], c=c)
            brow = sb("brow", [P, 2, ET], I32, c=c)
            browf = sb("browf", [P, 2, ET], c=c)
            bcol = sb("bcol", [2 * ET, 3], I32, c=c)
            bcf = sb("bcf", [2 * ET, 3], c=c)
            own = sb("own", [2 * ET, ET], c=c)
            sm = sb("sm", [ET, 10], c=c)
            fbase = sb("fbase", [ET, 1], c=c)
            TL = sb("TL", [ET, 2], c=c)
            ifn = sb("ifn", [ET, 1], I32, c=c)
            mark = sb("mark", [P, 3], c=c)
            ovl = sb("ovl", [2 * ET, 1], c=c)
        with ExitStack() as c:
            ndA = sb("ndA", [P, NT, 24], c=c)
            ndB = sb("ndB", [P, NT, 16], c=c)
            q = [sb(f"q{i}", [P, NT], c=c) for i in range(6)]
            lg = sb("lg", [P, NT, EX], c=c)
            lt = sb("lt", [P, NT, EX], c=c)
            sct = sb("sct", [P, EX, NT], c=c)
            tk = sb("tk", [P, TOPK // 8, NPAD * EX // P], c=c)
            tv = sb("tv", [P, TOPK], c=c)
            ti = sb("ti", [P, TOPK], U32, c=c)
            tif = sb("tif", [P, TOPK], c=c)
            tgi = sb("tgi", [P, TOPK], I32, c=c)
            tbase = sb("tbase", [P, 1], c=c)
            cv = sb("cv", [EX, TOPK // 8, 16 * TOPK], c=c)
            gv = sb("gv", [EX, TOPK], c=c)
            gi = sb("gi", [EX, TOPK], U32, c=c)
            gif = sb("gif", [EX, TOPK], c=c)
            gbase = sb("gbase", [EX, 1], c=c)
            gpi = sb("gpi", [EX, TOPK], I32, c=c)
            gcol = sb("gcol", [P, 2], c=c)
            pcl = sb("pcl", [P, 2], I32, c=c)
            tok = sb("tok", [P, 2], I32, c=c)
            tokf = sb("tokf", [P, 2], c=c)
            tokw = sb("tokw", [P, 2], I32, c=c)
            tw = sb("tw", [P, 6], c=c)
            fx = sb("fx", [P, 2, D], c=c)
            fn = sb("fn", [P, 2, D], c=c)
            fT = sb("fT", [P, DC, 2 * P], c=c)
            w1e = sb("w1e", [P, EX // 2, DC, 2 * FF], c=c)
            w2e = sb("w2e", [2 * FF, EX // 2, D], c=c)
            b1t = sb("b1t", [2 * FF, EX // 2], c=c)
            b2t = sb("b2t", [EX, D], c=c)
            h1 = sb("h1", [2 * FF, EX // 2, P], c=c)
            esel = sb("esel", [EX, 2, P], c=c)
            ct = sb("ct", [P, 2, D], c=c)
            dq = sb("dq", [P, 2, 2, P], c=c)
            dlo = sb("dlo", [P, 2, 2, P], c=c)
            fst = sb("fst", [P, 2, 2, 6], c=c)
            fmv = sb("fmv", [P, 2, 2], c=c)
            fsd = sb("fsd", [P, 2], c=c)
            frs = sb("frs", [P, 2], c=c)
            fnm = sb("fnm", [P, 2], c=c)
            diag = sb("diag", [P, 2, P], c=c)
            onesf = sb("onesf", [P, P], c=c)
            ebase = sb("ebase", [P, 2], c=c)

        def psum(name, shape):
            return ctx.enter_context(nc.psum_tensor(name, shape, F32))

        pT = psum("pT", [P, 2, 2, 512])
        pW = psum("pW", [P, 4, 512])
        pA = pW[:, 0:2, :]
        pB, pC = pW[:, 2, :], pW[:, 3, :]
        pBC = [pB, pC]
        pN = pT[:, 0, 0, :]

        x_landed = [sem(f"x_landed_slot{i}") for i in range(XS)]
        out_stored = [sem(f"out_stored_slot{i}") for i in range(XS)]
        x1_stored = [sem(f"x1_stored_slot{i}") for i in range(2)]
        records_stored = [sem(f"records_stored_slot{i}") for i in range(XS)]
        weights_landed = sem("weights_landed")
        ident_ready = sem("ident_ready")
        stats_ready = sem("stats_ready")
        var_ready = sem("var_ready")
        std_ready = sem("std_ready")
        rstd_ready = sem("rstd_ready")
        shift_ready = sem("shift_ready")
        xn_ready = sem("xn_ready")
        tile_turned = sem("tile_turned")
        high0_ready = sem("high0_ready")
        lows_ready = sem("lows_ready")
        w_high_ready = sem("w_high_ready")
        high1_ready = sem("high1_ready")
        tile_multiplied = sem("tile_multiplied")
        x1_ready = sem("x1_ready")
        x1_tail_ready = sem("x1_tail_ready")
        rows_ready = sem("rows_ready")
        squares_ready = sem("squares_ready")
        w1_turned = sem("w1_turned")
        w1_copied = sem("w1_copied")
        w1_projected = sem("w1_projected")
        projection_copied = sem("projection_copied")
        edges_landed = sem("edges_landed")
        ranks_ready = sem("ranks_ready")
        pool_step = sem("pool_step")
        pool_dma = sem("pool_dma")
        tables_ready = sem("tables_ready")
        z_landed = [sem(f"z_landed_slot{i}") for i in range(GQ)]
        v_landed = [sem(f"v_landed_slot{i}") for i in range(GQ)]
        rc0_landed = sem("rc0_landed")
        arg_ready = sem("arg_ready")
        tanh_ready = sem("tanh_ready")
        coef_ready = sem("coef_ready")
        split_ready = sem("split_ready")
        sel_ready = sem("sel_ready")
        agg_ready = sem("agg_ready")
        v_added = sem("v_added")
        v_stored = [sem(f"v_stored_slot{i}") for i in range(GQ)]
        rc_landed = sem("rc_landed")
        rc_diff_ready = sem("rc_diff_ready")
        carry_ready = sem("carry_ready")
        carry_copied = sem("carry_copied")
        carry_added = sem("carry_added")
        bound_sums_ready = sem("bound_sums_ready")
        bound_step = sem("bound_step")
        dst_sums_ready = sem("dst_sums_ready")
        xright_landed = [sem(f"xright_landed_slot{i}") for i in range(GQ)]
        final_ready = sem("final_ready")
        final_squares = sem("final_squares")
        final_stored = sem("final_stored")
        special_landed = sem("special_landed")
        special_rows = sem("special_rows")
        special_squares = sem("special_squares")
        special_stored = sem("special_stored")
        expert_w_landed = sem("expert_w_landed")
        nodes_landed = [sem(f"nodes_landed_{i}") for i in "AB"]
        dve_step = sem("dve_step")
        pool_const_ready = sem("pool_const_ready")
        pe_done = sem("pe_done")
        tail_dma = [sem(f"tail_dma_slot{i}") for i in range(10)]

        keys_ready = sem("keys_ready")
        w_low_ready = sem("w_low_ready")
        equal_step = sem("equal_step")
        offset_ready = sem("offset_ready")
        const_ready = sem("const_ready")
        partitions_ready = sem("partitions_ready")
        select_ready = sem("select_ready")
        hidden_ready = sem("hidden_ready")
        best_ready = sem("best_ready")
        degrees_ready = sem("degrees_ready")
        roots_ready = sem("roots_ready")
        norm_ready = sem("norm_ready")
        dst_row_landed = sem("dst_row_landed")
        special_cleared = sem("special_cleared")
        roots_of_var = sem("roots_of_var")
        exp_ready = sem("exp_ready")
        expert_std = sem("expert_std")
        final_var_ready = sem("final_var_ready")
        logits_ready = sem("logits_ready")
        scores_ready = sem("scores_ready")
        scores_masked = sem("scores_masked")
        candidates_ready = sem("candidates_ready")
        chosen_ready = sem("chosen_ready")
        tokens_ready = sem("tokens_ready")
        diag_ready = sem("diag_ready")
        same_token_ready = sem("same_token_ready")
        expert_var = sem("expert_var")
        expert_shift = sem("expert_shift")
        expert_xn_ready = sem("expert_xn_ready")
        expert_xT_ready = sem("expert_xT_ready")
        h1_cleared = sem("h1_cleared")
        relu_ready = sem("relu_ready")
        contrib_ready = sem("contrib_ready")
        sum_rows_ready = sem("sum_rows_ready")
        earlier_ready = sem("earlier_ready")
        writers_ready = sem("writers_ready")
        chosen_landed = [sem(f"chosen_landed_slot{i}") for i in range(2)]
        NWL = 4 + 2 * K + 4

        block = ctx.enter_context(nc.Block())


        dyn = lambda ap, t: ap[:, bass.ds(t, 1)]
        row = lambda ap, t: ap[:, bass.ds(t, 1), :].rearrange("p a b -> p (a b)")

        def node_loop(eng, step):
            turns, end = ET // XS, (NT - 3) // XS
            for t in range(-2, XS):
                step(0, t, True)
            with eng.Fori(1, turns, 1) as j:
                for u in range(XS):
                    step(j, u, True)
            for u in range(XS):
                step(turns, u, turns * XS + u < ET)
            with eng.Fori(turns + 1, end, 1) as j:
                for u in range(XS):
                    step(j, u, False)
            for u in range(NT - end * XS):
                step(end, u, False)

        def has(i, u, ahead):
            return 0 <= i + u + ahead < NT if isinstance(i, int) else True

        def early(i, u, before):
            return isinstance(i, int) and i + u - before < 0

        def group_tiles(lo, eng, step, after_first=None):
            step(lo or 0, 0, (lo or 0) % 2)
            if after_first:
                after_first()
            if lo is None:
                for u in range(1, GT):
                    step(0, u, u % 2)
                return
            with eng.Fori(lo + 1, lo + GT - 1, 2) as i:
                for u in range(2):
                    step(i, u, (lo + 1 + u) % 2)

        @block.sync
        def _(sp):
            def load(i, u):
                t = i + u
                if isinstance(t, int) and t == NT - 1:
                    sp.dma_start(xr[0:LAST, u % XS, :], x[t * P:N, :]).then_inc(x_landed[u % XS], 16)
                else:
                    sp.dma_start(xr[:, u % XS, :], x[bass.ds(t * P, P), :]).then_inc(x_landed[u % XS], 16)

            with nc.allow_non_contiguous_dma(reason="small weights"):
                sp.dma_start(wext[:, :, 0:H], W1.rearrange("(c p) h -> p c h", p=P)).then_inc(weights_landed, 16)
                sp.dma_start(wext[:, :, H + NQ:WX], rw.rearrange("(c p) e -> p c e", p=P)).then_inc(weights_landed, 16)
                for k in range(K):
                    for s in range(2):
                        sp.dma_start(Rp[:, :, s * K + k], Wg[k, s * H:(s + 1) * H, 0].rearrange("(c p) -> p c", p=P)).then_inc(weights_landed, 16)
                sp.dma_start(Rp[:, :, 2 * K:NP], rw[H:D, :].rearrange("(c p) e -> p c e", p=P)).then_inc(weights_landed, 16)
                sp.dma_start(Rp[:, :, NP:NQ], rw[0:H, :].rearrange("(c p) e -> p c e", p=P)).then_inc(weights_landed, 16)
                sp.dma_start(b1c[:, :], b1.rearrange("(c p) -> p c", p=P)).then_inc(weights_landed, 16)
                sp.dma_start(b1e[:, 0:H], b1.rearrange("(a h) -> a h", a=1).to_broadcast([P, H])).then_inc(weights_landed, 16)
                sp.dma_start(bgb[:, :], bg.rearrange("k a -> a k").to_broadcast([P, K])).then_inc(weights_landed, 16)
                sp.dma_start(rbb[:, :], rb.rearrange("(a h) -> a h", a=1).to_broadcast([P, EX])).then_inc(weights_landed, 16)
                for t in range(AHEAD):
                    load(0, t)
                sp.dma_start(ei[:, 0, :], dst.rearrange("(p j) -> p j", j=EJ)).then_inc(edges_landed, 16)
                sp.dma_start(ei[:, 1, :], src.rearrange("(p j) -> p j", j=EJ)).then_inc(edges_landed, 16)
                sp.dma_start(drow[0:EP, 0:NE], dst.rearrange("(a e) -> a e", a=1).to_broadcast([EP, NE])).then_inc(edges_landed, 16)

            def step(j, u, ranked):
                if u < 0:
                    return
                i = j * XS
                t = i + u
                last = isinstance(t, int) and t == NT - 1
                if has(i, u, AHEAD):
                    if not early(i, u, XS - AHEAD):
                        sp.wait_ge(out_stored[(u + AHEAD) % XS], j * 16 + (16 if u + AHEAD >= XS else 0))
                    load(i, u + AHEAD)
                sp.wait_ge(rows_ready, t + 1)
                if last:
                    sp.dma_start(out[t * P:N, :], xr[0:LAST, u % XS, :]).then_inc(out_stored[u % XS], 16)
                else:
                    sp.dma_start(out[bass.ds(t * P, P), :], xr[:, u % XS, :]).then_inc(out_stored[u % XS], 16)
                sp.dma_start(G[bass.ds(t * P, P), :], x1s[:, u % 2, :]).then_inc(x1_stored[u % 2], 16)
                sp.wait_ge(squares_ready, t * 2 + 2)
                sp.dma_start(NDA[bass.ds(t * P, P), :], recA[:, u % XS, :]).then_inc(records_stored[u % XS], 16)
                sp.dma_start(NDB[bass.ds(t * P, P), :], recB[:, u % XS, :]).then_inc(records_stored[u % XS], 16)

            node_loop(sp, step)

            for k in range(K):
                vd = Vd[k % 2]
                for g in range(GQ):
                    a, b = g * GT, (g + 1) * GT
                    sp.wait_ge(v_added, ET * k + b)
                    if k and g == 0:
                        sp.wait_ge(carry_ready, k)
                    sp.dma_start(RC[a:b, :], V[P - 1:P, a:b, :]).then_inc(rc_landed, 16)
                    sp.dma_start(vd[a * P:b * P, :].rearrange("(t p) c -> p t c", p=P), V[:, a:b, :]).then_inc(v_stored[g], 16)

            sp.wait_ge(final_stored, 16 * 2 * ET)
            sp.wait_ge(special_stored, 32)
            sp.dma_start(ndA[:, :, :].rearrange("p j c -> p (j c)"), NDA.rearrange("(p j) c -> p (j c)", p=P)).then_inc(nodes_landed[0], 16)
            sp.dma_start(ndB[:, :, :].rearrange("p j c -> p (j c)"), NDB.rearrange("(p j) c -> p (j c)", p=P)).then_inc(nodes_landed[1], 16)
            for e in range(EX):
                sp.dma_start(w1e[:, e // 2, :, (e % 2) * FF:(e % 2 + 1) * FF], fw1[e].rearrange("(c p) f -> p c f", p=P)).then_inc(expert_w_landed, 16)
            sp.wait_ge(scores_masked, 1)
            sp.dma_start(SC.rearrange("e (p j) -> p e j", p=P), sct[:, :, :]).then_inc(tail_dma[0], 16)
            sp.wait_ge(tail_dma[0], 16)
            sp.dma_start(tk[:, 0, :], SC.rearrange("e (g n) -> (e g) n", g=16)).then_inc(tail_dma[1], 16)
            sp.dma_start(w2e[:, :, :], fw2.rearrange("(e s) f h -> (s f) e h", s=2)).then_inc(expert_w_landed, 16)
            with nc.allow_non_contiguous_dma(reason="bias columns"):
                sp.dma_start(b1t[:, :], fb1.rearrange("(e s) f -> (s f) e", s=2)).then_inc(expert_w_landed, 16)
            sp.dma_start(b2t[:, :], fb2).then_inc(expert_w_landed, 16)
            sp.wait_ge(best_ready, 1)
            sp.dma_start(CV.rearrange("(p r) -> p r", p=P), tv[:, :]).then_inc(tail_dma[2], 16)
            sp.wait_ge(tail_dma[2], 16)
            sp.dma_start(cv[:, 0, :], CV.rearrange("(e n) -> e n", e=EX)).then_inc(tail_dma[4], 16)
            sp.wait_ge(candidates_ready, 1)
            sp.dma_start(CI.rearrange("(p r) a -> p (r a)", p=P), tgi[:, :]).then_inc(tail_dma[3], 16)
            sp.wait_ge(chosen_ready, 1)
            sp.dma_start(PQ[0:EX * TOPK].rearrange("(e r) -> e r", e=EX), gpi[:, :]).then_inc(tail_dma[5], 16)
            sp.dma_start(PQ[EX * TOPK:2 * EX * TOPK].rearrange("(e r) -> e r", e=EX), gv[:, :].bitcast(I32)).then_inc(tail_dma[5], 16)
            sp.wait_ge(tail_dma[5], 32)
            with nc.allow_non_contiguous_dma(reason="columns of chosen pairs"):
                sp.dma_start(pcl[:, :], PQ[0:EX * TOPK].rearrange("(h p) -> p h", p=P)).then_inc(tail_dma[6], 16)
                sp.dma_start(gcol[:, :].bitcast(I32), PQ[EX * TOPK:2 * EX * TOPK].rearrange("(h p) -> p h", p=P)).then_inc(tail_dma[7], 16)
            sp.wait_ge(tail_dma[9], 32)

        @block.tensor
        def _(pe):
            mmul = nc.tensor.matmul
            pe.wait_ge(weights_landed, 16 * NWL)
            pe.wait_ge(ident_ready, 1)
            def wturn(c):
                if c >= 2:
                    pe.wait_ge(w1_copied, c - 1)
                for q4 in range(HC):
                    mm = nc.tensor.transpose(pT[:, c % 2, 0, q4 * P:(q4 + 1) * P], wext[:, c, q4 * P:(q4 + 1) * P], ident[:, :])
                mm.then_inc(w1_turned, 1)

            wturn(0)
            for c in range(DC):
                if c + 1 < DC:
                    wturn(c + 1)
                pe.wait_ge(w1_copied, c + 1)
                if c >= 2:
                    pe.wait_ge(projection_copied, c - 1)
                for q4 in range(HC):
                    mm = mmul(pBC[c % 2][:, 0:NQ], lhsT=wT[:, c % 2, q4, :], rhs=Rp[:, q4, :], start=(q4 == 0), stop=(q4 == HC - 1))
                mm.then_inc(w1_projected, 1)
            def bias_products():
                pe.wait_ge(const_ready, 2)
                for q4 in range(HC):
                    mm = mmul(pC[:, 0:NQ], lhsT=b1c[:, q4:q4 + 1].to_broadcast([P, P]), rhs=Rp[:, q4, :], start=(q4 == 0), stop=(q4 == HC - 1))
                for c in range(DC):
                    mm = mmul(pC[:, NQ:NQ + EX], lhsT=ones[:, :], rhs=wext[:, c, H + NQ:WX], start=(c == 0), stop=(c == DC - 1))
                mm.then_inc(w1_projected, 1)

            pe.wait_ge(projection_copied, DC)
            def step(j, u, ranked):
                i = j * XS
                t = i + u
                if has(i, u, 1) and u >= -1:
                    pe.wait_ge(xn_ready, t + 2)
                    if not early(i, u, 1):
                        pe.wait_ge(lows_ready, t)
                        pe.wait_ge(high1_ready, t)
                    n = (u + 1) % 2
                    for c in range(DC):
                        mm = nc.tensor.transpose(pT[:, n, c // 4, (c % 4) * P:(c % 4 + 1) * P], xn[:, n, c * P:(c + 1) * P], ident[:, :])
                    mm.then_inc(tile_turned, 1)
                if u >= 0:
                    if isinstance(t, int) and t == 0:
                        bias_products()
                        pe.wait_ge(w_low_ready, DC)
                    if isinstance(t, int) and t == 1:
                        pe.wait_ge(projection_copied, DC + 1)
                    pe.wait_ge(lows_ready, t + 1)
                    pe.wait_ge(high1_ready, t + 1)
                    if not early(i, u, 2):
                        pe.wait_ge(x1_ready, t - 1)
                    n = u % 2
                    for c in range(DC):
                        first, last = c == 0, c == DC - 1
                        h, l = xh_[:, n, c, :], xl_[:, n, c, :]
                        for bank, o in ((pA[:, n, 0:WHALF], slice(0, WHALF)), (pBC[n][:, 0:WHALF], slice(WHALF, WX))):
                            mmul(bank, lhsT=h, rhs=wh[:, c, o], start=first, stop=False)
                            mmul(bank, lhsT=h, rhs=wl[:, c, o], start=False, stop=False)
                        for bank, o in ((pA[:, n, 0:WHALF], slice(0, WHALF)), (pBC[n][:, 0:WHALF], slice(WHALF, WX))):
                            mm = mmul(bank, lhsT=l, rhs=wh[:, c, o], start=False, stop=last)
                    mm.then_inc(tile_multiplied, 1)

            node_loop(pe, step)

            for k in range(K):
                for g in range(GQ):
                    def wide(i, u, n):
                        t = i + u
                        pe.wait_ge(sel_ready, t + (ET * k + 1))
                        if k or g or u >= 2:
                            pe.wait_ge(v_added, t + (ET * k - 1))
                        mmul(pW[:, 2 * n, 0:R // 2], lhsT=E32[:, n, :], rhs=row(Z[:, :, 0:R // 2], t), start=True, stop=True)
                        mmul(pW[:, 2 * n + 1, 0:R // 2], lhsT=E32[:, n, :], rhs=row(Z[:, :, R // 2:R], t), start=True, stop=True).then_inc(agg_ready, 1)
                    group_tiles(g * GT if k or g else None, pe, wide)
                if k < K - 1:
                    pe.wait_ge(split_ready, GQ // 2 * (k + 1))
                    pe.wait_ge(v_added, ET * (k + 1))
                    pe.wait_ge(select_ready, 2)
                    def bsum(t, start, stop):
                        return mmul(pC[0:2 * ET, 0:3 * K], lhsT=TBl[:, t, :], rhs=z3[:, t, :], start=start, stop=stop)
                    for t in range(ET):
                        mm = bsum(t, t == 0, t == ET - 1)
                    mm.then_inc(bound_sums_ready, 1)
                pe.wait_ge(rc_diff_ready, k + 1)
                mmul(pT[0:ET, 1, 0, :], lhsT=Lm[:, :], rhs=RC[:, 0:H], start=True, stop=True)
                mmul(pT[0:ET, 1, 1, 0:NP], lhsT=Lm[:, :], rhs=RC[:, H:R], start=True, stop=True).then_inc(carry_ready, 1)
                if k < K - 1:
                    pe.wait_ge(bound_step, 4 * (k + 1))
                    def nsum(t):
                        o = pN[:, t * 3 * K:(t + 1) * 3 * K]
                        mmul(o, lhsT=E[:, t, :], rhs=z3[:, t, :], start=True, stop=False)
                        return mmul(o, lhsT=Fsel[:, t, :], rhs=tb3[:, :], start=False, stop=True)
                    for t in range(ET):
                        mm = nsum(t)
                    mm.then_inc(dst_sums_ready, 1)
            pe.wait_ge(diag_ready, 1)
            for h in range(2):
                mm = mmul(pC[:, h * P:(h + 1) * P], lhsT=onesf[:, :], rhs=diag[:, h, :], start=True, stop=True)
            mm.then_inc(pe_done, 1)
            for h in range(2):
                pe.wait_ge(expert_xn_ready, h + 1)
                for c in range(DC):
                    mm = nc.tensor.transpose(pT[:, h, c // 4, (c % 4) * P:(c % 4 + 1) * P], fn[:, h, c * P:(c + 1) * P], ident[:, :])
                mm.then_inc(pe_done, 1)
            pe.wait_ge(expert_w_landed, 16 * (EX + 3))
            for e in range(EX // 2):
                pe.wait_ge(expert_xT_ready, e // 2 + 1)
                for c in range(DC):
                    mm = mmul(pA[:, e // 2, 2 * e * TOPK:2 * (e + 1) * TOPK], lhsT=w1e[:, e, c, :], rhs=fT[:, c, 2 * e * TOPK:2 * (e + 1) * TOPK],
                              start=(c == 0), stop=(c == DC - 1))
                if e % 2:
                    mm.then_inc(hidden_ready, 1)
            pe.wait_ge(pool_const_ready, 1)
            for h in range(2):
                pe.wait_ge(relu_ready, h + 1)
                for n in range(2):
                    o = pT[:, h, n, :]
                    for e in range(2 * h, 2 * h + 2):
                        mmul(o, lhsT=h1[:, e, :], rhs=w2e[:, e, n * 512:(n + 1) * 512], start=(e == 2 * h), stop=False)
                    mm = mmul(o, lhsT=esel[:, h, :], rhs=b2t[:, n * 512:(n + 1) * 512], start=False, stop=True)
                mm.then_inc(pe_done, 1)
            for f in range(2):
                pe.wait_ge(contrib_ready, f + 1)
                for h in range(2):
                    for n in range(2):
                        mm = mmul(pW[:, 2 * h + n, :], lhsT=dq[:, f, h, :], rhs=ct[:, f, n * 512:(n + 1) * 512], start=(f == 0), stop=(f == 1))
                    if f:
                        mm.then_inc(pe_done, 1)

        @block.scalar
        def _(act):
            A = nc.scalar.activation
            act.wait_ge(const_ready, 1)
            def ranks(t):
                A(junks[:, :], keyr[:, :], ACT.Sign, bias=dyn(key, t), scale=-1.0, accum_out=dyn(sgn, t)).then_inc(ranks_ready, 1)

            for c in range(DC):
                act.wait_ge(projection_copied, c + 1)
                A(wh[:, c, :], wext[:, c, :], ACT.Copy).then_inc(w_high_ready, 1)

            def deviation(t, u):
                act.wait_ge(var_ready, t + 1)
                A(sdv[:, u % 2:u % 2 + 1], recA[:, u % XS, 1:2], ACT.Sqrt, bias=eps[:, :]).then_inc(std_ready, 1)

            deviation(0, 0)

            def squares_of(t, u):
                act.wait_ge(rows_ready, t + 1)
                if not isinstance(t, int) or t:
                    act.wait_ge(squares_ready, t * 2)
                A(junka[:, 0, :], xr[:, u % XS, 0:H], ACT.Square, accum_out=recA[:, u % XS, 3:4]).then_inc(squares_ready, 1)
                A(junka[:, 1, :], xr[:, u % XS, H:D], ACT.Square, accum_out=recB[:, u % XS, 9:10]).then_inc(squares_ready, 1)

            def step(j, u, ranked):
                i = j * XS
                t = i + u
                if has(i, u, 1) and (u == -1 or not ranked):
                    act.wait_ge(tile_turned, t + 2)
                    if not early(i, u, 1):
                        act.wait_ge(tile_multiplied, t)
                    A(xh_[:, (u + 1) % 2, 4:8, :].rearrange("p a b -> p (a b)"), pT[:, (u + 1) % 2, 1, :], ACT.Copy).then_inc(high1_ready, 1)
                if has(i, u, 2):
                    n = (u + 2) % 2
                    act.wait_ge(shift_ready, t + 3)
                    if not early(i, u, 0):
                        act.wait_ge(tile_turned, t + 1)
                    A(xn[:, n, :], xr[:, (u + 2) % XS, :], ACT.Identity, bias=nmr[:, n:n + 1], scale=rsd[:, n:n + 1]).then_inc(xn_ready, 1)
                if u >= 0 and not ranked and not (isinstance(t, int) and t == ET):
                    squares_of(t - 1, u - 1)
                if u >= 0 and ranked:
                    if isinstance(t, int) and t == 0:
                        act.wait_ge(keys_ready, 1)
                    else:
                        act.wait_ge(ranks_ready, t)
                    ranks(t)
                if has(i, u, 3):
                    deviation(t + 3, u + 3)
                if u >= 0 and ranked:
                    squares_of(t, u)

            node_loop(act, step)
            squares_of(NT - 1, (NT - 1) % XS)
            act.wait_ge(degrees_ready, 1)
            A(w[10][:, :], w[9][:, :], ACT.Sqrt).then_inc(roots_ready, 1)

            for k in range(K):
                def tanh(g):
                    a, b = g * GT, (g + 1) * GT
                    act.wait_ge(arg_ready, GQ * k + g + 1)
                    A(al[:, a:b], pre[:, a:b], ACT.Tanh, bias=bgb[:, k:k + 1]).then_inc(tanh_ready, 1)

                def scale(i, u):
                    t, n = i + u, (i + u) % 2
                    if k or t >= 2:
                        act.wait_ge(agg_ready, t + (ET * k - 1))
                    A(E32[:, n, :], row(E, t), ACT.Copy, scale=dyn(m, t)).then_inc(sel_ready, 1)

                tanh(0)
                if k == 0:
                    act.wait_ge(select_ready, 1)
                for g in range(GQ):
                    act.wait_ge(coef_ready, GQ * k + g + 1)
                    for u in range(GT):
                        scale(g * GT, u)
                        if u == 1 and g + 1 < GQ:
                            tanh(g + 1)

            def squares(t):
                act.wait_ge(final_ready, t + 1)
                if not isinstance(t, int):
                    act.wait_ge(final_squares, t)
                A(junkc[:, :], row(Z[:, :, 0:H], t), ACT.Square, accum_out=row(Z[:, :, H + 9:H + 10], t)).then_inc(final_squares, 1)
            squares(0)
            with act.Fori(1, ET, 1) as t:
                squares(t)
            act.wait_ge(final_squares, ET)
            act.wait_ge(special_rows, 1)
            A(junkc[0:ET, :], Sx[:, 0:H], ACT.Square, accum_out=Sx[:, H + 9:H + 10]).then_inc(special_squares, 1)

            act.wait_ge(nodes_landed[0], 16)
            A(q[0][:, :], ndA[:, :, 1], ACT.Sqrt, bias=eps[:, :]).then_inc(roots_of_var, 1)
            act.wait_ge(final_var_ready, 1)
            A(q[4][:, :], q[3][:, :], ACT.Sqrt, bias=eps[:, :]).then_inc(roots_of_var, 1)
            act.wait_ge(logits_ready, 1)
            A(lt[:, :, :], lg[:, :, :], ACT.Exp).then_inc(exp_ready, 1)
            for h in range(2):
                act.wait_ge(expert_var, h + 1)
                A(fsd[:, h:h + 1], fmv[:, h, 1:2], ACT.Sqrt, bias=eps[:, :]).then_inc(expert_std, 1)
            for h in range(2):
                act.wait_ge(expert_shift, h + 1)
                A(fn[:, h, :], fx[:, h, :], ACT.Identity, bias=fnm[:, h:h + 1], scale=frs[:, h:h + 1]).then_inc(expert_xn_ready, 1)
            act.wait_ge(h1_cleared, 1)
            act.wait_ge(expert_w_landed, 16 * (EX + 3))
            for e in range(EX):
                act.wait_ge(hidden_ready, e // 4 + 1)
                c, f = (e % 4) * TOPK, slice((e % 2) * FF, (e % 2 + 1) * FF)
                ins = A(h1[f, e // 2, c:c + TOPK], pA[f, e // 4, e * TOPK:(e + 1) * TOPK], ACT.Relu, bias=b1t[f, e // 2:e // 2 + 1])
                if e % 4 == 3:
                    ins.then_inc(relu_ready, 1)

        @block.vector
        def _(dve):
            v = nc.vector
            chain = [0]

            def link(ins):
                chain[0] += 1
                ins.then_inc(dve_step, 1)
                dve.wait_ge(dve_step, chain[0])

            v.memset(eps[:, :], EPS).then_inc(const_ready, 1)
            v.memset(ones[:, :], 1.0).then_inc(const_ready, 1)
            v.memset(recA[:, :, :], 0.0)
            link(v.memset(recB[:, :, :], 0.0))

            def keys():
                dve.wait_ge(edges_landed, 48)
                dve.wait_ge(partitions_ready, 1)
                v.tensor_copy(pairs[:, :, 0], ei[:, 0, :])
                v.tensor_copy(pairs[:, :, 1], ei[:, 1, :])
                link(v.tensor_copy(dstf[:, :], ei[:, 0, :]))
                v.tensor_scalar(key[:, :], dstf[:, :], float(P), pcol[:, :], ALU.mult, ALU.add)
                v.scalar_tensor_tensor(keyr[:, :], drow[0:EP, 0:NE], float(P), keyr[:, :], ALU.mult, ALU.add).then_inc(keys_ready, 1)
                v.tensor_tensor(eq[:, :, :], dstf[:, :].unsqueeze(2).to_broadcast([EP, EJ, EJ]),
                                dstf[:, :].unsqueeze(1).to_broadcast([EP, EJ, EJ]), ALU.is_equal).then_inc(equal_step, 1)
                dve.wait_ge(equal_step, 1)
                v.tensor_reduce(ceq[:, :], eq[:, :, :], AX.X, ALU.add).then_inc(equal_step, 1)
                dve.wait_ge(equal_step, 3)
                link(v.tensor_reduce(clt[:, :], eq[:, :, :], AX.X, ALU.add))
                link(v.tensor_scalar(c0[:, :], ceq[:, :], -0.5, NE / 2.0 + 1.0, ALU.mult, ALU.add))
                v.tensor_tensor(c0[:, :], c0[:, :], clt[:, :], ALU.add).then_inc(offset_ready, 1)

            def lower(c):
                dve.wait_ge(w_high_ready, c + 1)
                v.tensor_tensor(wl[:, c, :], wext[:, c, :], wh[:, c, :].bitcast(F32), ALU.subtract).then_inc(w_low_ready, 1)

            dve.wait_ge(weights_landed, 16 * NWL)
            def turned(c):
                dve.wait_ge(w1_turned, c + 1)
                if c >= 2:
                    dve.wait_ge(w1_projected, c - 1)
                v.tensor_copy(wT[:, c % 2, :, :].rearrange("p a b -> p (a b)"), pT[:, c % 2, 0, :]).then_inc(w1_copied, 1)

            turned(0)
            for c in range(DC):
                if c + 1 < DC:
                    turned(c + 1)
                dve.wait_ge(w1_projected, c + 1)
                v.tensor_copy(wext[:, c, H:H + NQ], pBC[c % 2][:, 0:NQ]).then_inc(projection_copied, 1)
                if c:
                    lower(c - 1)
            lower(DC - 1)

            def bias_projections():
                dve.wait_ge(w1_projected, DC + 1)
                v.tensor_copy(b1e[:, H:R], pC[:, 0:NP])
                v.tensor_copy(bRa[:, :], pC[:, NP:NQ])
                v.tensor_copy(csrw[:, :], pC[:, NQ:NQ + EX]).then_inc(projection_copied, 1)
                dve.wait_ge(projection_copied, DC + 1)

            def step(j, u, ranked):
                i = j * XS
                t = i + u
                if has(i, u, 2):
                    s, n = (u + 2) % XS, (u + 2) % 2
                    dve.wait_ge(x_landed[s], slot16(j, u + 2))
                    v.bn_stats(bns[:, n, 0, :], xr[:, s, 0:H]).then_inc(stats_ready, 1)
                    v.bn_stats(bns[:, n, 1, :], xr[:, s, H:D]).then_inc(stats_ready, 1)
                    if not early(i, u, XS - 2):
                        dve.wait_ge(records_stored[s], slot32(j, u + 2 - XS))
                    dve.wait_ge(stats_ready, t * 2 + 6)
                    v.memset(recA[:, s, 4:5], 0.0)
                    v.bn_aggr(recA[:, s, 0:2], bns[:, n, :, :].rearrange("p a b -> p (a b)")).then_inc(var_ready, 1)
                if has(i, u, 1) and u >= -1:
                    dve.wait_ge(tile_turned, t + 2)
                    if not early(i, u, 1):
                        dve.wait_ge(tile_multiplied, t)
                    nt = (u + 1) % 2
                    half = lambda ap, k: ap[:, nt, 4 * k:4 * k + 4, :].rearrange("p a b -> p (a b)")
                    v.tensor_copy(half(xh_, 0), pT[:, nt, 0, :]).then_inc(high0_ready, 1)
                    if ranked and u >= 0:
                        v.tensor_copy(half(xh_, 1), pT[:, nt, 1, :]).then_inc(high1_ready, 1)
                if has(i, u, 2):
                    dve.wait_ge(std_ready, t + 3)
                    v.reciprocal(rsd[:, n:n + 1], sdv[:, n:n + 1]).then_inc(rstd_ready, 1)
                    dve.wait_ge(rstd_ready, t + 3)
                    v.tensor_scalar(nmr[:, n:n + 1], recA[:, s, 0:1], rsd[:, n:n + 1], -1.0, ALU.mult, ALU.mult).then_inc(shift_ready, 1)
                if has(i, u, 1) and u >= -1:
                    dve.wait_ge(high0_ready, t + 2)
                    v.tensor_tensor(half(xl_, 0), pT[:, nt, 0, :], half(xh_, 0).bitcast(F32), ALU.subtract)
                    dve.wait_ge(high1_ready, t + 2)
                    v.tensor_tensor(half(xl_, 1), pT[:, nt, 1, :], half(xh_, 1).bitcast(F32), ALU.subtract).then_inc(lows_ready, 1)
                if isinstance(t, int) and t == 0:
                    bias_projections()
                    keys()
                if u >= 0:
                    s, n = u % XS, u % 2
                    dve.wait_ge(tile_multiplied, t + 1)
                    if not early(i, u, 2):
                        dve.wait_ge(x1_stored[n], slot16(j, u - 2, 2))
                    v.tensor_tensor(x1s[:, n, WHALF:R], pBC[n][:, 0:R - WHALF], b1e[:, WHALF:R], ALU.add).then_inc(x1_tail_ready, 1)
                    v.tensor_copy(recA[:, s, 8:24], pBC[n][:, R - WHALF:WHALF])
                    v.tensor_tensor(x1s[:, n, 0:WHALF], pA[:, n, 0:WHALF], b1e[:, 0:WHALF], ALU.add).then_inc(x1_ready, 1)
                    dve.wait_ge(x1_tail_ready, t + 1)
                    v.tensor_copy(recB[:, s, 0:8], x1s[:, n, H + 8:R])
                    dve.wait_ge(x1_ready, t + 1)
                    dve.wait_ge(xn_ready, t + 1)
                    v.scalar_tensor_tensor(xr[:, s, 0:H], xr[:, s, 0:H], 1.0, x1s[:, n, 0:H], ALU.mult, ALU.add, accum_out=recA[:, s, 2:3])
                    v.scalar_tensor_tensor(xr[:, s, H:D], xr[:, s, H:D], 1.0, x1s[:, n, 0:H], ALU.mult, ALU.add, accum_out=recB[:, s, 8:9]).then_inc(rows_ready, 1)

            def slot16(j, u, ring=XS):
                return j * (16 * XS // ring) + 16 * (u // ring + 1)

            def slot32(j, u, ring=XS):
                return j * (32 * XS // ring) + 32 * (u // ring + 1)

            node_loop(dve, step)

            dve.wait_ge(tables_ready, 1)
            dve.wait_ge(dst_row_landed, 16)
            v.tensor_tensor(E[:, :, :], drow[:, :].rearrange("p (t e) -> p t e", e=P),
                            curf[:, :].unsqueeze(2).to_broadcast([P, ET, P]), ALU.is_equal).then_inc(select_ready, 1)
            link(v.tensor_tensor(TBl[:, :, :], browf[:, :, :].rearrange("p a b -> p (a b)").unsqueeze(1).to_broadcast([P, ET, 2 * ET]),
                                 curf[:, :].unsqueeze(2).to_broadcast([P, ET, 2 * ET]), ALU.is_equal))
            for s in range(2):
                v.memset(TBl[:, :, :].rearrange("p t b -> p (t b)")[:, s * ET:s * ET + (ET - 1) * (2 * ET + 1) + 1:2 * ET + 1], 0.0)
            v.scalar_tensor_tensor(Fsel[:, :, :], drow[0:2 * ET, :].rearrange("p (t e) -> p t e", e=P), bcf[:, 0:1],
                                   own[:, :].unsqueeze(2).to_broadcast([2 * ET, ET, P]), ALU.is_equal, ALU.mult).then_inc(select_ready, 1)

            dve.wait_ge(tables_ready, 2)
            sub = lambda o, a, b: link(v.tensor_tensor(o, a, b, ALU.subtract))
            add_ = lambda o, a, b: link(v.tensor_tensor(o, a, b, ALU.add))
            ts = lambda o, a, s1, s2, o0, o1: link(v.tensor_scalar(o, a, s1, s2, o0, o1))
            sub(w[9][:, :], TS[:, :, 1], TS[:, :, 0])
            sub(w[10][:, :], TD[:, :, 1], TD[:, :, 0])
            ts(w[0][:, :], w[9][:, :], 0.0, FAR, ALU.is_equal, ALU.mult)
            add_(w[0][:, :], w[0][:, :], TS[:, :, 1])
            ts(w[0][:, :], w[0][:, :], 1.0, -1.0, ALU.mult, ALU.add)
            link(v.tensor_copy(ilsrc[:, :], w[0][:, :]))
            ts(w[9][:, :], w[9][:, :], 1.0, 0.0, ALU.max, ALU.add)
            ts(w[10][:, :], w[10][:, :], 1.0, 0.0, ALU.max, ALU.add)
            v.tensor_tensor(w[9][:, :], w[9][:, :], w[10][:, :], ALU.mult).then_inc(degrees_ready, 1)
            dve.wait_ge(roots_ready, 1)
            link(v.reciprocal(norm[:, :], w[10][:, :]))
            link(v.tensor_tensor(w[11][:, :], norm[:, :], norm[:, :], ALU.mult))
            link(v.tensor_tensor(w[11][:, :], w[11][:, :], w[9][:, :], ALU.mult))
            ts(w[11][:, :], w[11][:, :], -0.5, 1.5, ALU.mult, ALU.add)
            link(v.tensor_tensor(norm[:, :], norm[:, :], w[11][:, :], ALU.mult))
            ts(sm[:, 0:1], bcf[0:ET, 2:3], 1.0, 0.0, ALU.mult, ALU.add)
            link(v.scalar_tensor_tensor(Lm[:, :], browf[0:ET, 0, :], sm[:, 0:1], Lm[:, :], ALU.is_equal, ALU.mult))
            ts(sm[:, 1:2], fbase[:, :], 1.0, float(P), ALU.mult, ALU.add)
            ts(sm[:, 2:3], TL[:, 1:2], 1.0, -1.0, ALU.mult, ALU.add)
            ts(sm[:, 3:4], sm[:, 2:3], sm[:, 1:2], 0.0, ALU.min, ALU.add)
            link(v.tensor_copy(fidx[:, :], sm[:, 3:4]))
            sub(sm[:, 4:5], sm[:, 2:3], sm[:, 3:4])
            ts(sm[:, 4:5], sm[:, 4:5], 0.0, FAR, ALU.is_gt, ALU.mult)
            ts(sm[:, 5:6], bcf[0:ET, 1:2], 2.0, 1.0, ALU.mult, ALU.add)
            add_(sm[:, 6:7], sm[:, 4:5], sm[:, 5:6])
            link(v.tensor_copy(ispo[:, :], sm[:, 6:7]))
            link(v.tensor_copy(ispx[:, :], sm[:, 5:6]))
            add_(sm[:, 7:8], sm[:, 4:5], bcf[0:ET, 1:2])
            link(v.tensor_copy(ispn[:, :], sm[:, 7:8]))
            v.memset(mark[:, 2:3], 0.0).then_inc(norm_ready, 1)

            def final(t):
                zr = row(Z[:, :, 0:H], t)
                v.scalar_tensor_tensor(zr, zr, 1.0, row(V[:, :, 0:H], t), ALU.mult, ALU.add, accum_out=row(Z[:, :, H + 8:H + 9], t))
                v.tensor_copy(row(Z[:, :, H:H + 8], t), row(V[:, :, H + 8:R], t)).then_inc(final_ready, 1)
            def finals():
                dve.wait_ge(v_added, ET * K)
                for g in range(GQ):
                    dve.wait_ge(xright_landed[g], 16 * GT)
                    with dve.Fori(g * GT, (g + 1) * GT, 1) as t:
                        final(t)

            for k in range(K):
                def argument(g):
                    a, b = g * GT, (g + 1) * GT
                    dve.wait_ge(z_landed[g], 16 * GT * (k + 1))
                    if k == 0:
                        dve.wait_ge(v_landed[g], 16 * GT)
                        link(v.tensor_copy(Vpi[:, a:b, :], V[:, a:b, H:H + K]))
                    v.tensor_tensor(pre[:, a:b], Z[:, a:b, H + K + k], Vpi[:, a:b, k], ALU.add).then_inc(arg_ready, 1)

                def coefficients(g):
                    a, b = g * GT, (g + 1) * GT
                    dve.wait_ge(tanh_ready, GQ * k + g + 1)
                    v.tensor_tensor(m[:, a:b], al[:, a:b], norm[:, a:b], ALU.mult).then_inc(coef_ready, 1)

                def split(g):
                    a, b = g * GT, (g + 2) * GT
                    dve.wait_ge(coef_ready, GQ * k + g + 2)
                    mb = m[:, a:b].unsqueeze(2).to_broadcast([P, 2 * GT, K])
                    link(v.tensor_tensor(zf[:, :, :], Z[:, a:b, H:H + K], mb, ALU.mult))
                    link(v.tensor_copy(z3[:, a:b, 0:K], zf[:, :, :]))
                    link(v.tensor_tensor(zf[:, :, :], zf[:, :, :], z3[:, a:b, 0:K], ALU.subtract))
                    link(v.tensor_copy(z3[:, a:b, K:2 * K], zf[:, :, :]))
                    link(v.tensor_tensor(zf[:, :, :], zf[:, :, :], z3[:, a:b, K:2 * K], ALU.subtract))
                    v.tensor_copy(z3[:, a:b, 2 * K:3 * K], zf[:, :, :]).then_inc(split_ready, 1)

                def add(i, u, n):
                    t = i + u
                    dve.wait_ge(agg_ready, t + (ET * k + 1))
                    vt = row(V, t).rearrange("p (a b) -> p a b", a=2)
                    v.tensor_tensor(vt, vt, pW[:, 2 * n:2 * n + 2, 0:R // 2], ALU.add).then_inc(v_added, 1)

                argument(0)
                coefficients(0)
                for g in range(GQ):
                    if g + 1 < GQ:
                        argument(g + 1)

                    def after_first():
                        if g + 1 < GQ:
                            coefficients(g + 1)
                        if k < K - 1 and g % 2:
                            split(g - 1)
                    group_tiles(g * GT if k or g else None, dve, add, after_first)
                if k == K - 1:
                    finals()
                if k == 0:
                    dve.wait_ge(rc0_landed, 16)
                dve.wait_ge(rc_landed, 16 * GQ * (k + 1))
                v.tensor_tensor(RC[:, :], RC[:, :], RC0[:, :], ALU.subtract).then_inc(rc_diff_ready, 1)
                if k < K - 1:
                    dve.wait_ge(bound_sums_ready, k + 1)
                    tc = 4 * k
                    v.tensor_copy(tbf[:, :], pC[0:2 * ET, 0:3 * K]).then_inc(bound_step, 1)
                    dve.wait_ge(bound_step, tc + 1)
                    link(v.tensor_tensor(tbf[:, 0:K], tbf[:, 0:K], tbf[:, K:2 * K], ALU.add))
                    link(v.tensor_tensor(tbf[:, 0:K], tbf[:, 0:K], tbf[:, 2 * K:3 * K], ALU.add))
                    v.tensor_copy(tb3[:, 0:K], tbf[:, 0:K]).then_inc(bound_step, 1)
                    dve.wait_ge(bound_step, tc + 2)
                    link(v.tensor_tensor(tbf[:, 0:K], tbf[:, 0:K], tb3[:, 0:K], ALU.subtract))
                    v.tensor_copy(tb3[:, K:2 * K], tbf[:, 0:K]).then_inc(bound_step, 1)
                    dve.wait_ge(bound_step, tc + 3)
                    link(v.tensor_tensor(tbf[:, 0:K], tbf[:, 0:K], tb3[:, K:2 * K], ALU.subtract))
                    v.tensor_copy(tb3[:, 2 * K:3 * K], tbf[:, 0:K]).then_inc(bound_step, 1)
                dve.wait_ge(carry_ready, k + 1)
                if k:
                    dve.wait_ge(carry_added, 16 * k)
                v.tensor_copy(corr[:, 0:H], pT[0:ET, 1, 0, :])
                v.tensor_copy(corr[:, H:R], pT[0:ET, 1, 1, 0:NP]).then_inc(carry_copied, 1)
                if k < K - 1:
                    dve.wait_ge(dst_sums_ready, k + 1)
                    nar = pN[:, 0:3 * K * ET].rearrange("p (t c) -> p t c", c=3 * K)
                    for s in range(3):
                        link(v.tensor_tensor(Vpi[:, :, :], Vpi[:, :, :], nar[:, :, s * K:(s + 1) * K], ALU.add))
            link(v.memset(Sx[:, :], 0.0))
            v.memset(Sv[:, :], 0.0).then_inc(special_cleared, 1)
            dve.wait_ge(special_landed, 32)
            v.tensor_copy(Sx[:, H:H + 8], Sv[:, H + 8:R])
            v.scalar_tensor_tensor(Sx[:, 0:H], Sx[:, 0:H], 1.0, Sv[:, 0:H], ALU.mult, ALU.add, accum_out=Sx[:, H + 8:H + 9]).then_inc(special_rows, 1)

            b8 = lambda ap: ap[:, :].unsqueeze(2).to_broadcast([P, NT, EX])
            c8 = lambda ap: ap[:, :].unsqueeze(1).to_broadcast([P, NT, EX])
            dve.wait_ge(nodes_landed[0], 16)
            dve.wait_ge(roots_of_var, 1)
            link(v.tensor_tensor(lt[:, :, :], ndA[:, :, 16:24], b8(q[0]), ALU.mult))
            link(v.tensor_tensor(lg[:, :, :], ndA[:, :, 8:16], lt[:, :, :], ALU.add))
            dve.wait_ge(nodes_landed[1], 16)
            link(v.tensor_tensor(q[1][:, :], ndA[:, :, 2], ndB[:, :, 8], ALU.add))
            link(v.tensor_scalar(q[1][:, :], q[1][:, :], 1.0 / D, None, ALU.mult))
            link(v.tensor_tensor(q[2][:, :], ndA[:, :, 3], ndB[:, :, 9], ALU.add))
            link(v.tensor_tensor(q[5][:, :], q[1][:, :], q[1][:, :], ALU.mult))
            v.scalar_tensor_tensor(q[3][:, :], q[2][:, :], 1.0 / D, q[5][:, :], ALU.mult, ALU.subtract).then_inc(final_var_ready, 1)
            dve.wait_ge(final_var_ready, 1)
            link(v.tensor_tensor(q[2][:, :], ndA[:, :, 0], q[1][:, :], ALU.subtract))
            link(v.tensor_tensor(lg[:, :, :], lg[:, :, :], ndB[:, :, 0:8], ALU.add))
            link(v.tensor_tensor(lg[:, :, :], lg[:, :, :], c8(bRa), ALU.add))
            link(v.tensor_tensor(lt[:, :, :], b8(q[2]), c8(csrw), ALU.mult))
            link(v.tensor_tensor(lg[:, :, :], lg[:, :, :], lt[:, :, :], ALU.add))
            dve.wait_ge(roots_of_var, 2)
            link(v.reciprocal(q[4][:, :], q[4][:, :]))
            link(v.tensor_tensor(lg[:, :, :], lg[:, :, :], b8(q[4]), ALU.mult))
            link(v.tensor_tensor(lg[:, :, :], lg[:, :, :], c8(rbb), ALU.add))
            link(v.tensor_reduce(q[1][:, :], lg[:, :, :], AX.X, ALU.max))
            v.tensor_tensor(lg[:, :, :], lg[:, :, :], b8(q[1]), ALU.subtract).then_inc(logits_ready, 1)
            dve.wait_ge(exp_ready, 1)
            link(v.tensor_reduce(q[2][:, :], lt[:, :, :], AX.X, ALU.add))
            link(v.reciprocal(q[3][:, :], q[2][:, :]))
            v.tensor_tensor(sct[:, :, :].rearrange("p e j -> p j e"), lt[:, :, :], b8(q[3]), ALU.mult).then_inc(scores_ready, 1)

            link(v.memset(onesf[:, :], 1.0))
            v.memset(h1[:, :, :], 0.0).then_inc(h1_cleared, 1)

            def best_values(vals, data):
                for r in range(TOPK // 8):
                    o = slice(8 * r, 8 * r + 8)
                    ins = v.max(vals[:, o], data[:, r, :])
                    if r < TOPK // 8 - 1:
                        link(ins)
                        link(v.match_replace(data[:, r + 1, :], vals[:, o], data[:, r, :], -2.0))
                return ins

            def best_places(vals, idx, data):
                for r in range(TOPK // 8):
                    o = slice(8 * r, 8 * r + 8)
                    ins = v.max_index(idx[:, o], vals[:, o], data[:, r, :])
                link(ins)
            dve.wait_ge(tail_dma[1], 16)
            best_values(tv, tk).then_inc(best_ready, 1)
            dve.wait_ge(best_ready, 1)
            best_places(tv, ti, tk)
            link(v.tensor_copy(tif[:, :], ti[:, :]))
            dve.wait_ge(pool_const_ready, 1)
            v.tensor_scalar(tgi[:, :], tif[:, :], tbase[:, :], None, ALU.add).then_inc(candidates_ready, 1)
            dve.wait_ge(tail_dma[4], 16)
            best_values(gv, cv).then_inc(best_ready, 1)
            dve.wait_ge(best_ready, 2)
            best_places(gv, gi, cv)
            link(v.tensor_copy(gif[:, :], gi[:, :]))
            v.tensor_scalar(gpi[:, :], gif[:, :], gbase[:, :], None, ALU.add).then_inc(chosen_ready, 1)

            dve.wait_ge(tail_dma[8], 32)
            link(v.tensor_copy(tokf[:, :], tokw[:, :]))
            link(v.tensor_tensor(tokf[:, :], tokf[:, :], ebase[:, :], ALU.subtract))
            v.tensor_copy(tok[:, :], tokf[:, :]).then_inc(tokens_ready, 1)
            for h in range(2):
                ins = v.tensor_scalar(diag[:, h, :], ident[:, :], tokf[:, h:h + 1], None, ALU.mult)
            ins.then_inc(diag_ready, 1)
            dve.wait_ge(pe_done, 1)
            for f in range(2):
                for h in range(2):
                    ins = v.tensor_scalar(dq[:, f, h, :], pC[:, h * P:(h + 1) * P], tokf[:, f:f + 1], None, ALU.is_equal)
            ins.then_inc(same_token_ready, 1)
            for h in range(2):
                dve.wait_ge(chosen_landed[h], 16)
                v.bn_stats(fst[:, h, 0, :], fx[:, h, 0:H])
                link(v.bn_stats(fst[:, h, 1, :], fx[:, h, H:D]))
                v.bn_aggr(fmv[:, h, :], fst[:, h, :, :].rearrange("p a b -> p (a b)")).then_inc(expert_var, 1)
            for h in range(2):
                dve.wait_ge(expert_std, h + 1)
                link(v.reciprocal(frs[:, h:h + 1], fsd[:, h:h + 1]))
                v.tensor_scalar(fnm[:, h:h + 1], fmv[:, h, 0:1], frs[:, h:h + 1], -1.0, ALU.mult, ALU.mult).then_inc(expert_shift, 1)
            dve.wait_ge(earlier_ready, 1)
            link(v.tensor_reduce(tw[:, 0:1], dlo[:, 0, 0, :], AX.X, ALU.add))
            link(v.tensor_reduce(tw[:, 1:2], dlo[:, 1, :, :], AX.XY, ALU.add))
            link(v.tensor_scalar(tw[:, 2:4], tw[:, 0:2], 1.0, FAR, ALU.min, ALU.mult))
            link(v.tensor_tensor(tw[:, 4:6], tw[:, 2:4], tokf[:, :], ALU.add))
            v.tensor_copy(tokw[:, :], tw[:, 4:6]).then_inc(writers_ready, 1)
            for h in range(2):
                dve.wait_ge(pe_done, 2 + h)
                v.tensor_copy(fT[:, 0:4, h * P:(h + 1) * P], pT[:, h, 0, :].rearrange("p (a b) -> p a b", b=P))
                v.tensor_copy(fT[:, 4:8, h * P:(h + 1) * P], pT[:, h, 1, :].rearrange("p (a b) -> p a b", b=P)).then_inc(expert_xT_ready, 1)
            dve.wait_ge(tail_dma[7], 16)
            for h in range(2):
                dve.wait_ge(pe_done, 4 + h)
                for n in range(2):
                    ins = v.tensor_scalar(ct[:, h, n * 512:(n + 1) * 512], pT[:, h, n, :], gcol[:, h:h + 1], None, ALU.mult)
                ins.then_inc(contrib_ready, 1)
            dve.wait_ge(expert_xn_ready, 2)
            for h in range(2):
                dve.wait_ge(pe_done, 6 + h)
                o = fx[:, h, :].rearrange("p (n c) -> p n c", n=2)
                v.tensor_tensor(o, o, pW[:, 2 * h:2 * h + 2, :], ALU.add).then_inc(sum_rows_ready, 1)

        @block.gpsimd
        def _(pool):
            g_ = nc.gpsimd
            chain = [0]

            def link(ins):
                chain[0] += 1
                ins.then_inc(pool_step, 1)
                pool.wait_ge(pool_step, chain[0])

            dmas = [0]

            def dma_all(issue):
                dmas[0] += issue()
                pool.wait_ge(pool_dma, 16 * dmas[0])

            link(g_.memset(ident[:, :], 0.0))
            g_.affine_select(out=ident[:, :], in_=ident[:, :], compare_op=ALU.not_equal, fill=1.0, base=0,
                             pattern=[[-1, P]], channel_multiplier=1).then_inc(ident_ready, 1)
            g_.iota(pcol[:, :], [[0, 1]], base=0, channel_multiplier=1, allow_small_or_imprecise_dtypes=True)
            g_.iota(keyr[:, :], [[1, EP], [0, EJ]], base=0, channel_multiplier=0, allow_small_or_imprecise_dtypes=True).then_inc(partitions_ready, 1)
            npad = EPAD - NE
            g_.memset(padi[:, 0:2], -1)
            g_.memset(padi[:, 2:2 + 2 * npad], PADV)
            link(g_.memset(padi[:, 2 + 2 * npad:4 + 2 * npad], 2 * NPAD))
            link(g_.memset(zt[:, :], 0.0))
            def init():
                pool.dma_start(SO[0:1, :], padi[:, 0:2]).then_inc(pool_dma, 16)
                pool.dma_start(SO[NE + 1:EPAD + 2, :].rearrange("(a n) c -> a (n c)", a=1), padi[:, 2:4 + 2 * npad]).then_inc(pool_dma, 16)
                pool.dma_start(T.rearrange("(p n) a -> p (n a)", p=P), zt[:, :]).then_inc(pool_dma, 16)
                return 3
            dma_all(init)
            pool.wait_ge(equal_step, 2)
            g_.affine_select(out=eq[:, :, :], in_=eq[:, :, :], compare_op=ALU.is_gt, fill=0.0, base=0,
                             pattern=[[1, EJ], [-1, EJ]], channel_multiplier=0).then_inc(equal_step, 1)
            g_.iota(slot[:, :], [[P, ET]], base=0, channel_multiplier=1, allow_small_or_imprecise_dtypes=True)
            g_.iota(slot1[:, :], [[P, ET]], base=1, channel_multiplier=1, allow_small_or_imprecise_dtypes=True)
            g_.iota(fbase[:, :], [[0, 1]], base=-1, channel_multiplier=P, allow_small_or_imprecise_dtypes=True)
            link(g_.memset(own[:, :], 1.0))
            link(g_.memset(Lm[:, :], 1.0))
            link(g_.affine_select(out=Lm[:, :], in_=Lm[:, :], compare_op=ALU.is_gt, fill=0.0, base=0,
                                  pattern=[[1, ET]], channel_multiplier=-1))
            link(g_.affine_select(out=own[:, :], in_=own[:, :], compare_op=ALU.not_equal, fill=0.0, base=0,
                                  pattern=[[-1, ET]], channel_multiplier=1))
            link(g_.affine_select(out=own[:, :], in_=own[:, :], compare_op=ALU.not_equal, fill=0.0, base=-ET,
                                  pattern=[[-1, ET]], channel_multiplier=1))
            link(g_.tensor_scalar(own[:, :], own[:, :], -1.0, 1.0, ALU.mult, ALU.add))

            pool.wait_ge(ranks_ready, EJ)
            pool.wait_ge(offset_ready, 1)
            link(g_.tensor_scalar(posf[:, :], sgn[:, :], 0.5, 0.0, ALU.mult, ALU.add))
            link(g_.tensor_tensor(posf[:, :], posf[:, :], c0[:, :], ALU.add))
            link(g_.tensor_copy(posi[:, :], posf[:, :]))

            def scatter(dst_, idx, src_, bound, s):
                pool.indirect_dma_start(out=dst_, out_offset=bass.IndirectOffsetOnAxis(ap=idx, axis=0), in_=src_, in_offset=None,
                                        bounds_check=bound, oob_is_err=False).then_inc(s, 16)

            def gather(dst_, src_, idx, bound, s):
                pool.indirect_dma_start(out=dst_, out_offset=None, in_=src_, in_offset=bass.IndirectOffsetOnAxis(ap=idx, axis=0),
                                        bounds_check=bound, oob_is_err=False).then_inc(s, 16)

            def sort():
                for j in range(EJ):
                    scatter(SO[:, :], posi[:, j:j + 1], pairs[:, j, :], EPAD + 1, pool_dma)
                return EJ
            dma_all(sort)

            def sorted_loads():
                for o, tile in ((1, cur), (2, nxt), (0, prv)):
                    pool.dma_start(tile[:, :, :], SO[o:o + EPAD, :].rearrange("(t p) c -> p t c", p=P)).then_inc(pool_dma, 16)
                pool.dma_start(curR[:, :, :], SO[1:1 + EPAD, :].rearrange("(t p) c -> t p c", p=P)).then_inc(pool_dma, 16)
                tiles = SO[1:1 + EPAD, :].rearrange("(t p) c -> p t c", p=P)
                with nc.allow_non_contiguous_dma(reason="boundary nodes"):
                    for s, r in ((0, 0), (1, P - 1)):
                        pool.dma_start(brow[:, s, :], tiles[r, :, 0].unsqueeze(0).to_broadcast([P, ET])).then_inc(pool_dma, 16)
                        pool.dma_start(bcol[s * ET:(s + 1) * ET, 0:1], tiles[r, :, 0:1]).then_inc(pool_dma, 16)
                        pool.dma_start(bcol[0:ET, 1 + s:2 + s], tiles[r, :, 0:1]).then_inc(pool_dma, 16)
                        pool.dma_start(bcol[ET:2 * ET, 1 + s:2 + s], tiles[r, :, 0:1]).then_inc(pool_dma, 16)
                return 12
            dma_all(sorted_loads)
            link(g_.tensor_copy(dR[:, :], curR[:, :, 0]))

            def rows_out():
                pool.dma_start(SD.rearrange("(t p) -> t p", p=P), dR[:, :]).then_inc(pool_dma, 16)
                return 1
            dma_all(rows_out)
            pool.wait_ge(keys_ready, 1)
            pool.dma_start(drow[:, :], SD.rearrange("(a n) -> a n", a=1).to_broadcast([P, EPAD])).then_inc(dst_row_landed, 16)

            def f32(dst_, src_):
                link(g_.tensor_copy(dst_, src_))
            f32(curf[:, :], cur[:, :, 0])
            f32(w[0][:, :], nxt[:, :, 0])
            f32(w[1][:, :], prv[:, :, 0])
            f32(w[2][:, :], cur[:, :, 1])
            f32(browf[:, :, :], brow[:, :, :])
            f32(bcf[:, :], bcol[:, :])
            f32(dRf[:, :], dR[:, :])
            sub = lambda o, a, b: link(g_.tensor_tensor(o, a, b, ALU.subtract))
            add = lambda o, a, b: link(g_.tensor_tensor(o, a, b, ALU.add))
            ts = lambda o, a, s1, s2, o0, o1: link(g_.tensor_scalar(o, a, s1, s2, o0, o1))
            sub(w[3][:, :], w[0][:, :], curf[:, :])
            ts(w[3][:, :], w[3][:, :], 0.0, FAR, ALU.is_equal, ALU.mult)
            sub(w[4][:, :], curf[:, :], w[1][:, :])
            ts(w[4][:, :], w[4][:, :], 0.0, FAR, ALU.is_equal, ALU.mult)
            ts(w[5][:, :], curf[:, :], 2.0, 0.0, ALU.mult, ALU.add)
            ts(w[6][:, :], curf[:, :], 2.0, 1.0, ALU.mult, ALU.add)
            add(w[4][:, :], w[4][:, :], w[5][:, :])
            link(g_.tensor_copy(ifst[:, :], w[4][:, :]))
            add(w[7][:, :], w[3][:, :], w[6][:, :])
            link(g_.tensor_copy(ilst[:, :], w[7][:, :]))
            link(g_.tensor_copy(iout[:, :], w[7][:, :]))
            add(w[8][:, :], w[3][:, :], curf[:, :])
            link(g_.tensor_copy(inode[:, :], w[8][:, :]))
            link(g_.tensor_copy(ixr[:, :], w[6][:, :]))
            link(g_.tensor_copy(isrc[:, :], w[2][:, :]))
            link(g_.tensor_copy(idst[:, :], curf[:, :]))
            link(g_.tensor_copy(ilast[:, :], bcf[0:ET, 2:3]))
            link(g_.tensor_copy(ifn[:, :], bcf[0:ET, 1:2]))

            sub(ovl[:, :], bcf[:, 1:2], bcf[:, 2:3])
            ts(ovl[:, :], ovl[:, :], 0.0, 1.0, ALU.is_equal, ALU.mult)
            ts(ovl[:, :], ovl[:, :], -1.0, 1.0, ALU.mult, ALU.add)
            link(g_.memset(ovl[0:ET, :], 1.0))
            ts(own[:, :], own[:, :], ovl[:, :], 0.0, ALU.mult, ALU.add)
            g_.memset(mark[:, 0:1], 0.0).then_inc(tables_ready, 1)

            def spans():
                for t in range(ET):
                    scatter(T, ifst[:, t:t + 1], slot[:, t:t + 1], 2 * NPAD - 1, pool_dma)
                    scatter(T, ilst[:, t:t + 1], slot1[:, t:t + 1], 2 * NPAD - 1, pool_dma)
                return 2 * ET
            dma_all(spans)
            T2 = T.rearrange("(n c) a -> n (c a)", c=2)

            def span_rows():
                for t in range(ET):
                    gather(TS[:, t, :], T2, isrc[:, t:t + 1], NPAD - 1, pool_dma)
                    gather(TD[:, t, :], T2, idst[:, t:t + 1], NPAD - 1, pool_dma)
                gather(TL[:, :], T2, ifn[:, :], NPAD - 1, pool_dma)
                return 2 * ET + 1
            dma_all(span_rows)
            g_.memset(mark[:, 1:2], 0.0).then_inc(tables_ready, 1)

            pool.wait_ge(x1_stored[0], 16 * ((NT + 1) // 2))
            pool.wait_ge(x1_stored[1], 16 * (NT // 2))
            for s in range(XS):
                n = (NT - s + XS - 1) // XS
                pool.wait_ge(out_stored[s], 16 * n)
                pool.wait_ge(records_stored[s], 32 * n)
            pool.wait_ge(tile_multiplied, NT)
            for g in range(GQ):
                for t in range(g * GT, (g + 1) * GT):
                    gather(Z[:, t, :], G, isrc[:, t:t + 1], NPAD - 1, z_landed[g])
            pool.wait_ge(norm_ready, 1)
            pool.wait_ge(select_ready, 2)
            for g in range(GQ):
                for t in range(g * GT, (g + 1) * GT):
                    gather(V[:, t, :], G, idst[:, t:t + 1], NPAD - 1, v_landed[g])
            gather(RC0[:, :], G, ilast[:, :], NPAD - 1, rc0_landed)

            def scatters(lo, hi):
                for t in range(lo, hi):
                    pool.wait_ge(final_squares, t + 1)
                    scatter(outh, iout[:, t:t + 1], Z[:, t, 0:H], 2 * N - 1, final_stored)
                    scatter(NDB, inode[:, t:t + 1], Z[:, t, H:R], NPAD - 1, final_stored)

            for k in range(K):
                if k == K - 1:
                    for g in range(GQ):
                        pool.wait_ge(agg_ready, ET * k + GT * (g + 1))
                        for t in range(g * GT, (g + 1) * GT):
                            gather(Z[:, t, 0:H], xh, ixr[:, t:t + 1], 2 * N - 1, xright_landed[g])
                    scatters(0, ET // 2)
                for g in range(GQ):
                    pool.wait_ge(v_stored[g], 16 * (k + 1))
                pool.wait_ge(carry_copied, k + 1)
                pool.indirect_dma_start(out=Vd[k % 2], out_offset=bass.IndirectOffsetOnAxis(ap=fidx[:, :], axis=0), in_=corr[:, :],
                                        in_offset=None, bounds_check=EPAD - 1, oob_is_err=True, compute_op=ALU.add).then_inc(carry_added, 16)
                if k < K - 1:
                    pool.wait_ge(carry_added, 16 * (k + 1))
                    for g in range(GQ):
                        for t in range(g * GT, (g + 1) * GT):
                            gather(Z[:, t, :], Vd[k % 2], ilsrc[:, t:t + 1], EPAD - 1, z_landed[g])

            scatters(ET // 2, 3 * ET // 4)
            pool.wait_ge(carry_added, 16 * K)
            pool.wait_ge(special_cleared, 1)
            gather(Sv[:, :], Vd[(K - 1) % 2], fidx[:, :], EPAD - 1, special_landed)
            gather(Sx[:, 0:H], xh, ispx[:, :], 2 * N - 1, special_landed)
            scatters(3 * ET // 4, ET)
            pool.wait_ge(final_stored, 16 * 2 * ET)
            pool.wait_ge(special_squares, 1)
            scatter(outh, ispo[:, :], Sx[:, 0:H], 2 * N - 1, special_stored)
            scatter(NDB, ispn[:, :], Sx[:, H:R], NPAD - 1, special_stored)
            pool.wait_ge(special_stored, 32)

            link(g_.iota(tbase[:, :], [[0, 1]], base=0, channel_multiplier=NPAD // 16, allow_small_or_imprecise_dtypes=True))
            link(g_.iota(gbase[:, :], [[0, 1]], base=0, channel_multiplier=16 * TOPK, allow_small_or_imprecise_dtypes=True))
            for r in range(4):
                for h in range(2):
                    link(g_.memset(ebase[32 * r:32 * r + 32, h:h + 1], float(NPAD * (4 * h + r))))
            link(g_.memset(esel[:, :, :], 1.0))
            for h in range(2):
                link(g_.affine_select(out=esel[:, h, :], in_=esel[:, h, :], compare_op=ALU.is_ge, fill=0.0, base=P * h,
                                      pattern=[[1, P]], channel_multiplier=-TOPK))
                link(g_.affine_select(out=esel[:, h, :], in_=esel[:, h, :], compare_op=ALU.is_ge, fill=0.0, base=TOPK - 1 - P * h,
                                      pattern=[[-1, P]], channel_multiplier=TOPK))
            g_.memset(tw[:, :], 0.0).then_inc(pool_const_ready, 1)
            pool.wait_ge(scores_ready, 1)
            g_.affine_select(out=sct[:, :, :], in_=sct[:, :, :], compare_op=ALU.is_ge, fill=-1.0, base=N - 1,
                             pattern=[[0, EX], [-1, NT]], channel_multiplier=-NT).then_inc(scores_masked, 1)
            pool.wait_ge(tail_dma[6], 16)
            pool.wait_ge(tail_dma[3], 16)
            for h in range(2):
                gather(tokw[:, h:h + 1], CI, pcl[:, h:h + 1], P * TOPK - 1, tail_dma[8])
            pool.wait_ge(tokens_ready, 1)
            for h in range(2):
                gather(fx[:, h, :], out, tok[:, h:h + 1], N - 1, chosen_landed[h])
            pool.wait_ge(same_token_ready, 1)
            g_.affine_select(out=dlo[:, 0, 0, :], in_=dq[:, 0, 0, :], compare_op=ALU.is_gt, fill=0.0, base=0,
                             pattern=[[-1, P]], channel_multiplier=1)
            g_.affine_select(out=dlo[:, 1, 1, :], in_=dq[:, 1, 1, :], compare_op=ALU.is_gt, fill=0.0, base=0,
                             pattern=[[-1, P]], channel_multiplier=1)
            g_.tensor_copy(dlo[:, 1, 0, :], dq[:, 1, 0, :]).then_inc(earlier_ready, 1)
            pool.wait_ge(writers_ready, 1)
            for h in range(2):
                pool.wait_ge(sum_rows_ready, h + 1)
                scatter(out, tokw[:, h:h + 1], fx[:, h, :], N - 1, tail_dma[9])
            pool.wait_ge(tail_dma[9], 32)


_INS = ["x", "src", "dst", "L0_gnn_W1", "L0_gnn_b1", "L0_gnn_Wg", "L0_gnn_bg", "L0_ffn_router_w", "L0_ffn_router_b",
        "L0_ffn_w1", "L0_ffn_b1", "L0_ffn_w2", "L0_ffn_b2"]


def kernel(**inputs):
    import numpy as _np
    import concourse.bacc as _bacc
    from concourse import mybir as _mybir
    from concourse.bass_utils import run_bass_kernel_spmd as _run

    nc = _bacc.Bacc("TRN2", target_bir_lowering=False, num_devices=1)
    arrays, args = {}, []
    for name in _INS:
        a = _np.ascontiguousarray(inputs[name])
        arrays[f"in_{name}"] = a
        args.append(nc.dram_tensor(f"in_{name}", a.shape, _mybir.dt.from_np(a.dtype), kind="ExternalInput").ap())
    f32, i32 = _mybir.dt.float32, _mybir.dt.int32
    args.append(nc.dram_tensor("out_0", inputs["x"].shape, f32, kind="ExternalOutput").ap())

    def scratch(name, shape, dt):
        return nc.dram_tensor(name, shape, dt, kind="Internal").ap()

    npad, epad = 10112, 5120
    args += [scratch("node_rows", (npad, 528), f32), scratch("sorted_pairs", (epad + 2, 2), i32),
             scratch("sorted_dst", (epad,), i32), scratch("spans", (2 * npad, 1), f32),
             [scratch("v_even", (epad, 528), f32), scratch("v_odd", (epad, 528), f32)],
             scratch("node_left", (npad, 24), f32), scratch("node_right", (npad, 16), f32),
             scratch("scores", (8, npad), f32), scratch("cand_values", (4096,), f32),
             scratch("cand_numbers", (4096, 1), i32), scratch("chosen", (512,), i32)]
    gnn_ffn(nc, *args)
    r = _run(nc, [arrays], core_ids=[0])
    return r.results[0]["out_0"]
```
